# Optimizing a Trainium2 kernel written in Bass

```python
import numpy as np
import jax
import jax.numpy as jnp

def _softmax(x, axis=-1):
    return jax.nn.softmax(x, axis=axis)

def _gelu(x):
    return jax.nn.gelu(x, approximate=True)

def _silu(x):
    return jax.nn.silu(x)

def _sigmoid(x):
    return jax.nn.sigmoid(x)

def _layernorm(x, axis=-1, eps=1e-05):
    m = jnp.mean(x, axis=axis, keepdims=True)
    v = jnp.var(x, axis=axis, keepdims=True)
    return (x - m) / jnp.sqrt(v + eps)

def _scatter_add(tgt, idx, src, axis=0):
    return tgt.at[idx].add(src)

def _segment_sum(src, seg, n):
    return jax.ops.segment_sum(src, seg, n)
kernel_name = 'mk_adj_ffn_d2_adj_r2_ffacf2'

def setup_inputs(seed: int=0):
    np.random.seed(seed)
    _w = jnp.asarray

    def _rec_inputs():
        import jax
        import jax.numpy as jnp
        _gk = jax.random.key(seed)
        x = 7.22e-05 + 1 * jax.random.normal(jax.random.fold_in(_gk, 1), (64, 128, 256), jnp.float32)
        _a = jax.random.bernoulli(jax.random.fold_in(_gk, 2), 0.03125, (64, 128, 128))
        _a = jnp.logical_or(_a, jnp.eye(128, dtype=bool))
        _af = _a.astype(jnp.float32)
        _af = _af * jax.random.uniform(jax.random.fold_in(_gk, 3), (64, 128, 128), jnp.float32, 0.05, 1)
        adj = _af
        _nm = jnp.ones((64, 128), dtype=bool)
        nodemask = jnp.where(_nm, 1.0, 0.0).astype(jnp.float32)
        return (x, adj, nodemask)
    x, adj, nodemask = _rec_inputs()

    def _L0_gnn_setup():
        import jax, jax.numpy as jnp
        import numpy as np
        B, N, IN_DIM, ATT_DIM = (2, 4096, 256, 256)
        key = jax.random.key(seed)
        k1, k2, k3, k4 = jax.random.split(key, 4)
        X = jax.random.normal(k1, (B, N, IN_DIM), dtype=jnp.float32)
        adj = jax.random.uniform(k2, (B, N, N), dtype=jnp.float32)
        mask = jnp.ones((B, N), dtype=jnp.float32)
        Wqk = jax.random.normal(k3, (IN_DIM, 2 * ATT_DIM), dtype=jnp.float32) / np.sqrt(IN_DIM)
        Wv = jax.random.normal(k4, (IN_DIM, IN_DIM), dtype=jnp.float32) / np.sqrt(IN_DIM)
        return {'X': X, 'adj': adj, 'mask': mask, 'Wqk': Wqk, 'Wv': Wv}
    _L0_gnn_all = _L0_gnn_setup()
    _L0_gnn_in = {k: v for k, v in _L0_gnn_all.items() if k in ('Wqk', 'Wv')}
    del _L0_gnn_all

    def _L0_ffn_setup():
        import jax, jax.numpy as jnp
        import numpy as np
        MAX_THRESHOLD = 0.25
        B, S, D, E = (8, 2048, 256, 8)
        key = jax.random.key(seed)
        ks = jax.random.split(key, 5)
        scale = 1.0 / np.sqrt(D)
        return {'inputs': jax.random.normal(ks[0], (B, S, D), dtype=jnp.float32), 'W_gate': jax.random.normal(ks[1], (D, E), dtype=jnp.float32) * scale, 'b_gate': jnp.zeros((E,), dtype=jnp.float32), 'W_thr': jax.random.normal(ks[2], (D, 1), dtype=jnp.float32) * scale, 'b_thr': jnp.zeros((1,), dtype=jnp.float32), 'W_exp': jax.random.normal(ks[3], (E, D, D), dtype=jnp.float32) * scale, 'b_exp': jnp.zeros((E, D), dtype=jnp.float32)}
    _L0_ffn_all = _L0_ffn_setup()
    _L0_ffn_in = {k: v for k, v in _L0_ffn_all.items() if k in ('W_gate', 'b_gate', 'W_thr', 'b_thr', 'W_exp', 'b_exp')}
    del _L0_ffn_all

    def _L1_gnn_setup():
        import jax, jax.numpy as jnp
        import numpy as np
        B, N, F_IN, F_HID, F_OUT = (32, 512, 256, 256, 256)

        def _gcn_layer(x, adj, W, b):
            support = jnp.einsum('bnf,fh->bnh', x, W)
            return jnp.einsum('bnm,bmh->bnh', adj, support) + b
        key = jax.random.key(seed)
        ks = jax.random.split(key, 8)

        def xavier(k, fan_in, fan_out):
            bound = float(np.sqrt(6.0 / (fan_in + fan_out)))
            return jax.random.uniform(k, (fan_in, fan_out), jnp.float32, -bound, bound)
        return {'batch_graph': jax.random.normal(ks[0], (B, N, F_IN), jnp.float32), 'adj': jax.random.uniform(ks[1], (B, N, N), jnp.float32), 'W1': xavier(ks[2], F_IN, F_HID), 'b1': jnp.zeros((F_HID,), jnp.float32), 'W2': xavier(ks[3], F_HID, F_HID), 'b2': jnp.zeros((F_HID,), jnp.float32), 'W3': xavier(ks[4], F_HID, F_OUT), 'b3': jnp.zeros((F_OUT,), jnp.float32)}
    _L1_gnn_all = _L1_gnn_setup()
    _L1_gnn_in = {k: v for k, v in _L1_gnn_all.items() if k in ('W1', 'b1', 'W2', 'b2', 'W3', 'b3')}
    del _L1_gnn_all

    def _L1_ffn_setup():
        import jax, jax.numpy as jnp
        import numpy as np
        NUM_EXPERTS = 8
        TOP_K = 2
        key = jax.random.key(seed)
        k0, k1, k2, k3, k4 = jax.random.split(key, 5)
        sl, bs, hs, ffn = (1024, 2, 256, 1024)
        T = sl * bs
        x = jax.random.normal(k0, (sl, bs, hs), jnp.float32)
        expert_weights = jax.random.uniform(k1, (T, TOP_K), jnp.float32)
        expert_indices = jax.random.randint(k2, (T, TOP_K), 0, NUM_EXPERTS)
        w1 = jax.random.normal(k3, (NUM_EXPERTS, hs, ffn), jnp.float32) * hs ** (-0.5)
        w2 = jax.random.normal(k4, (NUM_EXPERTS, ffn, hs), jnp.float32) * ffn ** (-0.5)
        return dict(x=x, expert_weights=expert_weights, expert_indices=expert_indices, w1=w1, w2=w2)
    _L1_ffn_all = _L1_ffn_setup()
    _L1_ffn_in = {k: v for k, v in _L1_ffn_all.items() if k in ('expert_weights', 'expert_indices', 'w1', 'w2')}
    del _L1_ffn_all
    return {'x': x, 'adj': adj, 'nodemask': nodemask, 'L0_gnn_Wqk': _L0_gnn_in['Wqk'], 'L0_gnn_Wv': _L0_gnn_in['Wv'], 'L0_ffn_W_gate': _L0_ffn_in['W_gate'], 'L0_ffn_b_gate': _L0_ffn_in['b_gate'], 'L0_ffn_W_thr': _L0_ffn_in['W_thr'], 'L0_ffn_b_thr': _L0_ffn_in['b_thr'], 'L0_ffn_W_exp': _L0_ffn_in['W_exp'], 'L0_ffn_b_exp': _L0_ffn_in['b_exp'], 'L1_gnn_W1': _L1_gnn_in['W1'], 'L1_gnn_b1': _L1_gnn_in['b1'], 'L1_gnn_W2': _L1_gnn_in['W2'], 'L1_gnn_b2': _L1_gnn_in['b2'], 'L1_gnn_W3': _L1_gnn_in['W3'], 'L1_gnn_b3': _L1_gnn_in['b3'], 'L1_ffn_expert_weights': _L1_ffn_in['expert_weights'], 'L1_ffn_expert_indices': _L1_ffn_in['expert_indices'], 'L1_ffn_w1': _L1_ffn_in['w1'], 'L1_ffn_w2': _L1_ffn_in['w2']}

def reference(x, adj, nodemask, L0_gnn_Wqk, L0_gnn_Wv, L0_ffn_W_gate, L0_ffn_b_gate, L0_ffn_W_thr, L0_ffn_b_thr, L0_ffn_W_exp, L0_ffn_b_exp, L1_gnn_W1, L1_gnn_b1, L1_gnn_W2, L1_gnn_b2, L1_gnn_W3, L1_gnn_b3, L1_ffn_expert_weights, L1_ffn_expert_indices, L1_ffn_w1, L1_ffn_w2):
    import jax
    import jax.numpy as jnp

    def _L0_gnn_ref(X, adj, mask, Wqk, Wv):
        import jax, jax.numpy as jnp
        import numpy as np
        B, N, IN_DIM, ATT_DIM = (2, 4096, 256, 256)
        qk = X @ Wqk
        q, k = jnp.split(qk, 2, axis=-1)
        v = X @ Wv
        att_dim = q.shape[-1]
        inv_scale = 1.0 / jnp.sqrt(jnp.float32(att_dim))
        k_m = k * mask[:, :, None]
        agg = jnp.einsum('bij,bjd->bid', adj, k_m)
        w = inv_scale * mask * jnp.einsum('bid,bid->bi', q, agg)
        L = jax.nn.softmax(w, axis=1)[:, :, None] * v
        return L

    def _L0_ffn_ref(inputs, W_gate, b_gate, W_thr, b_thr, W_exp, b_exp):
        import jax, jax.numpy as jnp
        import numpy as np
        MAX_THRESHOLD = 0.25
        B, S, D, E = (8, 2048, 256, 8)
        d = inputs.shape[-1]
        x = inputs.reshape(-1, d)
        gate_logits = jax.nn.softmax(x @ W_gate + b_gate, axis=-1)
        thresholds = jax.nn.sigmoid(x @ W_thr + b_thr) * MAX_THRESHOLD
        adapted = gate_logits - thresholds
        selected = (adapted >= 0).astype(x.dtype)
        weights = adapted * selected
        wsum = jnp.sum(weights, axis=-1, keepdims=True)
        wsum = jnp.where(wsum == 0, jnp.ones_like(wsum), wsum)
        weights = weights / wsum
        ex_out = jnp.einsum('td,edf->etf', x, W_exp) + b_exp[:, None, :]
        results = jnp.einsum('etf,te->tf', ex_out, weights)
        return results.reshape(inputs.shape[:-1] + (results.shape[-1],))

    def _L1_gnn_ref(batch_graph, adj, W1, b1, W2, b2, W3, b3):
        import jax, jax.numpy as jnp
        import numpy as np
        B, N, F_IN, F_HID, F_OUT = (32, 512, 256, 256, 256)

        def _gcn_layer(x, adj, W, b):
            support = jnp.einsum('bnf,fh->bnh', x, W)
            return jnp.einsum('bnm,bmh->bnh', adj, support) + b
        x = jax.nn.relu(_gcn_layer(batch_graph, adj, W1, b1))
        x = jax.nn.relu(_gcn_layer(x, adj, W2, b2))
        out = _gcn_layer(x, adj, W3, b3)
        return out

    def _L1_ffn_ref(x, expert_weights, expert_indices, w1, w2):
        import jax, jax.numpy as jnp
        import numpy as np
        NUM_EXPERTS = 8
        TOP_K = 2
        'Dropless MoE: sort assignments by expert, gather tokens, grouped MLP,\n            scatter-combine with top-k router weights (megablocks gather/scatter semantics).'
        in_shape = x.shape
        hs = in_shape[-1]
        x_flat = x.reshape(-1, hs)
        T = x_flat.shape[0]
        flat_ids = expert_indices.reshape(-1)
        order = jnp.argsort(flat_ids)
        bin_ids = flat_ids[order]
        token_ids = order // TOP_K
        xg = x_flat[token_ids]
        y = jnp.zeros_like(xg)
        for e in range(NUM_EXPERTS):
            h = jax.nn.gelu(xg @ w1[e], approximate=False)
            y = jnp.where((bin_ids == e)[:, None], h @ w2[e], y)
        w = expert_weights.reshape(-1)[order][:, None]
        out = jnp.zeros((T, hs), x.dtype).at[token_ids].add(w * y)
        return out.reshape(in_shape)
    x = x + _L0_gnn_ref(_layernorm(x, axis=-1), adj, nodemask, L0_gnn_Wqk, L0_gnn_Wv)
    x = x + _L0_ffn_ref(_layernorm(x, axis=-1), L0_ffn_W_gate, L0_ffn_b_gate, L0_ffn_W_thr, L0_ffn_b_thr, L0_ffn_W_exp, L0_ffn_b_exp)
    x = x + _L1_gnn_ref(_layernorm(x, axis=-1), adj, L1_gnn_W1, L1_gnn_b1, L1_gnn_W2, L1_gnn_b2, L1_gnn_W3, L1_gnn_b3)
    x = x + _L1_ffn_ref(_layernorm(x, axis=-1), L1_ffn_expert_weights, L1_ffn_expert_indices, L1_ffn_w1, L1_ffn_w2)
    return x

_drawn_inputs = setup_inputs


def setup_inputs(seed=0):
    import zlib

    import numpy as np

    out = dict(_drawn_inputs(seed))
    spreads = {'L0_ffn_b_gate': (0.0, 0.1),
     'L0_ffn_b_exp': (0.0, 0.1),
     'L1_gnn_b1': (0.0, 0.1),
     'L1_gnn_b2': (0.0, 0.1),
     'L1_gnn_b3': (0.0, 0.1)}
    factors = {'L0_gnn_Wqk': 3.583, 'L0_gnn_Wv': 2.882}
    for name, (base, spread) in spreads.items():
        noise = np.random.default_rng([zlib.crc32(name.encode()), seed]).standard_normal(out[name].shape)
        drawn = base * np.exp(spread * noise) if base else spread * noise
        out[name] = jnp.asarray(drawn.astype(out[name].dtype))
    for name, factor in factors.items():
        out[name] = (out[name] * factor).astype(out[name].dtype)
    return out
```

```python
from contextlib import ExitStack

import concourse.bass as bass
from concourse import mybir

ALU = mybir.AluOpType
ACT = mybir.ActivationFunctionType
AX = mybir.AxisListType
F32 = mybir.dt.float32
F32R = mybir.dt.float32r
I32 = mybir.dt.int32

P = 128
EPS = 1e-5
MAX_THRESHOLD = 0.25
ENGINES = 5
EXPERT_BANK = (3, 4, 5, 4)


class Graph:

    def __init__(self, n, half, par):
        self.n, self.half, self.par = n, half, par

    def plus(self, k):
        total = self.par + k
        return Graph(self.n + k, self.half + total // 2, total % 2)


def wait_from(eng, sem, value):
    if not (isinstance(value, int) and value <= 0):
        eng.wait_ge(sem, value)


def pairs_of_graphs(eng, body, first, last):
    with eng.Fori(first // 2, last // 2) as half:
        for par in range(2):
            body(Graph(half * 2 + par, half, par))


def split_product(pe, out, lhs, rhs, first, last):
    (lhs_hi, lhs_lo), (rhs_hi, rhs_lo) = lhs, rhs
    pe.matmul(out, lhs_lo, rhs_hi, start=first, stop=False)
    pe.matmul(out, lhs_hi, rhs_lo, start=False, stop=False)
    return pe.matmul(out, lhs_hi, rhs_hi, start=False, stop=last)


def build(nc, x, adj, nodemask, Wqk, Wv, W_gate, b_gate, W_thr, b_thr, W_exp, b_exp,
          W1, b1, W2, b2, W3, b3, moe_weights, moe_indices, moe_w1, moe_w2, out):
    B, N, D = x.shape
    A = Wqk.shape[1] // 2
    E = W_gate.shape[1]
    ME, _, F = moe_w1.shape
    T, TOP = moe_indices.shape
    KD = D // P
    KF = F // P
    TT = T // P
    SLOTS = 256
    HALVES = SLOTS // P
    TILES = (T * TOP + ME * (SLOTS - 1)) // SLOTS
    NG = TT * TOP
    MAXT = T * TOP // SLOTS
    INV = 1.0 / float(A) ** 0.5
    assert N == P and D == A == 2 * P and E == ME == 8

    xg = nc.dram_tensor("routed_x", [TILES * SLOTS, D], F32)
    yg = nc.dram_tensor("routed_y", [TILES * SLOTS, D], F32)

    ctx = ExitStack()
    with ctx:
        def sb(name, shape, dt=F32, stack=ctx):
            return stack.enter_context(nc.sbuf_tensor(name, shape, dt))

        sems = {}

        def sem(name):
            if name not in sems:
                sems[name] = ctx.enter_context(nc.semaphore(name))
            return sems[name]

        bank = [ctx.enter_context(nc.psum_tensor(f"bank{i}", [P, 512], F32)) for i in range(8)]

        ident = sb("ident", [P, P])
        ones = sb("ones", [P, P])
        below = sb("below", [P, P])
        zeros = sb("zeros", [P, D])
        wraw = sb("wraw", [P, 2 * KD * F])
        wsplit = sb("wsplit", [P, 4 * KD * F], F32R)
        gnn_hi = sb("gnn_hi", [P, 3 * KD * D], F32R)
        gnn_lo = sb("gnn_lo", [P, 3 * KD * D], F32R)
        NGATE = E + 2
        gate_raw = sb("gate_raw", [P, KD * NGATE])
        gate_hi = sb("gate_hi", [P, KD * NGATE], F32R)
        gate_lo = sb("gate_lo", [P, KD * NGATE], F32R)
        gate_bias = sb("gate_bias", [P, E + 1])
        bexp = sb("bexp", [E, D])
        b12 = sb("b12", [P, 2 * KD])
        b3_all = sb("b3_all", [P, D])
        mask_rows = sb("mask_rows", [B, P])
        mask_all = sb("mask_all", [P, B])
        w_all = sb("w_all", [P, B])
        p_all = sb("p_all", [P, B])

        ri_i = sb("ri_i", [P, NG], I32)
        rw = sb("rw", [P, NG])
        ri_f = sb("ri_f", [P, NG])
        ends = [sb(f"ends{i}", [P, ME]) for i in range(2)]
        counts = sb("counts", [P, ME])
        ntiles = sb("ntiles", [P, ME])
        base = sb("base", [P, ME])
        steps_i = sb("steps_i", [P, MAXT], I32)
        steps_f = sb("steps_f", [P, MAXT])
        tiles_i = sb("tiles_i", [P, TILES], I32)
        tiles_f = sb("tiles_f", [P, TILES])
        slot_f = sb("slot_f", [P, NG])
        slot_i = sb("slot_i", [P, NG], I32)
        texp_f = sb("texp_f", [P, TILES])
        texp_i = sb("texp_i", [P, TILES], I32)

        xin = [sb(f"xin{i}", [P, D]) for i in range(2)]
        adjin = [sb(f"adjin{i}", [P, P]) for i in range(2)]
        stats = sb("stats", [P, 6])
        mv = sb("mv", [P, 2])
        veps = sb("veps", [P, 1])
        rstd = sb("rstd", [P, 1])
        statsb = sb("statsb", [P, 6])
        mvb = sb("mvb", [P, 2])
        vepsb = sb("vepsb", [P, 1])
        rstdb = sb("rstdb", [P, 1])
        minus_half = sb("minus_half", [P, 1])
        xn = [sb(f"xn{i}", [P, D]) for i in range(2)]
        xT_hi = [sb(f"xT_hi{i}", [P, D], F32R) for i in range(2)]
        xT_lo = [sb(f"xT_lo{i}", [P, D], F32R) for i in range(2)]
        yT_hi = sb("yT_hi", [P, D], F32R)
        yT_lo = sb("yT_lo", [P, D], F32R)
        mcol = [sb(f"mcol{i}", [P, 1]) for i in range(2)]
        wcol = [sb(f"wcol{i}", [P, 1]) for i in range(2)]
        adjTm = [sb(f"adjTm{i}", [P, P]) for i in range(2)]
        agg_sb = [sb(f"agg_sb{i}", [P, D]) for i in range(2)]
        x1 = [sb(f"x1_{i}", [P, D]) for i in range(2)]
        x2 = [sb(f"x2_{i}", [P, D]) for i in range(2)]
        x2b = [sb(f"x2b_{i}", [P, D]) for i in range(2)]
        xo = [sb(f"xo{i}", [P, D]) for i in range(2)]
        gl = sb("gl", [P, E + 1])
        gmx = sb("gmx", [P, 1])
        gx = sb("gx", [P, E + 1])
        ge = sb("ge", [P, E + 1])
        gden = sb("gden", [P, 2])
        grec = sb("grec", [P, 2])
        gthr = sb("gthr", [P, 1])
        gad = sb("gad", [P, E])
        gsel = sb("gsel", [P, E])
        gsum = sb("gsum", [P, 1])
        gsum1 = sb("gsum1", [P, 1])
        gri = sb("gri", [P, 1])
        gw = sb("gw", [P, E])
        gwT = sb("gwT", [E, P])
        adjTs = [sb(f"adjTs{i}", [P, P]) for i in range(2)]
        sup = [sb(f"sup{i}", [P, D]) for i in range(3)]
        hid = [sb(f"hid{i}", [P, D]) for i in range(2)]
        hid_hi = [sb(f"hid_hi{i}", [P, D], F32R) for i in range(2)]
        hid_lo = [sb(f"hid_lo{i}", [P, D], F32R) for i in range(2)]
        sx = sb("sx", [P, D])
        sidx = sb("sidx", [P, TOP], I32)
        wmx = sb("wmx", [B, 1])
        wneg = sb("wneg", [B, 1])
        wrow = sb("wrow", [B, P])
        wsm = sb("wsm", [B, 1])
        wrc = sb("wrc", [B, 1])
        prow = sb("prow", [B, P])

        early = ExitStack()
        v_all = sb("v_all", [P, B * D], F32, early)
        adjT_all = sb("adjT_all", [P, B * P], F32, early)
        mv_hi = sb("mv_hi", [P, KD * 2 * D], F32R, early)
        mv_lo = sb("mv_lo", [P, KD * 2 * D], F32R, early)
        early.close()
        late = ExitStack()
        mx = sb("mx", [P, HALVES * D], F32, late)
        mxn = sb("mxn", [P, HALVES * D], F32, late)
        mT_hi = sb("mT_hi", [P, KD * SLOTS], F32R, late)
        mT_lo = sb("mT_lo", [P, KD * SLOTS], F32R, late)
        hf = [sb(f"hf{i}", [P, 512], F32, late) for i in range(2)]
        h_hi = sb("h_hi", [P, KF * SLOTS], F32R, late)
        h_lo = sb("h_lo", [P, KF * SLOTS], F32R, late)
        my = sb("my", [P, HALVES * D], F32, late)
        fx = [sb(f"fx{i}", [P, D], F32, late) for i in range(2)]
        fy = [[sb(f"fy{i}_{k}", [P, D], F32, late) for k in range(TOP)] for i in range(2)]
        facc = [sb(f"facc{i}", [P, D], F32, late) for i in range(2)]
        fo = [sb(f"fo{i}", [P, D], F32, late) for i in range(2)]
        late.close()
        setup = ExitStack()
        qkv_raw = sb("qkv_raw", [P, KD * (2 * A + D)], F32, setup)
        qkT = sb("qkT", [P, 2 * KD * D], F32, setup)
        gnn_raw = sb("gnn_raw", [P, 3 * KD * D], F32, setup)
        mv_f = sb("mv_f", [P, KD * 2 * D], F32, setup)
        onehot = sb("onehot", [P, ME * NG], F32, setup)
        scan = [sb(f"scan{i}", [P, ME * NG], F32, setup) for i in range(2)]
        ranks = sb("ranks", [P, ME * NG], F32, setup)
        cmp_n = sb("cmp_n", [P, ME * MAXT], F32, setup)
        cmp_t = sb("cmp_t", [P, TILES * ME], F32, setup)
        setup.close()

        mvh, mvl = (t[:, :].rearrange("p (k n) -> p k n", k=KD) for t in (mv_hi, mv_lo))
        gnh, gnl = (t[:, :].rearrange("p (l k n) -> p l k n", l=3, k=KD) for t in (gnn_hi, gnn_lo))
        HW = KD * F
        exh, exl = (wsplit[:, i * 2 * HW:(i + 1) * 2 * HW].rearrange("p (k n) -> p k n", k=KD) for i in range(2))
        m1h, m1l = (wsplit[:, i * HW:(i + 1) * HW].rearrange("p (k n) -> p k n", k=KD) for i in range(2))
        m2h, m2l = (wsplit[:, (2 + i) * HW:(3 + i) * HW].rearrange("p (k n) -> p k n", k=KF) for i in range(2))
        oh3 = onehot[:, :].rearrange("p (e g) -> p e g", e=ME)
        sc3 = [s[:, :].rearrange("p (e g) -> p e g", e=ME) for s in scan]
        rk3 = ranks[:, :].rearrange("p (e g) -> p e g", e=ME)

        block = ctx.enter_context(nc.Block())

        def phase_end(eng, k):
            eng.drain().then_inc(sem("phase_done"), 1)
            eng.wait_ge(sem("phase_done"), ENGINES * k)

        def own_wait(eng, *waits):
            for s, v in waits:
                wait_from(eng, s, v)
            eng.sem_inc(sem("passed"), 1)

        def norm_stats(dve, src, bufs, name, n):
            st, mean_var, veps, _ = bufs
            step = sem(name + "_step")
            nc.vector.bn_stats(st[:, :], src).then_inc(step, 1)
            own_wait(dve, (step, n * 3 + 1))
            nc.vector.bn_aggr(mean_var[:, :], st[:, :]).then_inc(step, 1)
            dve.wait_ge(step, n * 3 + 2)
            nc.vector.tensor_scalar(veps[:, :], mean_var[:, 1:2], EPS, None, ALU.add).then_inc(step, 1)

        def norm_rstd(pool, bufs, name, n):
            _, _, veps, rs = bufs
            pool.wait_ge(sem(name + "_step"), n * 3 + 3)
            nc.gpsimd.tensor_tensor(rs[:, :], veps[:, :], minus_half[:, :], ALU.pow).then_inc(
                sem(name + "_rstd"), 1)

        def norm_apply(dve, src, dst, bufs, name, n):
            _, mean_var, _, rs = bufs
            dve.wait_ge(sem(name + "_rstd"), n + 1)
            nc.vector.tensor_scalar(dst, src, mean_var[:, 0:1], rs[:, 0:1], ALU.subtract, ALU.mult).then_inc(
                sem(name + "_normed"), 1)

        LNA, LNB = (stats, mv, veps, rstd), (statsb, mvb, vepsb, rstdb)

        @block.sync
        def _(sp):
            sp.dma_start(qkv_raw[:, 0:KD * 2 * A].rearrange("p (k n) -> p k n", k=KD),
                         Wqk.rearrange("(k p) n -> p k n", p=P)).then_inc(sem("qkv_in"), 16)
            sp.dma_start(qkv_raw[:, KD * 2 * A:].rearrange("p (k n) -> p k n", k=KD),
                         Wv.rearrange("(k p) n -> p k n", p=P)).then_inc(sem("qkv_in"), 16)
            sp.dma_start(mask_rows[:, :], nodemask).then_inc(sem("mask_in"), 16)
            sp.dma_start(ri_i[:, :].rearrange("p (c k) -> p c k", k=TOP),
                         moe_indices.rearrange("(c p) k -> p c k", p=P)).then_inc(sem("route_in"), 16)
            sp.dma_start(rw[:, :].rearrange("p (c k) -> p c k", k=TOP),
                         moe_weights.rearrange("(c p) k -> p c k", p=P)).then_inc(sem("route_w_in"), 16)
            for l, w in enumerate((W1, W2, W3)):
                sp.dma_start(gnn_raw[:, l * KD * D:(l + 1) * KD * D].rearrange("p (k n) -> p k n", k=KD),
                             w.rearrange("(k p) n -> p k n", p=P)).then_inc(sem("gnn_in"), 16)
            sp.wait_ge(sem("gate_zeroed"), 1)
            gr = gate_raw[:, :].rearrange("p (k n) -> p k n", k=KD)
            sp.dma_start(gr[:, :, 0:E], W_gate.rearrange("(k p) n -> p k n", p=P)).then_inc(sem("gate_in"), 16)
            sp.dma_start(gr[:, :, E:E + 1], W_thr.rearrange("(k p) n -> p k n", p=P), allow_slow_non_contiguous=True).then_inc(sem("gate_in"), 16)
            sp.dma_start(gate_bias[:, 0:E], b_gate.partition_broadcast(P)).then_inc(sem("gate_in"), 16)
            sp.dma_start(gate_bias[:, E:E + 1], b_thr.partition_broadcast(P)).then_inc(sem("gate_in"), 16)
            sp.dma_start(bexp[:, :], b_exp).then_inc(sem("bias_in"), 16)
            sp.dma_start(b3_all[:, :], b3.partition_broadcast(P)).then_inc(sem("bias_in"), 16)
            for l, b in enumerate((b1, b2)):
                sp.dma_start(b12[:, l * KD:(l + 1) * KD], b.rearrange("(k p) -> p k", p=P), allow_slow_non_contiguous=True).then_inc(
                    sem("bias_in"), 16)
            wv = wraw[:, :].rearrange("p (k e n) -> p k e n", k=KD, e=E)
            for e in range(E):
                sp.dma_start(wv[:, :, e, :], W_exp[e].rearrange("(k p) n -> p k n", p=P)).then_inc(
                    sem("experts_in"), 16)
            sp.wait_ge(sem("zeroed"), 1)
            for i in range(TILES * HALVES):
                sp.dma_start(xg[i * P:(i + 1) * P, :], zeros[:, :]).then_inc(sem("slots_zeroed"), 16)
            phase_end(sp, 1)

            def load1(g):
                wait_from(sp, sem("a_normed"), g.n - 1)
                sp.dma_start(xin[g.par][:, :], x[bass.ds(g.n, 1)].rearrange("o p d -> (o p) d")).then_inc(
                    sem(f"x_in{g.par}"), 16)
                wait_from(sp, sem("a_turned"), g.n - 1)
                sp.dma_start(adjin[g.par][:, :], adj[bass.ds(g.n, 1)].rearrange("o p d -> (o p) d")).then_inc(
                    sem(f"adj_in{g.par}"), 16)

            for n in range(2):
                load1(Graph(n, 0, n))
            pairs_of_graphs(sp, load1, 2, B)
            phase_end(sp, 2)

            def load2(g):
                wait_from(sp, sem("x1_ready"), g.n - 1)
                sp.dma_start(xin[g.par][:, :], x[bass.ds(g.n, 1)].rearrange("o p d -> (o p) d")).then_inc(
                    sem(f"x_in{g.par}"), 16)

            def store(g):
                sp.wait_ge(sem("x3_ready"), g.n + 1)
                sp.dma_start(out[bass.ds(g.n, 1)].rearrange("o p d -> (o p) d"), xo[g.par][:, :]).then_inc(
                    sem(f"x3_out{g.par}"), 16)

            def step(g):
                load2(g.plus(2))
                store(g.plus(-2))

            for n in range(4):
                load2(Graph(n, n // 2, n % 2))
            pairs_of_graphs(sp, step, 2, B - 2)
            for n in range(B - 2, B + 2):
                store(Graph(n - 2, n // 2 - 1, n % 2))
            for par in range(2):
                sp.wait_ge(sem(f"x3_out{par}"), 16 * (B // 2))
            phase_end(sp, 3)

            def load_rows(j):
                for h in range(HALVES):
                    wait_from(sp, sem(f"m{h}_normed"), j)
                sp.dma_start(mx[:, :].rearrange("p (h d) -> p h d", h=HALVES),
                             xg[bass.ds(j * SLOTS, SLOTS), :].rearrange("(h p) d -> p h d", p=P)).then_inc(
                    sem("rows_in"), 16)

            def load_weights(j):
                e = sp.value_load(texp_i[0:1, bass.ds(j, 1)], min_val=0, max_val=ME - 1)
                wait_from(sp, sem("w1_split"), j)
                sp.dma_start(wraw[:, 0:HW].rearrange("p (k n) -> p k n", k=KD),
                             moe_w1[bass.ds(e, 1)].rearrange("o (k p) n -> p (o k) n", p=P)).then_inc(
                    sem("w1_in"), 16)
                wait_from(sp, sem("w2_split"), j)
                sp.dma_start(wraw[:, HW:2 * HW].rearrange("p (k n) -> p k n", k=KF),
                             moe_w2[bass.ds(e, 1)].rearrange("o (k p) n -> p (o k) n", p=P)).then_inc(
                    sem("w2_in"), 16)

            def store_tile(j):
                sp.wait_ge(sem("y_ready"), j + 1)
                sp.dma_start(yg[bass.ds(j * SLOTS, SLOTS), :].rearrange("(h p) d -> p h d", p=P),
                             my[:, :].rearrange("p (h d) -> p h d", h=HALVES)).then_inc(sem("y_out"), 16)

            load_rows(0)
            load_weights(0)
            load_rows(1)
            load_weights(1)
            load_rows(2)
            with sp.Fori(0, TILES - 3) as j:
                store_tile(j)
                load_weights(j + 2)
                load_rows(j + 3)
            store_tile(TILES - 3)
            load_weights(TILES - 1)
            store_tile(TILES - 2)
            store_tile(TILES - 1)
            sp.wait_ge(sem("y_out"), 16 * TILES)
            phase_end(sp, 4)

            def load3(g):
                wait_from(sp, sem("f1"), g.n - 1)
                sp.dma_start(fx[g.par][:, :], out[bass.ds(g.n, 1)].rearrange("o p d -> (o p) d")).then_inc(
                    sem(f"fx_in{g.par}"), 16)

            def store3(g):
                sp.wait_ge(sem("f2"), g.n + 1)
                sp.dma_start(out[bass.ds(g.n, 1)].rearrange("o p d -> (o p) d"), fo[g.par][:, :]).then_inc(
                    sem(f"fo_out{g.par}"), 16)

            def step3(g):
                load3(g)
                store3(g.plus(-2))

            for n in range(2):
                load3(Graph(n, 0, n))
            pairs_of_graphs(sp, step3, 2, TT)
            for n in range(TT, TT + 2):
                store3(Graph(n - 2, n // 2 - 1, n % 2))
            for par in range(2):
                sp.wait_ge(sem(f"fo_out{par}"), 16 * (TT // 2))

        @block.gpsimd
        def _(pool):
            nc.gpsimd.memset(gate_raw[:, :], 0.0).then_inc(sem("gate_zeroed"), 1)
            nc.gpsimd.memset(minus_half[:, :], -0.5).then_inc(sem("minus_half_set"), 1)
            nc.gpsimd.memset(zeros[:, :], 0.0).then_inc(sem("zeroed"), 1)
            nc.gpsimd.memset(ones[:, :], 1.0).then_inc(sem("ones_set"), 1)
            nc.gpsimd.memset(ident[:, :], 0.0).then_inc(sem("ident_zeroed"), 1)
            pool.wait_ge(sem("ident_zeroed"), 1)
            nc.gpsimd.affine_select(out=ident[:, :], in_=ident[:, :], compare_op=ALU.not_equal, fill=1.0,
                                    base=0, pattern=[[-1, P]], channel_multiplier=1).then_inc(sem("ident_set"), 1)
            pool.wait_ge(sem("ones_set"), 1)
            nc.gpsimd.affine_select(out=below[:, :], in_=ones[:, :], compare_op=ALU.is_gt, fill=0.0,
                                    base=0, pattern=[[1, P]], channel_multiplier=-1).then_inc(sem("below_set"), 1)
            nc.gpsimd.iota(steps_i[:, :], pattern=[[SLOTS, MAXT]], base=0, channel_multiplier=0).then_inc(
                sem("iotas_set"), 1)
            nc.gpsimd.iota(tiles_i[:, :], pattern=[[1, TILES]], base=0, channel_multiplier=0).then_inc(
                sem("iotas_set"), 1)
            phase_end(pool, 1)
            pool.wait_ge(sem("minus_half_set"), 1)
            norm_rstd(pool, LNA, "a", 0)
            with pool.Fori(1, B) as n:
                norm_rstd(pool, LNA, "a", n)
            phase_end(pool, 2)

            def split_hidden(l, g):
                own_wait(pool, (sem(f"hid{l}_ready"), g.n + 1), (sem(f"sup{l + 1}_done"), g.n))
                nc.gpsimd.tensor_copy(hid_hi[l][:, :], hid[l][:, :]).then_inc(sem(f"hid{l}_hi"), 1)
                pool.wait_ge(sem(f"hid{l}_hi"), g.n + 1)
                nc.gpsimd.tensor_tensor(hid_lo[l][:, :], hid[l][:, :], hid_hi[l][:, :].bitcast(F32),
                                        ALU.subtract).then_inc(sem(f"hid{l}_split"), 1)

            def take_adj(g):
                own_wait(pool, (sem("x3_summed"), g.n - 1))
                nc.gpsimd.tensor_copy(adjTs[g.par][:, :], adjT_all[:, bass.ds(g.n * P, P)]).then_inc(
                    sem("adjTs_ready"), 1)

            def add_b3(g):
                pool.wait_ge(sem("combined"), g.n * 9 + 9)
                wait_from(pool, sem("x3_ready"), g.n - 1)
                nc.gpsimd.tensor_tensor(x2b[g.par][:, :], x2[g.par][:, :], b3_all[:, :], ALU.add).then_inc(
                    sem("x2b_ready"), 1)

            def step(g, a=True, nxt=True, b1=True, b2=True):
                if b1:
                    take_adj(g.plus(-1))
                    add_b3(g.plus(-1))
                if nxt:
                    norm_rstd(pool, LNA, "c", g.n + 1)
                if b2:
                    split_hidden(1, g.plus(-2))
                if b1:
                    split_hidden(0, g.plus(-1))
                if a:
                    norm_rstd(pool, LNB, "d", g.n)

            def route(c):
                own_wait(pool, (sem("scattered"), c * (16 * TOP)))
                pool.dma_start(sx[:, :], out[bass.ds(c, 1)].rearrange("o p d -> (o p) d")).then_inc(
                    sem("sx_in"), 16)
                nc.gpsimd.tensor_copy(sidx[:, :], slot_i[:, bass.ds(c * TOP, TOP)]).then_inc(sem("sidx_ready"), 1)

            def scatter(c):
                own_wait(pool, (sem("sx_in"), (c + 1) * 16), (sem("sidx_ready"), c + 1))
                for k in range(TOP):
                    nc.gpsimd.indirect_dma_start(
                        out=xg[:, :], out_offset=bass.IndirectOffsetOnAxis(ap=sidx[:, k:k + 1], axis=0),
                        in_=sx[:, :], in_offset=None).then_inc(sem("scattered"), 16)

            LEAD = TT + 4
            norm_rstd(pool, LNA, "c", 0)
            step(Graph(0, 0, 0), b1=False, b2=False)
            step(Graph(1, 0, 1), b2=False)
            pairs_of_graphs(pool, step, 2, LEAD)
            for par in range(2):
                pool.wait_ge(sem(f"x3_out{par}"), 16 * (TT // 2))
            pool.wait_ge(sem("slots_zeroed"), 16 * TILES * HALVES)

            def routed_pair(half):
                g = Graph(half * 2, half, 0)
                step(g)
                route(half - LEAD // 2)
                step(g.plus(1))
                scatter(half - LEAD // 2)

            routed_pair(LEAD // 2)
            with pool.Fori(LEAD // 2 + 1, LEAD // 2 + TT) as half:
                routed_pair(half)
            pairs_of_graphs(pool, step, LEAD + 2 * TT, B - 2)
            step(Graph(B - 2, B // 2 - 1, 0))
            step(Graph(B - 1, B // 2 - 1, 1), nxt=False)
            step(Graph(B, B // 2, 0), a=False, nxt=False)
            step(Graph(B + 1, B // 2, 1), a=False, nxt=False, b1=False)
            pool.wait_ge(sem("scattered"), 16 * TOP * TT)
            phase_end(pool, 3)

            def rstd_rows(j):
                for h in range(HALVES):
                    norm_rstd(pool, (LNA, LNB)[h], f"m{h}", j)

            def split_h(j):
                for q in range(KF // 2):
                    pool.wait_ge(sem("h_hi"), j * (KF // 2) + (q + 1))
                    nc.gpsimd.tensor_tensor(h_lo[:, q * 512:(q + 1) * 512], hf[q % 2][:, :],
                                            h_hi[:, q * 512:(q + 1) * 512].bitcast(F32),
                                            ALU.subtract).then_inc(sem("h_split"), 1)

            rstd_rows(0)
            rstd_rows(1)
            split_h(0)
            rstd_rows(2)
            with pool.Fori(1, TILES - 2) as j:
                split_h(j)
                rstd_rows(j + 2)
            split_h(TILES - 2)
            split_h(TILES - 1)
            phase_end(pool, 4)

            def gather(g):
                own_wait(pool, (sem("f2"), g.n - 1))
                nc.gpsimd.tensor_copy(sidx[:, :], slot_i[:, bass.ds(g.n * TOP, TOP)]).then_inc(
                    sem("gidx_ready"), 1)
                own_wait(pool, (sem("gidx_ready"), g.n + 1))
                for k in range(TOP):
                    nc.gpsimd.indirect_dma_start(
                        out=fy[g.par][k][:, :], out_offset=None, in_=yg[:, :],
                        in_offset=bass.IndirectOffsetOnAxis(ap=sidx[:, k:k + 1], axis=0)).then_inc(
                        sem(f"fy_in{g.par}"), 16)
                own_wait(pool, (sem(f"fy_in{g.par}"), (g.half + 1) * (16 * TOP)))

            for n in range(2):
                gather(Graph(n, 0, n))
            pairs_of_graphs(pool, gather, 2, TT)

        @block.scalar
        def _(act):
            def copy_const(dst, src, name):
                return nc.scalar.copy(dst, src).then_inc(sem(name), 1)

            act.wait_ge(sem("experts_in"), 16 * E)
            for i in range(2):
                copy_const(exh[:, i, :], wraw[:, i * 2 * P * 8:(i + 1) * 2 * P * 8], "experts_hi")
            act.wait_ge(sem("gnn_in"), 48)
            copy_const(gnn_hi[:, :], gnn_raw[:, :], "gnn_hi")
            act.wait_ge(sem("gate_in"), 64)
            copy_const(gate_hi[:, :], gate_raw[:, :], "gate_hi")
            act.wait_ge(sem("mv_ready"), KD + 1)
            copy_const(mv_hi[:, :], mv_f[:, :], "mv_hi")
            phase_end(act, 1)

            def first(g):
                act.wait_ge(sem("a_turned"), g.n + 1)
                wait_from(act, sem("qv_done"), g.n - 1)
                nc.scalar.copy(xT_hi[g.par][:, :], bank[g.par][:, 0:D]).then_inc(sem("a_hi"), 1)
                nc.scalar.copy(adjT_all[:, bass.ds(g.n * P, P)], bank[2 + g.par][:, 0:P]).then_inc(
                    sem("adjT_kept"), 1)
                act.wait_ge(sem("mcol_ready"), g.n + 1)
                wait_from(act, sem("agg_done"), g.n - 1)
                nc.scalar.activation(adjTm[g.par][:, :], bank[2 + g.par][:, 0:P], ACT.Copy,
                                     scale=mcol[g.par][:, 0:1]).then_inc(sem("adjTm_ready"), 1)

            def second(g):
                act.wait_ge(sem("qv_done"), g.n + 1)
                nc.scalar.copy(v_all[:, bass.ds(g.n * D, D)], bank[4 + g.par][:, D:2 * D]).then_inc(
                    sem("v_kept"), 1)
                act.wait_ge(sem("agg_done"), g.n + 1)
                wait_from(act, sem("w_dotted"), g.n - 1)
                nc.scalar.copy(agg_sb[g.par][:, :], bank[6 + g.par][:, 0:D]).then_inc(sem("agg_kept"), 1)

            def both(g):
                first(g)
                second(g.plus(-1))

            first(Graph(0, 0, 0))
            both(Graph(1, 0, 1))
            pairs_of_graphs(act, both, 2, B)
            second(Graph(B - 1, B // 2 - 1, 1))
            act.wait_ge(sem("wneg_ready"), 1)
            nc.scalar.activation(wrow[:, :], bank[0][0:B, 0:P], ACT.Exp, bias=wneg[:, 0:1],
                                 accum_out=wsm[:, :]).then_inc(sem("wexp_ready"), 1)
            phase_end(act, 2)

            def gate_exp(g):
                act.wait_ge(sem("gx_ready"), 2 * g.n + 2)
                nc.scalar.activation(ge[:, :], gx[:, :], ACT.Exp).then_inc(sem("ge_ready"), 1)

            def keep_sup(l, g):
                act.wait_ge(sem(f"sup{l}_done"), g.n + 1)
                wait_from(act, sem("x3_summed" if l == 2 else f"agg{l}_done"), g.n)
                nc.scalar.copy(sup[l][:, :], bank[6][:, 0:D]).then_inc(sem(f"sup{l}_kept"), 1)

            def relu(l, g):
                act.wait_ge(sem(f"agg{l}_done"), g.n + 1)
                wait_from(act, sem(f"hid{l}_split"), g.n)
                for c in range(KD):
                    last = nc.scalar.activation(hid[l][:, c * P:(c + 1) * P], bank[7][:, c * P:(c + 1) * P],
                                                ACT.Relu, bias=b12[:, l * KD + c:l * KD + c + 1])
                last.then_inc(sem(f"hid{l}_ready"), 1)

            def hi_a(g):
                act.wait_ge(sem("c_turned"), g.n + 1)
                wait_from(act, sem("experts_done"), 4 * (g.n - 1))
                nc.scalar.copy(xT_hi[g.par][:, :], bank[0][:, 0:D]).then_inc(sem("c_hi"), 1)

            def hi_b(g):
                act.wait_ge(sem("d_turned"), g.n + 1)
                wait_from(act, sem("sup0_done"), g.n)
                nc.scalar.copy(yT_hi[:, :], bank[1][:, 0:D]).then_inc(sem("d_hi"), 1)

            def keep_gwT(g):
                act.wait_ge(sem("gw_turned"), g.n + 1)
                nc.scalar.copy(gwT[:, :], bank[2][0:E, P:2 * P]).then_inc(sem("gwT_kept"), 1)

            def step(g, a=True, nxt=True, b1=True, b2=True):
                one, two = g.plus(-1), g.plus(-2)
                if b2:
                    keep_sup(1, two)
                if b1:
                    hi_b(one)
                if b2:
                    relu(1, two)
                if b1:
                    keep_sup(0, one)
                if a:
                    keep_gwT(g)
                if nxt:
                    hi_a(g.plus(1))
                if b1:
                    relu(0, one)
                if b2:
                    keep_sup(2, two)
                if nxt:
                    gate_exp(g.plus(1))

            act.wait_ge(sem("bias_in"), 64)
            hi_a(Graph(0, 0, 0))
            gate_exp(Graph(0, 0, 0))
            step(Graph(0, 0, 0), b1=False, b2=False)
            step(Graph(1, 0, 1), b2=False)
            pairs_of_graphs(act, step, 2, B - 2)
            step(Graph(B - 2, B // 2 - 1, 0))
            step(Graph(B - 1, B // 2 - 1, 1), nxt=False)
            step(Graph(B, B // 2, 0), a=False, nxt=False)
            step(Graph(B + 1, B // 2, 1), a=False, nxt=False, b1=False)
            phase_end(act, 3)

            def prepare(j):
                act.wait_ge(sem("m_turned"), j + 1)
                wait_from(act, sem("layer1_done"), 4 * j)
                nc.scalar.copy(mT_hi[:, :], bank[0][:, :]).then_inc(sem("m_hi"), 1)
                act.wait_ge(sem("w1_in"), (j + 1) * 16)
                for k in range(KD):
                    nc.scalar.copy(m1h[:, k, :], wraw[:, k * F:(k + 1) * F]).then_inc(sem("w1_hi"), 1)

            def middle(j):
                wait_from(act, sem("layer2_done"), j)
                act.wait_ge(sem("w2_in"), (j + 1) * 16)
                for q in range(2):
                    nc.scalar.copy(wsplit[:, 2 * HW + q * HW // 2:2 * HW + (q + 1) * HW // 2],
                                   wraw[:, HW + q * HW // 2:HW + (q + 1) * HW // 2]).then_inc(sem("w2_hi"), 1)
                for q in range(KF // 2):
                    act.wait_ge(sem("layer1_done"), j * 4 + (q + 1))
                    wait_from(act, sem("h_split"), j * 4 + (q - 1))
                    nc.scalar.activation(hf[q % 2][:, :], bank[2 + q][:, :], ACT.Gelu).then_inc(sem("gelu"), 1)

            def keep_y(j):
                act.wait_ge(sem("layer2_done"), j + 1)
                wait_from(act, sem("y_out"), j * 16)
                nc.scalar.copy(my[:, :], bank[1][:, :]).then_inc(sem("y_ready"), 1)

            prepare(0)
            middle(0)
            prepare(1)
            with act.Fori(1, TILES - 1) as j:
                keep_y(j - 1)
                middle(j)
                prepare(j + 1)
            keep_y(TILES - 2)
            middle(TILES - 1)
            keep_y(TILES - 1)
            phase_end(act, 4)

        @block.vector
        def _(dve):
            count = 0

            def step_done(ins):
                nonlocal count
                ins.then_inc(sem("routed"), 1)
                count += 1
                return count

            dve.wait_ge(sem("route_in"), 16)
            indices = step_done(nc.vector.tensor_copy(ri_f[:, :], ri_i[:, :]))
            dve.wait_ge(sem("iotas_set"), 2)
            step_done(nc.vector.tensor_copy(steps_f[:, :], steps_i[:, :]))
            iotas = step_done(nc.vector.tensor_copy(tiles_f[:, :], tiles_i[:, :]))
            dve.wait_ge(sem("routed"), indices)
            for e in range(ME):
                nc.vector.tensor_scalar(oh3[:, e, :], ri_f[:, :], float(e), None, ALU.is_equal).then_inc(
                    sem("onehot"), 1)
            dve.wait_ge(sem("totals_done"), 1)

            def running_sum(bufs, width):
                cur, shift = 0, 1
                while shift < width:
                    dve.wait_ge(sem("routed"), count)
                    src, dst = bufs[cur], bufs[1 - cur]
                    step_done(nc.vector.tensor_tensor(dst[..., shift:], src[..., shift:], src[..., :width - shift],
                                                      ALU.add))
                    step_done(nc.vector.tensor_copy(dst[..., :shift], src[..., :shift]))
                    cur, shift = 1 - cur, shift * 2
                dve.wait_ge(sem("routed"), count)
                return cur

            step_done(nc.vector.tensor_copy(scan[0][:, :], bank[1][:, 0:ME * NG]))
            cur = running_sum(sc3, NG)
            step_done(nc.vector.tensor_copy(counts[:, :], sc3[cur][:, :, NG - 1]))
            dve.wait_ge(sem("routed"), step_done(nc.vector.tensor_tensor(
                ranks[:, :], scan[cur][:, :], bank[1][:, 0:ME * NG], ALU.subtract)))
            step_done(nc.vector.tensor_tensor(ranks[:, :], ranks[:, :], bank[1][:, ME * NG:2 * ME * NG], ALU.add))
            dve.wait_ge(sem("routed"), step_done(nc.vector.tensor_tensor(
                cmp_n[:, :].rearrange("p (e m) -> p e m", e=ME),
                counts[:, :].unsqueeze(2).broadcast_to([P, ME, MAXT]),
                steps_f[:, :].unsqueeze(1).broadcast_to([P, ME, MAXT]), ALU.is_gt)))
            dve.wait_ge(sem("routed"), step_done(nc.vector.tensor_reduce(
                ntiles[:, :], cmp_n[:, :].rearrange("p (e m) -> p e m", e=ME), AX.X, ALU.add)))
            step_done(nc.vector.tensor_copy(ends[0][:, :], ntiles[:, :]))
            cur = running_sum([t[:, :] for t in ends], ME)
            step_done(nc.vector.tensor_tensor(base[:, :], ends[cur][:, :], ntiles[:, :], ALU.subtract))
            dve.wait_ge(sem("routed"), step_done(nc.vector.tensor_tensor(
                cmp_t[:, :].rearrange("p (t e) -> p t e", e=ME),
                tiles_f[:, :].unsqueeze(2).broadcast_to([P, TILES, ME]),
                ends[cur][:, :].unsqueeze(1).broadcast_to([P, TILES, ME]), ALU.is_ge)))
            dve.wait_ge(sem("routed"), step_done(nc.vector.tensor_reduce(
                texp_f[:, :], cmp_t[:, :].rearrange("p (t e) -> p t e", e=ME), AX.X, ALU.add)))
            step_done(nc.vector.tensor_scalar(texp_i[:, :], texp_f[:, :], float(ME - 1), None, ALU.min))
            dve.wait_ge(sem("routed"), step_done(nc.vector.tensor_scalar(
                counts[:, :], base[:, :], float(SLOTS), None, ALU.mult)))
            for e in range(ME):
                step_done(nc.vector.scalar_tensor_tensor(
                    out=sc3[0][:, e, :], in0=rk3[:, e, :], scalar=counts[:, e:e + 1], in1=oh3[:, e, :],
                    op0=ALU.add, op1=ALU.mult))
            dve.wait_ge(sem("routed"), count)
            dve.wait_ge(sem("routed"), step_done(nc.vector.tensor_reduce(
                slot_f[:, :], scan[0][:, :].rearrange("p (e g) -> p g e", e=ME), AX.X, ALU.add)))
            step_done(nc.vector.tensor_copy(slot_i[:, :], slot_f[:, :]))
            dve.wait_ge(sem("mask_turned"), 1)
            nc.vector.tensor_copy(mask_all[:, :], bank[2][:, 0:B]).then_inc(sem("mask_ready"), 1)
            for c in range(2):
                dve.wait_ge(sem("qk_turned"), c + 1)
                nc.vector.tensor_copy(qkT[:, c * 512:(c + 1) * 512], bank[3 + c][:, :]).then_inc(sem("qkT_kept"), 1)
            mvf = mv_f[:, :].rearrange("p (k n) -> p k n", k=KD)
            dve.wait_ge(sem("m_done"), 1)
            for k in range(KD):
                nc.vector.tensor_copy(mvf[:, k, 0:D], bank[5][:, k * D:(k + 1) * D]).then_inc(sem("mv_ready"), 1)
            dve.wait_ge(sem("qkv_in"), 32)
            nc.vector.tensor_copy(mvf[:, :, D:2 * D],
                                  qkv_raw[:, KD * 2 * A:].rearrange("p (k n) -> p k n", k=KD)).then_inc(
                sem("mv_ready"), 1)
            dve.wait_ge(sem("experts_hi"), 2)
            for i in range(2):
                nc.vector.tensor_tensor(exl[:, i, :], wraw[:, i * HW:(i + 1) * HW], exh[:, i, :].bitcast(F32),
                                        ALU.subtract).then_inc(sem("experts_split"), 1)
            dve.wait_ge(sem("gnn_hi"), 1)
            nc.vector.tensor_tensor(gnn_lo[:, :], gnn_raw[:, :], gnn_hi[:, :].bitcast(F32),
                                    ALU.subtract).then_inc(sem("gnn_split"), 1)
            dve.wait_ge(sem("gate_hi"), 1)
            nc.vector.tensor_tensor(gate_lo[:, :], gate_raw[:, :], gate_hi[:, :].bitcast(F32),
                                    ALU.subtract).then_inc(sem("gate_split"), 1)
            dve.wait_ge(sem("mv_hi"), 1)
            nc.vector.tensor_tensor(mv_lo[:, :], mv_f[:, :], mv_hi[:, :].bitcast(F32),
                                    ALU.subtract).then_inc(sem("mv_split"), 1)
            phase_end(dve, 1)

            def stats_first(g):
                dve.wait_ge(sem(f"x_in{g.par}"), (g.half + 1) * 16)
                norm_stats(dve, xin[g.par][:, :], LNA, "a", g.n)

            def norm_first(g):
                wait_from(dve, sem("adjTm_ready"), g.n - 1)
                nc.vector.tensor_copy(mcol[g.par][:, :], mask_all[:, bass.ds(g.n, 1)]).then_inc(
                    sem("mcol_ready"), 1)
                wait_from(dve, sem("agg_done"), g.n - 1)
                norm_apply(dve, xin[g.par][:, :], xn[g.par][:, :], LNA, "a", g.n)

            def low_first(g):
                dve.wait_ge(sem("a_hi"), g.n + 1)
                wait_from(dve, sem("qv_done"), g.n - 1)
                nc.vector.tensor_tensor(xT_lo[g.par][:, :], bank[g.par][:, 0:D], xT_hi[g.par][:, :].bitcast(F32),
                                        ALU.subtract).then_inc(sem("a_split"), 1)

            def dot(g):
                dve.wait_ge(sem("v_kept"), g.n + 1)
                dve.wait_ge(sem("agg_kept"), g.n + 1)
                nc.vector.tensor_tensor_reduce(out=agg_sb[g.par][:, :], in0=bank[4 + g.par][:, 0:D],
                                               in1=agg_sb[g.par][:, :], scale=1.0, scalar=0.0, op0=ALU.mult,
                                               op1=ALU.add, accum_out=wcol[g.par][:, :]).then_inc(
                    sem("w_dotted"), 1)
                dve.wait_ge(sem("w_dotted"), g.n + 1)
                nc.vector.tensor_scalar(w_all[:, bass.ds(g.n, 1)], wcol[g.par][:, :],
                                        mask_all[:, bass.ds(g.n, 1)], INV, ALU.mult, ALU.mult).then_inc(sem("w_kept"), 1)

            def both(g, ahead=2):
                low_first(g)
                if ahead >= 1:
                    norm_first(g.plus(1))
                if ahead >= 2:
                    stats_first(g.plus(2))
                if not isinstance(g.n, int) or g.n >= 2:
                    dot(g.plus(-2))

            stats_first(Graph(0, 0, 0))
            norm_first(Graph(0, 0, 0))
            stats_first(Graph(1, 0, 1))
            both(Graph(0, 0, 0))
            both(Graph(1, 0, 1))
            pairs_of_graphs(dve, both, 2, B - 2)
            both(Graph(B - 2, B // 2 - 1, 0), ahead=1)
            both(Graph(B - 1, B // 2 - 1, 1), ahead=0)
            dot(Graph(B - 2, B // 2 - 1, 0))
            dot(Graph(B - 1, B // 2 - 1, 1))
            dve.wait_ge(sem("w_turned"), 1)
            nc.vector.tensor_reduce(wmx[:, :], bank[0][0:B, 0:P], AX.X, ALU.max).then_inc(sem("wmx_ready"), 1)
            dve.wait_ge(sem("wmx_ready"), 1)
            nc.vector.tensor_scalar(wneg[:, :], wmx[:, :], -1.0, None, ALU.mult).then_inc(sem("wneg_ready"), 1)
            dve.wait_ge(sem("wexp_ready"), 1)
            nc.vector.reciprocal(wrc[:, :], wsm[:, :]).then_inc(sem("wrc_ready"), 1)
            dve.wait_ge(sem("wrc_ready"), 1)
            nc.vector.tensor_scalar(prow[:, :], wrow[:, :], wrc[:, 0:1], None, ALU.mult).then_inc(
                sem("prow_ready"), 1)
            dve.wait_ge(sem("p_turned"), 1)
            nc.vector.tensor_copy(p_all[:, :], bank[1][:, 0:B]).then_inc(sem("p_ready"), 1)
            phase_end(dve, 2)

            def attend(g):
                dve.wait_ge(sem(f"x_in{g.par}"), 16 * (B // 2) + (g.half + 1) * 16)
                nc.vector.scalar_tensor_tensor(out=x1[g.par][:, :], in0=v_all[:, bass.ds(g.n * D, D)],
                                               scalar=p_all[:, bass.ds(g.n, 1)], in1=xin[g.par][:, :],
                                               op0=ALU.mult, op1=ALU.add).then_inc(sem("x1_ready"), 1)

            def stats_a(g):
                dve.wait_ge(sem("x1_ready"), g.n + 1)
                norm_stats(dve, x1[g.par][:, :], LNA, "c", g.n)

            def norm_a(g):
                wait_from(dve, sem("c_turned"), g.n)
                norm_apply(dve, x1[g.par][:, :], xn[0][:, :], LNA, "c", g.n)

            def low_a(g):
                dve.wait_ge(sem("c_hi"), g.n + 1)
                wait_from(dve, sem("experts_done"), 4 * (g.n - 1))
                nc.vector.tensor_tensor(xT_lo[g.par][:, :], bank[0][:, 0:D], xT_hi[g.par][:, :].bitcast(F32),
                                        ALU.subtract).then_inc(sem("c_split"), 1)

            def low_b(g):
                dve.wait_ge(sem("d_hi"), g.n + 1)
                wait_from(dve, sem("sup0_done"), g.n)
                nc.vector.tensor_tensor(yT_lo[:, :], bank[1][:, 0:D], yT_hi[:, :].bitcast(F32),
                                        ALU.subtract).then_inc(sem("d_split"), 1)

            def gate_start(g):
                dve.wait_ge(sem("gate_done"), g.n + 1)
                nc.vector.tensor_tensor(gl[:, :], bank[2][:, 0:E + 1], gate_bias[:, :], ALU.add).then_inc(
                    sem("gate_step"), 1)
                dve.wait_ge(sem("gate_step"), g.n * 11 + 1)
                nc.vector.tensor_reduce(gmx[:, :], gl[:, 0:E], AX.X, ALU.max).then_inc(sem("gate_step"), 1)
                nc.vector.tensor_scalar(gx[:, E:E + 1], gl[:, E:E + 1], -1.0, None, ALU.mult).then_inc(
                    sem("gx_ready"), 1)
                dve.wait_ge(sem("gate_step"), g.n * 11 + 2)
                nc.vector.tensor_scalar(gx[:, 0:E], gl[:, 0:E], gmx[:, 0:1], None, ALU.subtract).then_inc(
                    sem("gx_ready"), 1)

            def gate_end(g):
                dve.wait_ge(sem("ge_ready"), g.n + 1)
                nc.vector.tensor_reduce(gden[:, 0:1], ge[:, 0:E], AX.X, ALU.add).then_inc(sem("gate_step"), 1)
                nc.vector.tensor_scalar(gden[:, 1:2], ge[:, E:E + 1], 1.0, None, ALU.add).then_inc(
                    sem("gate_step"), 1)
                dve.wait_ge(sem("gate_step"), g.n * 11 + 4)
                nc.vector.reciprocal(grec[:, :], gden[:, :]).then_inc(sem("gate_step"), 1)
                dve.wait_ge(sem("gate_step"), g.n * 11 + 5)
                nc.vector.tensor_scalar(gthr[:, :], grec[:, 1:2], MAX_THRESHOLD, None, ALU.mult).then_inc(
                    sem("gate_step"), 1)
                dve.wait_ge(sem("gate_step"), g.n * 11 + 6)
                nc.vector.tensor_scalar(gad[:, :], ge[:, 0:E], grec[:, 0:1], gthr[:, 0:1], ALU.mult,
                                        ALU.subtract).then_inc(sem("gate_step"), 1)
                dve.wait_ge(sem("gate_step"), g.n * 11 + 7)
                nc.vector.tensor_scalar(gsel[:, :], gad[:, :], 0.0, None, ALU.max).then_inc(sem("gate_step"), 1)
                dve.wait_ge(sem("gate_step"), g.n * 11 + 8)
                nc.vector.tensor_reduce(gsum[:, :], gsel[:, :], AX.X, ALU.add).then_inc(sem("gate_step"), 1)
                dve.wait_ge(sem("gate_step"), g.n * 11 + 9)
                nc.vector.scalar_tensor_tensor(out=gsum1[:, :], in0=gsum[:, :], scalar=0.0, in1=gsum[:, :],
                                               op0=ALU.is_equal, op1=ALU.add).then_inc(sem("gate_step"), 1)
                dve.wait_ge(sem("gate_step"), g.n * 11 + 10)
                nc.vector.reciprocal(gri[:, :], gsum1[:, :]).then_inc(sem("gate_step"), 1)
                dve.wait_ge(sem("gate_step"), g.n * 11 + 11)
                wait_from(dve, sem("combined"), g.n * 9)
                wait_from(dve, sem("gw_turned"), g.n)
                nc.vector.tensor_scalar(gw[:, :], gsel[:, :], gri[:, 0:1], None, ALU.mult).then_inc(
                    sem("gw_ready"), 1)

            def combine(g, c):
                dve.wait_ge(sem("experts_done"), g.n * 4 + (c + 1))
                if c == 0:
                    dve.wait_ge(sem("gw_ready"), g.n + 1)
                    wait_from(dve, sem("x2b_ready"), g.n - 1)
                for h in range(2):
                    e = 2 * c + h
                    at = e if e < 6 else e + 1
                    if at > 0:
                        dve.wait_ge(sem("combined"), g.n * 9 + at)
                    src = x1 if e == 0 else x2
                    nc.vector.scalar_tensor_tensor(
                        out=x2[g.par][:, :], in0=bank[EXPERT_BANK[c]][:, h * D:(h + 1) * D], scalar=gw[:, e:e + 1],
                        in1=src[g.par][:, :], op0=ALU.mult, op1=ALU.add).then_inc(sem("combined"), 1)

            def add_bias(g):
                dve.wait_ge(sem("bexp_done"), g.n + 1)
                dve.wait_ge(sem("combined"), g.n * 9 + 6)
                nc.vector.tensor_tensor(x2[g.par][:, :], bank[2][:, D:2 * D], x2[g.par][:, :],
                                        ALU.add).then_inc(sem("combined"), 1)

            def stats_b(g):
                dve.wait_ge(sem("combined"), g.n * 9 + 9)
                norm_stats(dve, x2[g.par][:, :], LNB, "d", g.n)

            def norm_b(g):
                wait_from(dve, sem("d_turned"), g.n)
                norm_apply(dve, x2[g.par][:, :], xn[1][:, :], LNB, "d", g.n)

            def finish(g):
                dve.wait_ge(sem("x3_summed"), g.n + 1)
                dve.wait_ge(sem("x2b_ready"), g.n + 1)
                wait_from(dve, sem(f"x3_out{g.par}"), g.half * 16)
                nc.vector.tensor_tensor(xo[g.par][:, :], bank[7][:, 0:D], x2b[g.par][:, :], ALU.add).then_inc(
                    sem("x3_ready"), 1)

            def step(g, a=True, nxt=True, b1=True, b2=True):
                one, two, new = g.plus(-1), g.plus(-2), g.plus(1)
                if nxt:
                    attend(new)
                    stats_a(new)
                if a:
                    combine(g, 0)
                if nxt:
                    norm_a(new)
                if b1:
                    low_b(one)
                if a:
                    combine(g, 1)
                if nxt:
                    low_a(new)
                if a:
                    combine(g, 2)
                    add_bias(g)
                if nxt:
                    gate_start(new)
                if a:
                    combine(g, 3)
                    stats_b(g)
                if nxt:
                    gate_end(new)
                if a:
                    norm_b(g)
                if b2:
                    finish(two)

            dve.wait_ge(sem("p_ready"), 1)
            attend(Graph(0, 0, 0))
            stats_a(Graph(0, 0, 0))
            norm_a(Graph(0, 0, 0))
            low_a(Graph(0, 0, 0))
            gate_start(Graph(0, 0, 0))
            gate_end(Graph(0, 0, 0))
            step(Graph(0, 0, 0), b1=False, b2=False)
            step(Graph(1, 0, 1), b2=False)
            pairs_of_graphs(dve, step, 2, B - 2)
            step(Graph(B - 2, B // 2 - 1, 0))
            step(Graph(B - 1, B // 2 - 1, 1), nxt=False)
            step(Graph(B, B // 2, 0), a=False, nxt=False)
            step(Graph(B + 1, B // 2, 1), a=False, nxt=False, b1=False)
            phase_end(dve, 3)

            def norm_rows(j):
                dve.wait_ge(sem("rows_in"), (j + 1) * 16)
                for h in range(HALVES):
                    norm_stats(dve, mx[:, h * D:(h + 1) * D], (LNA, LNB)[h], f"m{h}", j)
                wait_from(dve, sem("m_turned"), j)
                for h in range(HALVES):
                    norm_apply(dve, mx[:, h * D:(h + 1) * D], mxn[:, h * D:(h + 1) * D], (LNA, LNB)[h], f"m{h}", j)

            def prepare(j):
                dve.wait_ge(sem("m_hi"), j + 1)
                nc.vector.tensor_tensor(mT_lo[:, :], bank[0][:, :], mT_hi[:, :].bitcast(F32),
                                        ALU.subtract).then_inc(sem("m_split"), 1)
                for k in range(KD):
                    dve.wait_ge(sem("w1_hi"), j * 2 + (k + 1))
                    last = nc.vector.tensor_tensor(m1l[:, k, :], wraw[:, k * F:(k + 1) * F],
                                                   m1h[:, k, :].bitcast(F32), ALU.subtract)
                last.then_inc(sem("w1_split"), 1)

            def middle(j):
                for q in range(2):
                    dve.wait_ge(sem("w2_hi"), j * 2 + (q + 1))
                    lo = 3 * HW + q * HW // 2
                    last = nc.vector.tensor_tensor(wsplit[:, lo:lo + HW // 2],
                                                   wraw[:, HW + q * HW // 2:HW + (q + 1) * HW // 2],
                                                   wsplit[:, lo - HW:lo - HW // 2].bitcast(F32), ALU.subtract)
                last.then_inc(sem("w2_split"), 1)
                for q in range(KF // 2):
                    dve.wait_ge(sem("gelu"), j * 4 + (q + 1))
                    nc.vector.tensor_copy(h_hi[:, q * 512:(q + 1) * 512], hf[q % 2][:, :]).then_inc(
                        sem("h_hi"), 1)

            norm_rows(0)
            prepare(0)
            norm_rows(1)
            middle(0)
            prepare(1)
            norm_rows(2)
            with dve.Fori(1, TILES - 2) as j:
                middle(j)
                prepare(j + 1)
                norm_rows(j + 2)
            middle(TILES - 2)
            prepare(TILES - 1)
            middle(TILES - 1)
            phase_end(dve, 4)

            def add(g):
                dve.wait_ge(sem(f"fx_in{g.par}"), (g.half + 1) * 16)
                dve.wait_ge(sem(f"fy_in{g.par}"), 16 * TOP * (g.half + 1))
                wait_from(dve, sem("f2"), g.n - 1)
                nc.vector.scalar_tensor_tensor(out=facc[g.par][:, :], in0=fy[g.par][0][:, :],
                                               scalar=rw[:, bass.ds(g.n * TOP, 1)], in1=fx[g.par][:, :],
                                               op0=ALU.mult, op1=ALU.add).then_inc(sem("f1"), 1)
                dve.wait_ge(sem("f1"), g.n + 1)
                wait_from(dve, sem(f"fo_out{g.par}"), g.half * 16)
                nc.vector.scalar_tensor_tensor(out=fo[g.par][:, :], in0=fy[g.par][1][:, :],
                                               scalar=rw[:, bass.ds(g.n * TOP + 1, 1)], in1=facc[g.par][:, :],
                                               op0=ALU.mult, op1=ALU.add).then_inc(sem("f2"), 1)

            dve.wait_ge(sem("route_w_in"), 16)
            for n in range(2):
                add(Graph(n, 0, n))
            pairs_of_graphs(dve, add, 2, TT)

        @block.tensor
        def _(pe):
            pe.wait_ge(sem("onehot"), ME)
            pe.wait_ge(sem("below_set"), 1)
            nc.tensor.matmul(bank[1][:, 0:ME * NG], ones[:, :], onehot[:, :], start=True, stop=True)
            nc.tensor.matmul(bank[1][:, ME * NG:2 * ME * NG], below[:, :], onehot[:, :], start=True,
                             stop=True).then_inc(sem("totals_done"), 1)
            pe.wait_ge(sem("mask_in"), 16)
            pe.wait_ge(sem("ident_set"), 1)
            nc.tensor.transpose(bank[2][:, 0:B], mask_rows[:, :], ident[0:B, 0:B]).then_inc(
                sem("mask_turned"), 1)
            pe.wait_ge(sem("qkv_in"), 32)
            for c in range(2):
                for a in range(KD):
                    for k in range(KD):
                        src = qkv_raw[:, k * 2 * A + c * A + a * P:k * 2 * A + c * A + (a + 1) * P]
                        last = nc.tensor.transpose(bank[3 + c][:, a * D + k * P:a * D + (k + 1) * P], src,
                                                   ident[:, :])
                last.then_inc(sem("qk_turned"), 1)
            pe.wait_ge(sem("qkT_kept"), 2)
            for k in range(KD):
                for a in range(KD):
                    last = nc.tensor.matmul(bank[5][:, k * D:(k + 1) * D],
                                            qkT[:, a * D + k * P:a * D + (k + 1) * P],
                                            qkT[:, KD * D + a * D:KD * D + (a + 1) * D],
                                            start=(a == 0), stop=(a == KD - 1))
            last.then_inc(sem("m_done"), 1)
            phase_end(pe, 1)

            def turn(g):
                pe.wait_ge(sem("a_normed"), g.n + 1)
                wait_from(pe, sem("a_split"), g.n - 1)
                for k in range(KD):
                    nc.tensor.transpose(bank[g.par][:, k * P:(k + 1) * P], xn[g.par][:, k * P:(k + 1) * P],
                                        ident[:, :])
                pe.wait_ge(sem(f"adj_in{g.par}"), (g.half + 1) * 16)
                wait_from(pe, sem("adjTm_ready"), g.n - 1)
                nc.tensor.transpose(bank[2 + g.par][:, 0:P], adjin[g.par][:, :], ident[:, :]).then_inc(
                    sem("a_turned"), 1)

            def products(g):
                pe.wait_ge(sem("a_split"), g.n + 1)
                wait_from(pe, sem("w_dotted"), g.n - 1)
                for k in range(KD):
                    s = slice(k * P, (k + 1) * P)
                    last = split_product(nc.tensor, bank[4 + g.par][:, :],
                                         (xT_hi[g.par][:, s], xT_lo[g.par][:, s]), (mvh[:, k, :], mvl[:, k, :]),
                                         k == 0, k == KD - 1)
                last.then_inc(sem("qv_done"), 1)
                pe.wait_ge(sem("adjTm_ready"), g.n + 1)
                wait_from(pe, sem("agg_kept"), g.n - 1)
                nc.tensor.matmul(bank[6 + g.par][:, 0:D], adjTm[g.par][:, :], xn[g.par][:, :], start=True,
                                 stop=True).then_inc(sem("agg_done"), 1)

            def both(g):
                turn(g)
                products(g.plus(-1))

            turn(Graph(0, 0, 0))
            both(Graph(1, 0, 1))
            pairs_of_graphs(pe, both, 2, B)
            products(Graph(B - 1, B // 2 - 1, 1))
            pe.wait_ge(sem("w_kept"), B)
            nc.tensor.transpose(bank[0][0:B, 0:P], w_all[:, :], ident[:, :]).then_inc(sem("w_turned"), 1)
            pe.wait_ge(sem("prow_ready"), 1)
            nc.tensor.transpose(bank[1][:, 0:B], prow[:, :], ident[0:B, 0:B]).then_inc(sem("p_turned"), 1)
            phase_end(pe, 2)

            def turn_a(g):
                pe.wait_ge(sem("c_normed"), g.n + 1)
                wait_from(pe, sem("c_split"), g.n)
                for k in range(KD):
                    last = nc.tensor.transpose(bank[0][:, k * P:(k + 1) * P], xn[0][:, k * P:(k + 1) * P],
                                               ident[:, :])
                last.then_inc(sem("c_turned"), 1)

            def turn_b(g):
                pe.wait_ge(sem("d_normed"), g.n + 1)
                wait_from(pe, sem("d_split"), g.n)
                for k in range(KD):
                    last = nc.tensor.transpose(bank[1][:, k * P:(k + 1) * P], xn[1][:, k * P:(k + 1) * P],
                                               ident[:, :])
                last.then_inc(sem("d_turned"), 1)

            def gate(g):
                pe.wait_ge(sem("c_split"), g.n + 1)
                wait_from(pe, sem("combined"), g.n * 9 - 2)
                for k in range(KD):
                    s, w = slice(k * P, (k + 1) * P), slice(k * NGATE, (k + 1) * NGATE)
                    last = split_product(nc.tensor, bank[2][:, 0:NGATE],
                                         (xT_hi[g.par][:, s], xT_lo[g.par][:, s]),
                                         (gate_hi[:, w], gate_lo[:, w]), k == 0, k == KD - 1)
                last.then_inc(sem("gate_done"), 1)

            def experts(g, c, k):
                if k == 0:
                    behind = {0: 2 - 9, 1: 9 - 9, 2: 6 - 9, 3: 4}[c]
                    wait_from(pe, sem("combined"), g.n * 9 + behind)
                s = slice(k * P, (k + 1) * P)
                last = split_product(nc.tensor, bank[EXPERT_BANK[c]][:, :], (xT_hi[g.par][:, s], xT_lo[g.par][:, s]),
                                     (exh[:, k, c * 512:(c + 1) * 512], exl[:, k, c * 512:(c + 1) * 512]),
                                     k == 0, k == KD - 1)
                if k == KD - 1:
                    last.then_inc(sem("experts_done"), 1)

            def turn_gw(g):
                pe.wait_ge(sem("gw_ready"), g.n + 1)
                nc.tensor.transpose(bank[2][0:E, P:2 * P], gw[:, :], ident[:, :]).then_inc(sem("gw_turned"), 1)

            def bias(g):
                pe.wait_ge(sem("gwT_kept"), g.n + 1)
                nc.tensor.matmul(bank[2][:, D:2 * D], gwT[:, :], bexp[:, :], start=True, stop=True).then_inc(
                    sem("bexp_done"), 1)

            def support(l, g):
                pe.wait_ge(sem("d_split" if l == 0 else f"hid{l - 1}_split"), g.n + 1)
                if l == 1:
                    wait_from(pe, sem("sup2_kept"), g.n)
                elif l == 0:
                    wait_from(pe, sem("sup1_kept"), g.n)
                else:
                    nxt = g.n + 2
                    pe.wait_ge(sem("sup0_kept"), min(nxt, B) if isinstance(nxt, int) else nxt)
                hi, lo = (yT_hi, yT_lo) if l == 0 else (hid_hi[l - 1], hid_lo[l - 1])
                for k in range(KD):
                    s = slice(k * P, (k + 1) * P)
                    last = split_product(nc.tensor, bank[6][:, 0:D], (hi[:, s], lo[:, s]),
                                         (gnh[:, l, k, :], gnl[:, l, k, :]), k == 0, k == KD - 1)
                last.then_inc(sem(f"sup{l}_done"), 1)

            def aggregate(l, g):
                pe.wait_ge(sem(f"sup{l}_kept"), g.n + 1)
                if l == 1:
                    wait_from(pe, sem("x3_ready"), g.n)
                    wait_from(pe, sem("hid0_ready"), g.n + 1)
                else:
                    pe.wait_ge(sem("adjTs_ready"), g.n + 1)
                    wait_from(pe, sem("hid1_ready"), g.n)
                for c in range(KD):
                    last = nc.tensor.matmul(bank[7][:, c * P:(c + 1) * P], sup[l][:, c * P:(c + 1) * P],
                                            adjTs[g.par][:, :], start=True, stop=True)
                last.then_inc(sem(f"agg{l}_done"), 1)

            def last_sum(g):
                pe.wait_ge(sem("sup2_kept"), g.n + 1)
                after = g.n + 2
                pe.wait_ge(sem("hid0_ready"), after if not isinstance(after, int) else min(after, B))
                nc.tensor.matmul(bank[7][:, 0:D], adjTs[g.par][:, :], sup[2][:, :], start=True,
                                 stop=True).then_inc(sem("x3_summed"), 1)

            def step(g, a=True, nxt=True, b1=True, b2=True):
                one, two, new = g.plus(-1), g.plus(-2), g.plus(1)
                if a:
                    experts(g, 0, 0)
                    experts(g, 0, 1)
                if b2:
                    support(1, two)
                if a:
                    experts(g, 1, 0)
                if b1:
                    turn_b(one)
                if b2:
                    aggregate(1, two)
                if a:
                    experts(g, 1, 1)
                    turn_gw(g)
                if b1:
                    support(0, one)
                if nxt:
                    turn_a(new)
                if a:
                    experts(g, 2, 0)
                    bias(g)
                if b1:
                    aggregate(0, one)
                if a:
                    experts(g, 2, 1)
                if b2:
                    support(2, two)
                if a:
                    experts(g, 3, 0)
                if nxt:
                    gate(new)
                if a:
                    experts(g, 3, 1)
                if b2:
                    last_sum(two)

            turn_a(Graph(0, 0, 0))
            gate(Graph(0, 0, 0))
            step(Graph(0, 0, 0), b1=False, b2=False)
            step(Graph(1, 0, 1), b2=False)
            pairs_of_graphs(pe, step, 2, B - 2)
            step(Graph(B - 2, B // 2 - 1, 0))
            step(Graph(B - 1, B // 2 - 1, 1), nxt=False)
            step(Graph(B, B // 2, 0), a=False, nxt=False)
            step(Graph(B + 1, B // 2, 1), a=False, nxt=False, b1=False)
            phase_end(pe, 3)

            def turn_tile(j):
                for h in range(HALVES):
                    pe.wait_ge(sem(f"m{h}_normed"), j + 1)
                wait_from(pe, sem("m_split"), j)
                for k in range(KD):
                    for h in range(HALVES):
                        last = nc.tensor.transpose(bank[0][:, k * SLOTS + h * P:k * SLOTS + (h + 1) * P],
                                                   mxn[:, h * D + k * P:h * D + (k + 1) * P], ident[:, :])
                last.then_inc(sem("m_turned"), 1)

            def layer1(j):
                pe.wait_ge(sem("m_split"), j + 1)
                pe.wait_ge(sem("w1_split"), j + 1)
                for q in range(KF // 2):
                    wait_from(pe, sem("gelu"), (j - 1) * 4 + (q + 1))
                    for m in (2 * q, 2 * q + 1):
                        for k in range(KD):
                            f, s = slice(m * P, (m + 1) * P), slice(k * SLOTS, (k + 1) * SLOTS)
                            last = split_product(nc.tensor, bank[2 + q][:, (m % 2) * SLOTS:(m % 2 + 1) * SLOTS],
                                                 (m1h[:, k, f], m1l[:, k, f]), (mT_hi[:, s], mT_lo[:, s]),
                                                 k == 0, k == KD - 1)
                    last.then_inc(sem("layer1_done"), 1)

            def layer2(j):
                pe.wait_ge(sem("w2_split"), j + 1)
                wait_from(pe, sem("y_ready"), j)
                for h in range(HALVES):
                    for m in range(KF):
                        if h == 0 and m % 2 == 0:
                            pe.wait_ge(sem("h_split"), j * 4 + (m // 2 + 1))
                        s = slice(m * SLOTS + h * P, m * SLOTS + (h + 1) * P)
                        last = split_product(nc.tensor, bank[1][:, h * D:(h + 1) * D], (h_hi[:, s], h_lo[:, s]),
                                             (m2h[:, m, :], m2l[:, m, :]), m == 0, m == KF - 1)
                last.then_inc(sem("layer2_done"), 1)

            turn_tile(0)
            layer1(0)
            with pe.Fori(1, TILES) as j:
                turn_tile(j)
                layer2(j - 1)
                layer1(j)
            layer2(TILES - 1)
            phase_end(pe, 4)


_INS = ['x', 'adj', 'nodemask', 'L0_gnn_Wqk', 'L0_gnn_Wv', 'L0_ffn_W_gate', 'L0_ffn_b_gate', 'L0_ffn_W_thr',
        'L0_ffn_b_thr', 'L0_ffn_W_exp', 'L0_ffn_b_exp', 'L1_gnn_W1', 'L1_gnn_b1', 'L1_gnn_W2', 'L1_gnn_b2',
        'L1_gnn_W3', 'L1_gnn_b3', 'L1_ffn_expert_weights', 'L1_ffn_expert_indices', 'L1_ffn_w1', 'L1_ffn_w2']
_OUT = ((64, 128, 256), 'float32')


def kernel(**inputs):
    import numpy as _np
    import concourse.bacc as _bacc
    from concourse import mybir as _mybir
    from concourse.bass_utils import run_bass_kernel_spmd as _run

    nc = _bacc.Bacc("TRN2", target_bir_lowering=False, num_devices=1)
    arrays, args = {}, []
    for name in _INS:
        a = _np.ascontiguousarray(inputs[name])
        arrays[f"in_{name}_dram"] = a
        args.append(nc.dram_tensor(f"in_{name}_dram", a.shape, _mybir.dt.from_np(a.dtype), kind="ExternalInput").ap())
    shape, dtype = _OUT
    args.append(nc.dram_tensor("out_dram", shape, _mybir.dt.from_np(_np.dtype(dtype)), kind="ExternalOutput").ap())
    build(nc, *args)
    r = _run(nc, [arrays], core_ids=[0])
    return r.results[0]["out_dram"]
```

```python
from contextlib import ExitStack

import concourse.bass as bass
from concourse import mybir

ALU = mybir.AluOpType
ACT = mybir.ActivationFunctionType
AX = mybir.AxisListType
F32 = mybir.dt.float32
F32R = mybir.dt.float32r
I32 = mybir.dt.int32

P = 128
EPS = 1e-5
MAX_THRESHOLD = 0.25
ENGINES = 5
TINY = 1e-38
EXPERT_BANK = (3, 4, 5, 4)


class Graph:

    def __init__(self, n, half, par):
        self.n, self.half, self.par = n, half, par

    def plus(self, k):
        total = self.par + k
        return Graph(self.n + k, self.half + total // 2, total % 2)


def wait_from(eng, sem, value):
    if not (isinstance(value, int) and value <= 0):
        eng.wait_ge(sem, value)


def pairs_of_graphs(eng, body, first, last):
    with eng.Fori(first // 2, last // 2) as half:
        for par in range(2):
            body(Graph(half * 2 + par, half, par))


def split_product(pe, out, lhs, rhs, first, last):
    (lhs_hi, lhs_lo), (rhs_hi, rhs_lo) = lhs, rhs
    pe.matmul(out, lhs_lo, rhs_hi, start=first, stop=False)
    pe.matmul(out, lhs_hi, rhs_lo, start=False, stop=False)
    return pe.matmul(out, lhs_hi, rhs_hi, start=False, stop=last)


def build(nc, x, adj, nodemask, Wqk, Wv, W_gate, b_gate, W_thr, b_thr, W_exp, b_exp,
          W1, b1, W2, b2, W3, b3, moe_weights, moe_indices, moe_w1, moe_w2, out):
    B, N, D = x.shape
    A = Wqk.shape[1] // 2
    E = W_gate.shape[1]
    ME, _, F = moe_w1.shape
    T, TOP = moe_indices.shape
    KD = D // P
    KF = F // P
    TT = T // P
    SLOTS = 256
    HALVES = SLOTS // P
    TILES = (T * TOP + ME * (SLOTS - 1)) // SLOTS
    NG = TT * TOP
    MAXT = T * TOP // SLOTS
    INV = 1.0 / float(A) ** 0.5
    assert N == P and D == A == 2 * P and E == ME == 8

    xg = nc.dram_tensor("routed_x", [TILES * SLOTS, D], F32)
    yg = nc.dram_tensor("routed_y", [TILES * SLOTS, D], F32)

    ctx = ExitStack()
    with ctx:
        def sb(name, shape, dt=F32, stack=ctx):
            return stack.enter_context(nc.sbuf_tensor(name, shape, dt))

        sems = {}

        def sem(name):
            if name not in sems:
                sems[name] = ctx.enter_context(nc.semaphore(name))
            return sems[name]

        bank = [ctx.enter_context(nc.psum_tensor(f"bank{i}", [P, 512], F32)) for i in range(8)]

        ident = sb("ident", [P, P])
        ones = sb("ones", [P, P])
        below = sb("below", [P, P])
        zeros = sb("zeros", [P, D])
        wraw = sb("wraw", [P, 2 * KD * F])
        wsplit = sb("wsplit", [P, 4 * KD * F], F32R)
        gnn_hi = sb("gnn_hi", [P, 3 * KD * D], F32R)
        gnn_lo = sb("gnn_lo", [P, 3 * KD * D], F32R)
        NGATE = E + 2
        gate_raw = sb("gate_raw", [P, KD * NGATE])
        gate_hi = sb("gate_hi", [P, KD * NGATE], F32R)
        gate_lo = sb("gate_lo", [P, KD * NGATE], F32R)
        gate_bias = sb("gate_bias", [P, E + 1])
        bexp = sb("bexp", [E, D])
        b12 = sb("b12", [P, 2 * KD])
        b3_all = sb("b3_all", [P, D])
        mask_rows = sb("mask_rows", [B, P])
        mask_all = sb("mask_all", [P, B])
        w_all = sb("w_all", [P, B])
        p_all = sb("p_all", [P, B])

        ri_i = sb("ri_i", [P, NG], I32)
        rw = sb("rw", [P, NG])
        ri_f = sb("ri_f", [P, NG])
        ends = [sb(f"ends{i}", [P, ME]) for i in range(2)]
        counts = sb("counts", [P, ME])
        ntiles = sb("ntiles", [P, ME])
        base = sb("base", [P, ME])
        steps_i = sb("steps_i", [P, MAXT], I32)
        steps_f = sb("steps_f", [P, MAXT])
        tiles_i = sb("tiles_i", [P, TILES], I32)
        tiles_f = sb("tiles_f", [P, TILES])
        slot_f = sb("slot_f", [P, NG])
        slot_i = sb("slot_i", [P, NG], I32)
        texp_f = sb("texp_f", [P, TILES])
        texp_i = sb("texp_i", [P, TILES], I32)

        phase1 = ExitStack()
        adjin = [sb(f"adjin{i}", [P, P], F32, phase1) for i in range(2)]
        adjTm = [sb(f"adjTm{i}", [P, P], F32, phase1) for i in range(2)]
        agg_sb = [sb(f"agg_sb{i}", [P, D], F32, phase1) for i in range(2)]
        mv_hi = sb("mv_hi", [P, KD * 2 * D], F32R, phase1)
        mv_lo = sb("mv_lo", [P, KD * 2 * D], F32R, phase1)
        phase1.close()
        x1 = [sb(f"x1_{i}", [P, D]) for i in range(2)]
        x2 = [sb(f"x2_{i}", [P, D]) for i in range(2)]
        x2b = [sb(f"x2b_{i}", [P, D]) for i in range(2)]
        xo = [sb(f"xo{i}", [P, D]) for i in range(2)]
        pv = sb("pv", [P, D])
        odd = sb("odd", [P, D])
        even = sb("even", [P, D])
        bias_sb = sb("bias_sb", [P, D])
        xin = [sb(f"xin{i}", [P, D]) for i in range(2)]
        stats = sb("stats", [P, 6])
        mv = sb("mv", [P, 2])
        veps = sb("veps", [P, 1])
        rstd = sb("rstd", [P, 1])
        statsb = sb("statsb", [P, 6])
        mvb = sb("mvb", [P, 2])
        vepsb = sb("vepsb", [P, 1])
        rstdb = sb("rstdb", [P, 1])
        minus_half = sb("minus_half", [P, 1])
        xn = [sb(f"xn{i}", [P, D]) for i in range(2)]
        wcol = [sb(f"wcol{i}", [P, 1]) for i in range(2)]
        xT_hi = [sb(f"xT_hi{i}", [P, D], F32R) for i in range(2)]
        xT_lo = [sb(f"xT_lo{i}", [P, D], F32R) for i in range(2)]
        yT_hi = sb("yT_hi", [P, D], F32R)
        yT_lo = sb("yT_lo", [P, D], F32R)
        gneg = sb("gneg", [P, E + 1])
        gmin = sb("gmin", [P, 1])
        ge = sb("ge", [P, E])
        gesum = sb("gesum", [P, 1])
        gtanh = sb("gtanh", [P, 1])
        gthr = sb("gthr", [P, 1])
        gad = sb("gad", [P, E])
        gsel = sb("gsel", [P, E])
        gsum = sb("gsum", [P, 1])
        gri = sb("gri", [P, 1])
        gw = [sb(f"gw{i}", [P, E]) for i in range(2)]
        gwT = sb("gwT", [E, P])
        adjTs = [sb(f"adjTs{i}", [P, P]) for i in range(2)]
        sup = [sb(f"sup{i}", [P, D]) for i in range(3)]
        hid = [sb(f"hid{i}", [P, D]) for i in range(2)]
        hid_hi = [sb(f"hid_hi{i}", [P, D], F32R) for i in range(2)]
        hid_lo = [sb(f"hid_lo{i}", [P, D], F32R) for i in range(2)]
        sx = sb("sx", [P, D])
        sidx = sb("sidx", [P, TOP], I32)
        wmx = sb("wmx", [B, 1])
        wneg = sb("wneg", [B, 1])
        wrow = sb("wrow", [B, P])
        wsm = sb("wsm", [B, 1])
        wrc = sb("wrc", [B, 1])
        prow = sb("prow", [B, P])

        early = ExitStack()
        v_all = sb("v_all", [P, B * D], F32, early)
        adjT_all = sb("adjT_all", [P, B * P], F32, early)
        early.close()
        late = ExitStack()
        mx = sb("mx", [P, HALVES * D], F32, late)
        mxn = sb("mxn", [P, HALVES * D], F32, late)
        mT_hi = sb("mT_hi", [P, KD * SLOTS], F32R, late)
        mT_lo = sb("mT_lo", [P, KD * SLOTS], F32R, late)
        hf = [sb(f"hf{i}", [P, 512], F32, late) for i in range(KF // 2)]
        h_hi = [sb(f"h_hi{i}", [P, KF * SLOTS], F32R, late) for i in range(2)]
        h_lo = [sb(f"h_lo{i}", [P, KF * SLOTS], F32R, late) for i in range(2)]
        my = sb("my", [P, HALVES * D], F32, late)
        fx = [sb(f"fx{i}", [P, D], F32, late) for i in range(2)]
        fy = [[sb(f"fy{i}_{k}", [P, D], F32, late) for k in range(TOP)] for i in range(2)]
        facc = [sb(f"facc{i}", [P, D], F32, late) for i in range(2)]
        fo = [sb(f"fo{i}", [P, D], F32, late) for i in range(2)]
        late.close()
        setup = ExitStack()
        qkv_raw = sb("qkv_raw", [P, KD * (2 * A + D)], F32, setup)
        qkT = sb("qkT", [P, 2 * KD * D], F32, setup)
        gnn_raw = sb("gnn_raw", [P, 3 * KD * D], F32, setup)
        mv_f = sb("mv_f", [P, KD * 2 * D], F32, setup)
        onehot = sb("onehot", [P, ME * NG], F32, setup)
        scan = [sb(f"scan{i}", [P, ME * NG], F32, setup) for i in range(2)]
        ranks = sb("ranks", [P, ME * NG], F32, setup)
        cmp_n = sb("cmp_n", [P, ME * MAXT], F32, setup)
        cmp_t = sb("cmp_t", [P, TILES * ME], F32, setup)
        setup.close()

        mvh, mvl = (t[:, :].rearrange("p (k n) -> p k n", k=KD) for t in (mv_hi, mv_lo))
        gnh, gnl = (t[:, :].rearrange("p (l k n) -> p l k n", l=3, k=KD) for t in (gnn_hi, gnn_lo))
        HW = KD * F
        exh, exl = (wsplit[:, i * 2 * HW:(i + 1) * 2 * HW].rearrange("p (k n) -> p k n", k=KD) for i in range(2))
        m1h, m1l = (wsplit[:, i * HW:(i + 1) * HW].rearrange("p (k n) -> p k n", k=KD) for i in range(2))
        m2h, m2l = (wsplit[:, (2 + i) * HW:(3 + i) * HW].rearrange("p (k n) -> p k n", k=KF) for i in range(2))
        oh3 = onehot[:, :].rearrange("p (e g) -> p e g", e=ME)
        sc3 = [s[:, :].rearrange("p (e g) -> p e g", e=ME) for s in scan]
        rk3 = ranks[:, :].rearrange("p (e g) -> p e g", e=ME)

        block = ctx.enter_context(nc.Block())

        def phase_end(eng, k):
            eng.drain().then_inc(sem("phase_done"), 1)
            eng.wait_ge(sem("phase_done"), ENGINES * k)

        def steps_of_tiles(eng, step):
            last_pair = (TILES - 2) // 2 * 2
            step(Graph(1, 0, 1))
            pairs_of_graphs(eng, step, 2, last_pair)
            for n in range(last_pair, TILES):
                step(Graph(n, n // 2, n % 2))

        def has_next(g, ahead):
            return not isinstance(g.n, int) or g.n + ahead < TILES

        def own_wait(eng, *waits):
            for s, v in waits:
                wait_from(eng, s, v)
            eng.sem_inc(sem("passed"), 1)

        def norm_stats(dve, src, bufs, name, n):
            st, mean_var, _, _ = bufs
            step = sem(name + "_step")
            nc.vector.bn_stats(st[:, :], src).then_inc(step, 1)
            own_wait(dve, (step, n * 2 + 1))
            nc.vector.bn_aggr(mean_var[:, :], st[:, :]).then_inc(step, 1)

        def norm_rstd(pool, bufs, name, n):
            _, mean_var, veps, rs = bufs
            own_wait(pool, (sem(name + "_step"), n * 2 + 2))
            nc.gpsimd.tensor_scalar(veps[:, :], mean_var[:, 1:2], EPS, None, ALU.add).then_inc(
                sem(name + "_veps"), 1)
            pool.wait_ge(sem(name + "_veps"), n + 1)
            nc.gpsimd.tensor_tensor(rs[:, :], veps[:, :], minus_half[:, :], ALU.pow).then_inc(
                sem(name + "_rstd"), 1)

        def norm_apply(dve, src, dst, bufs, name, n):
            _, mean_var, _, rs = bufs
            dve.wait_ge(sem(name + "_rstd"), n + 1)
            nc.vector.tensor_scalar(dst, src, mean_var[:, 0:1], rs[:, 0:1], ALU.subtract, ALU.mult).then_inc(
                sem(name + "_normed"), 1)

        LNA, LNB = (stats, mv, veps, rstd), (statsb, mvb, vepsb, rstdb)

        @block.sync
        def _(sp):
            sp.dma_start(qkv_raw[:, 0:KD * 2 * A].rearrange("p (k n) -> p k n", k=KD),
                         Wqk.rearrange("(k p) n -> p k n", p=P)).then_inc(sem("qkv_in"), 16)
            sp.dma_start(qkv_raw[:, KD * 2 * A:].rearrange("p (k n) -> p k n", k=KD),
                         Wv.rearrange("(k p) n -> p k n", p=P)).then_inc(sem("qkv_in"), 16)
            sp.dma_start(mask_rows[:, :], nodemask).then_inc(sem("mask_in"), 16)
            sp.dma_start(ri_i[:, :].rearrange("p (c k) -> p c k", k=TOP),
                         moe_indices.rearrange("(c p) k -> p c k", p=P)).then_inc(sem("route_in"), 16)
            sp.dma_start(rw[:, :].rearrange("p (c k) -> p c k", k=TOP),
                         moe_weights.rearrange("(c p) k -> p c k", p=P)).then_inc(sem("route_w_in"), 16)
            for l, w in enumerate((W1, W2, W3)):
                sp.dma_start(gnn_raw[:, l * KD * D:(l + 1) * KD * D].rearrange("p (k n) -> p k n", k=KD),
                             w.rearrange("(k p) n -> p k n", p=P)).then_inc(sem("gnn_in"), 16)
            sp.wait_ge(sem("gate_zeroed"), 1)
            gr = gate_raw[:, :].rearrange("p (k n) -> p k n", k=KD)
            sp.dma_start(gr[:, :, 0:E], W_gate.rearrange("(k p) n -> p k n", p=P)).then_inc(sem("gate_in"), 16)
            sp.dma_start(gr[:, :, E:E + 1], W_thr.rearrange("(k p) n -> p k n", p=P), allow_slow_non_contiguous=True).then_inc(sem("gate_in"), 16)
            sp.dma_start(gate_bias[:, 0:E], b_gate.partition_broadcast(P)).then_inc(sem("gate_in"), 16)
            sp.dma_start(gate_bias[:, E:E + 1], b_thr.partition_broadcast(P)).then_inc(sem("gate_in"), 16)
            sp.dma_start(bexp[:, :], b_exp).then_inc(sem("bias_in"), 16)
            sp.dma_start(b3_all[:, :], b3.partition_broadcast(P)).then_inc(sem("bias_in"), 16)
            for l, b in enumerate((b1, b2)):
                sp.dma_start(b12[:, l * KD:(l + 1) * KD], b.rearrange("(k p) -> p k", p=P), allow_slow_non_contiguous=True).then_inc(
                    sem("bias_in"), 16)
            wv = wraw[:, :].rearrange("p (k e n) -> p k e n", k=KD, e=E)
            for e in range(E):
                sp.dma_start(wv[:, :, e, :], W_exp[e].rearrange("(k p) n -> p k n", p=P)).then_inc(
                    sem("experts_in"), 16)
            sp.wait_ge(sem("zeroed"), 1)
            for i in range(TILES * HALVES):
                sp.dma_start(xg[i * P:(i + 1) * P, :], zeros[:, :]).then_inc(sem("slots_zeroed"), 16)
            phase_end(sp, 1)

            def load1(g):
                wait_from(sp, sem("a_normed"), g.n - 1)
                sp.dma_start(xin[g.par][:, :], x[bass.ds(g.n, 1)].rearrange("o p d -> (o p) d")).then_inc(
                    sem(f"x_in{g.par}"), 16)
                wait_from(sp, sem("a_turned"), g.n - 1)
                sp.dma_start(adjin[g.par][:, :], adj[bass.ds(g.n, 1)].rearrange("o p d -> (o p) d")).then_inc(
                    sem(f"adj_in{g.par}"), 16)

            for n in range(2):
                load1(Graph(n, 0, n))
            pairs_of_graphs(sp, load1, 2, B)
            phase_end(sp, 2)

            def load2(g):
                wait_from(sp, sem("x1_ready"), g.n - 1)
                sp.dma_start(xin[g.par][:, :], x[bass.ds(g.n, 1)].rearrange("o p d -> (o p) d")).then_inc(
                    sem(f"x_in{g.par}"), 16)

            def store(g):
                sp.wait_ge(sem("x3_ready"), g.n + 1)
                sp.dma_start(out[bass.ds(g.n, 1)].rearrange("o p d -> (o p) d"), xo[g.par][:, :]).then_inc(
                    sem(f"x3_out{g.par}"), 16)

            def step(g):
                load2(g.plus(2))
                store(g.plus(-2))

            for n in range(4):
                load2(Graph(n, n // 2, n % 2))
            pairs_of_graphs(sp, step, 2, B - 2)
            for n in range(B - 2, B + 2):
                store(Graph(n - 2, n // 2 - 1, n % 2))
            for par in range(2):
                sp.wait_ge(sem(f"x3_out{par}"), 16 * (B // 2))
            phase_end(sp, 3)

            def load_rows(j):
                for h in range(HALVES):
                    wait_from(sp, sem(f"m{h}_normed"), j)
                sp.dma_start(mx[:, :].rearrange("p (h d) -> p h d", h=HALVES),
                             xg[bass.ds(j * SLOTS, SLOTS), :].rearrange("(h p) d -> p h d", p=P)).then_inc(
                    sem("rows_in"), 16)

            def load_w1(j):
                e = sp.value_load(texp_i[0:1, bass.ds(j, 1)], min_val=0, max_val=ME - 1)
                wait_from(sp, sem("w1_split"), j)
                sp.dma_start(wraw[:, 0:HW].rearrange("p (k n) -> p k n", k=KD),
                             moe_w1[bass.ds(e, 1)].rearrange("o (k p) n -> p (o k) n", p=P)).then_inc(
                    sem("w1_in"), 16)

            def load_w2(j):
                e = sp.value_load(texp_i[0:1, bass.ds(j, 1)], min_val=0, max_val=ME - 1)
                wait_from(sp, sem("w2_split"), j)
                sp.dma_start(wraw[:, HW:2 * HW].rearrange("p (k n) -> p k n", k=KF),
                             moe_w2[bass.ds(e, 1)].rearrange("o (k p) n -> p (o k) n", p=P)).then_inc(
                    sem("w2_in"), 16)

            def store_tile(j):
                sp.wait_ge(sem("y_ready"), j + 1)
                sp.dma_start(yg[bass.ds(j * SLOTS, SLOTS), :].rearrange("(h p) d -> p h d", p=P),
                             my[:, :].rearrange("p (h d) -> p h d", h=HALVES)).then_inc(sem("y_out"), 16)

            def tile_step(g):
                if has_next(g, 1):
                    load_w1(g.n + 1)
                if has_next(g, 2):
                    load_rows(g.n + 2)
                load_w2(g.n)
                if not (isinstance(g.n, int) and g.n == 1):
                    store_tile(g.n - 2)

            load_rows(0)
            load_w1(0)
            load_w2(0)
            load_rows(1)
            load_w1(1)
            load_rows(2)
            steps_of_tiles(sp, tile_step)
            store_tile(TILES - 2)
            store_tile(TILES - 1)
            sp.wait_ge(sem("y_out"), 16 * TILES)
            phase_end(sp, 4)

            def load3(g):
                wait_from(sp, sem("f1"), g.n - 1)
                sp.dma_start(fx[g.par][:, :], out[bass.ds(g.n, 1)].rearrange("o p d -> (o p) d")).then_inc(
                    sem(f"fx_in{g.par}"), 16)

            def store3(g):
                sp.wait_ge(sem("f2"), g.n + 1)
                sp.dma_start(out[bass.ds(g.n, 1)].rearrange("o p d -> (o p) d"), fo[g.par][:, :]).then_inc(
                    sem(f"fo_out{g.par}"), 16)

            def step3(g):
                load3(g)
                store3(g.plus(-2))

            for n in range(2):
                load3(Graph(n, 0, n))
            pairs_of_graphs(sp, step3, 2, TT)
            for n in range(TT, TT + 2):
                store3(Graph(n - 2, n // 2 - 1, n % 2))
            for par in range(2):
                sp.wait_ge(sem(f"fo_out{par}"), 16 * (TT // 2))

        @block.gpsimd
        def _(pool):
            nc.gpsimd.memset(gate_raw[:, :], 0.0).then_inc(sem("gate_zeroed"), 1)
            nc.gpsimd.memset(minus_half[:, :], -0.5).then_inc(sem("minus_half_set"), 1)
            nc.gpsimd.memset(zeros[:, :], 0.0).then_inc(sem("zeroed"), 1)
            nc.gpsimd.memset(ones[:, :], 1.0).then_inc(sem("ones_set"), 1)
            nc.gpsimd.memset(ident[:, :], 0.0).then_inc(sem("ident_zeroed"), 1)
            pool.wait_ge(sem("ident_zeroed"), 1)
            nc.gpsimd.affine_select(out=ident[:, :], in_=ident[:, :], compare_op=ALU.not_equal, fill=1.0,
                                    base=0, pattern=[[-1, P]], channel_multiplier=1).then_inc(sem("ident_set"), 1)
            pool.wait_ge(sem("ones_set"), 1)
            nc.gpsimd.affine_select(out=below[:, :], in_=ones[:, :], compare_op=ALU.is_gt, fill=0.0,
                                    base=0, pattern=[[1, P]], channel_multiplier=-1).then_inc(sem("below_set"), 1)
            nc.gpsimd.iota(steps_i[:, :], pattern=[[SLOTS, MAXT]], base=0, channel_multiplier=0).then_inc(
                sem("iotas_set"), 1)
            nc.gpsimd.iota(tiles_i[:, :], pattern=[[1, TILES]], base=0, channel_multiplier=0).then_inc(
                sem("iotas_set"), 1)
            phase_end(pool, 1)
            pool.wait_ge(sem("minus_half_set"), 1)
            norm_rstd(pool, LNA, "a", 0)
            with pool.Fori(1, B) as n:
                norm_rstd(pool, LNA, "a", n)
            phase_end(pool, 2)

            def split_hidden(l, g):
                pool.wait_ge(sem(f"hid{l}_ready"), g.n + 1)
                wait_from(pool, sem(f"sup{l + 1}_done"), g.n)
                nc.gpsimd.tensor_tensor(hid_lo[l][:, :], hid[l][:, :], hid_hi[l][:, :].bitcast(F32),
                                        ALU.subtract).then_inc(sem(f"hid{l}_split"), 1)

            def attend(g):
                pool.wait_ge(sem("pv_ready"), g.n + 1)
                pool.wait_ge(sem(f"x_in{g.par}"), (g.half + 1) * 16 + 16 * (B // 2))
                wait_from(pool, sem("combined"), (g.n - 2) * 9 + 1)
                nc.gpsimd.tensor_tensor(x1[g.par][:, :], pv[:, :], xin[g.par][:, :], ALU.add).then_inc(
                    sem("x1_ready"), 1)

            def add_b3(g):
                pool.wait_ge(sem("combined"), g.n * 9 + 9)
                wait_from(pool, sem("x3_ready"), g.n - 1)
                nc.gpsimd.tensor_tensor(x2b[g.par][:, :], x2[g.par][:, :], b3_all[:, :], ALU.add).then_inc(
                    sem("x2b_ready"), 1)

            def step(g, a=True, nxt=True, nx2=True, b1=True, b2=True, routed=None):
                if nxt:
                    norm_rstd(pool, LNA, "c", g.n + 1)
                if b1:
                    add_b3(g.plus(-1))
                if nx2:
                    attend(g.plus(2))
                if b2:
                    split_hidden(1, g.plus(-2))
                if routed is not None:
                    (scatter if g.par else route)(routed)
                if b1:
                    split_hidden(0, g.plus(-1))
                if a:
                    norm_rstd(pool, LNB, "d", g.n)

            def route(c):
                own_wait(pool, (sem("scattered"), c * (16 * TOP)))
                pool.dma_start(sx[:, :], out[bass.ds(c, 1)].rearrange("o p d -> (o p) d")).then_inc(
                    sem("sx_in"), 16)
                nc.gpsimd.tensor_copy(sidx[:, :], slot_i[:, bass.ds(c * TOP, TOP)]).then_inc(sem("sidx_ready"), 1)

            def scatter(c):
                own_wait(pool, (sem("sx_in"), (c + 1) * 16), (sem("sidx_ready"), c + 1))
                for k in range(TOP):
                    nc.gpsimd.indirect_dma_start(
                        out=xg[:, :], out_offset=bass.IndirectOffsetOnAxis(ap=sidx[:, k:k + 1], axis=0),
                        in_=sx[:, :], in_offset=None).then_inc(sem("scattered"), 16)

            LEAD = TT + 4
            attend(Graph(0, 0, 0))
            norm_rstd(pool, LNA, "c", 0)
            attend(Graph(1, 0, 1))
            step(Graph(0, 0, 0), b1=False, b2=False)
            step(Graph(1, 0, 1), b2=False)
            pairs_of_graphs(pool, step, 2, LEAD)
            for par in range(2):
                pool.wait_ge(sem(f"x3_out{par}"), 16 * (TT // 2))
            pool.wait_ge(sem("slots_zeroed"), 16 * TILES * HALVES)

            def routed_pair(half):
                g = Graph(half * 2, half, 0)
                step(g, routed=half - LEAD // 2)
                step(g.plus(1), routed=half - LEAD // 2)

            routed_pair(LEAD // 2)
            with pool.Fori(LEAD // 2 + 1, LEAD // 2 + TT) as half:
                routed_pair(half)
            pairs_of_graphs(pool, step, LEAD + 2 * TT, B - 2)
            step(Graph(B - 2, B // 2 - 1, 0), nx2=False)
            step(Graph(B - 1, B // 2 - 1, 1), nxt=False, nx2=False)
            step(Graph(B, B // 2, 0), a=False, nxt=False, nx2=False)
            step(Graph(B + 1, B // 2, 1), a=False, nxt=False, nx2=False, b1=False)
            pool.wait_ge(sem("scattered"), 16 * TOP * TT)
            phase_end(pool, 3)

            def rstd_rows(j):
                for h in range(HALVES):
                    norm_rstd(pool, (LNA, LNB)[h], f"m{h}", j)

            def split_h(g):
                wait_from(pool, sem("layer2_done"), g.n - 1)
                for q in range(KF // 2):
                    pool.wait_ge(sem("h_hi"), g.n * (KF // 2) + (q + 1))
                    nc.gpsimd.tensor_tensor(h_lo[g.par][:, q * 512:(q + 1) * 512], hf[q][:, :],
                                            h_hi[g.par][:, q * 512:(q + 1) * 512].bitcast(F32),
                                            ALU.subtract).then_inc(sem("h_split"), 1)

            def tile_step(g):
                split_h(g)
                if has_next(g, 2):
                    rstd_rows(g.n + 2)

            rstd_rows(0)
            rstd_rows(1)
            split_h(Graph(0, 0, 0))
            rstd_rows(2)
            steps_of_tiles(pool, tile_step)
            phase_end(pool, 4)

            def gather(g):
                own_wait(pool, (sem("f2"), g.n - 1))
                nc.gpsimd.tensor_copy(sidx[:, :], slot_i[:, bass.ds(g.n * TOP, TOP)]).then_inc(
                    sem("gidx_ready"), 1)
                own_wait(pool, (sem("gidx_ready"), g.n + 1))
                for k in range(TOP):
                    nc.gpsimd.indirect_dma_start(
                        out=fy[g.par][k][:, :], out_offset=None, in_=yg[:, :],
                        in_offset=bass.IndirectOffsetOnAxis(ap=sidx[:, k:k + 1], axis=0)).then_inc(
                        sem(f"fy_in{g.par}"), 16)
                own_wait(pool, (sem(f"fy_in{g.par}"), (g.half + 1) * (16 * TOP)))

            for n in range(2):
                gather(Graph(n, 0, n))
            pairs_of_graphs(pool, gather, 2, TT)

        @block.scalar
        def _(act):
            def copy_const(dst, src, name):
                return nc.scalar.copy(dst, src).then_inc(sem(name), 1)

            act.wait_ge(sem("experts_in"), 16 * E)
            for i in range(2):
                copy_const(exh[:, i, :], wraw[:, i * 2 * P * 8:(i + 1) * 2 * P * 8], "experts_hi")
            act.wait_ge(sem("gnn_in"), 48)
            copy_const(gnn_hi[:, :], gnn_raw[:, :], "gnn_hi")
            act.wait_ge(sem("gate_in"), 64)
            copy_const(gate_hi[:, :], gate_raw[:, :], "gate_hi")
            act.wait_ge(sem("mv_ready"), KD + 1)
            copy_const(mv_hi[:, :], mv_f[:, :], "mv_hi")
            phase_end(act, 1)
            act.wait_ge(sem("mask_ready"), 1)

            def first(g):
                act.wait_ge(sem("a_turned"), g.n + 1)
                wait_from(act, sem("qv_done"), g.n - 1)
                nc.scalar.copy(xT_hi[g.par][:, :], bank[g.par][:, 0:D]).then_inc(sem("a_hi"), 1)
                nc.scalar.copy(adjT_all[:, bass.ds(g.n * P, P)], bank[2 + g.par][:, 0:P]).then_inc(
                    sem("adjT_kept"), 1)
                wait_from(act, sem("agg_done"), g.n - 1)
                nc.scalar.activation(adjTm[g.par][:, :], bank[2 + g.par][:, 0:P], ACT.Copy,
                                     scale=mask_all[:, bass.ds(g.n, 1)]).then_inc(sem("adjTm_ready"), 1)

            def second(g):
                act.wait_ge(sem("agg_done"), g.n + 1)
                wait_from(act, sem("w_dotted"), g.n - 1)
                nc.scalar.copy(agg_sb[g.par][:, :], bank[6 + g.par][:, 0:D]).then_inc(sem("agg_kept"), 1)
                act.wait_ge(sem("qv_done"), g.n + 1)
                nc.scalar.copy(v_all[:, bass.ds(g.n * D, D)], bank[4 + g.par][:, D:2 * D]).then_inc(
                    sem("v_kept"), 1)

            def both(g):
                first(g)
                second(g.plus(-1))

            first(Graph(0, 0, 0))
            both(Graph(1, 0, 1))
            pairs_of_graphs(act, both, 2, B)
            second(Graph(B - 1, B // 2 - 1, 1))
            act.wait_ge(sem("wneg_ready"), 1)
            nc.scalar.activation(wrow[:, :], bank[0][0:B, 0:P], ACT.Exp, bias=wneg[:, 0:1],
                                 accum_out=wsm[:, :]).then_inc(sem("wexp_ready"), 1)
            phase_end(act, 2)

            def gate_exp(g):
                act.wait_ge(sem("gmin_ready"), g.n + 1)
                nc.scalar.activation(ge[:, :], gneg[:, 0:E], ACT.Exp, bias=gmin[:, 0:1], scale=-1.0,
                                     accum_out=gesum[:, :]).then_inc(sem("ge_ready"), 1)
                nc.scalar.activation(gtanh[:, :], gneg[:, E:E + 1], ACT.Tanh, scale=-0.5).then_inc(
                    sem("ge_ready"), 1)

            def scale_v(g):
                wait_from(act, sem("x1_ready"), g.n)
                nc.scalar.activation(pv[:, :], v_all[:, bass.ds(g.n * D, D)], ACT.Copy,
                                     scale=p_all[:, bass.ds(g.n, 1)]).then_inc(sem("pv_ready"), 1)

            def take_adj(g):
                wait_from(act, sem("x3_summed"), g.n - 1)
                nc.scalar.copy(adjTs[g.par][:, :], adjT_all[:, bass.ds(g.n * P, P)]).then_inc(
                    sem("adjTs_ready"), 1)

            def keep_bias(g):
                act.wait_ge(sem("bexp_done"), g.n + 1)
                wait_from(act, sem("combined"), (g.n - 1) * 9 + 2)
                nc.scalar.copy(bias_sb[:, :], bank[2][:, D:2 * D]).then_inc(sem("bias_kept"), 1)

            def keep_sup(l, g):
                act.wait_ge(sem(f"sup{l}_done"), g.n + 1)
                wait_from(act, sem("x3_summed" if l == 2 else f"agg{l}_done"), g.n)
                nc.scalar.copy(sup[l][:, :], bank[6][:, 0:D]).then_inc(sem(f"sup{l}_kept"), 1)

            def relu(l, g):
                act.wait_ge(sem(f"agg{l}_done"), g.n + 1)
                wait_from(act, sem(f"hid{l}_split"), g.n)
                wait_from(act, sem(f"sup{l + 1}_done"), g.n)
                for dst in (hid_hi[l], hid[l]):
                    for c in range(KD):
                        last = nc.scalar.activation(dst[:, c * P:(c + 1) * P], bank[7][:, c * P:(c + 1) * P],
                                                    ACT.Relu, bias=b12[:, l * KD + c:l * KD + c + 1])
                last.then_inc(sem(f"hid{l}_ready"), 1)

            def hi_a(g):
                act.wait_ge(sem("c_turned"), g.n + 1)
                wait_from(act, sem("experts_done"), 4 * (g.n - 1))
                nc.scalar.copy(xT_hi[g.par][:, :], bank[0][:, 0:D]).then_inc(sem("c_hi"), 1)

            def hi_b(g):
                act.wait_ge(sem("d_turned"), g.n + 1)
                wait_from(act, sem("sup0_done"), g.n)
                nc.scalar.copy(yT_hi[:, :], bank[1][:, 0:D]).then_inc(sem("d_hi"), 1)

            def keep_gwT(g):
                act.wait_ge(sem("gw_turned"), g.n + 1)
                nc.scalar.copy(gwT[:, :], bank[2][0:E, P:2 * P]).then_inc(sem("gwT_kept"), 1)

            def step(g, a=True, nxt=True, nx2=True, b1=True, b2=True):
                one, two = g.plus(-1), g.plus(-2)
                if b1:
                    take_adj(one)
                if a:
                    keep_gwT(g)
                if nx2:
                    scale_v(g.plus(2))
                if a:
                    keep_bias(g)
                if b2:
                    keep_sup(1, two)
                    relu(1, two)
                if b1:
                    hi_b(one)
                if nxt:
                    hi_a(g.plus(1))
                if b1:
                    keep_sup(0, one)
                if nxt:
                    gate_exp(g.plus(1))
                if b1:
                    relu(0, one)
                if b2:
                    keep_sup(2, two)

            act.wait_ge(sem("bias_in"), 64)
            act.wait_ge(sem("p_ready"), 1)
            scale_v(Graph(0, 0, 0))
            scale_v(Graph(1, 0, 1))
            hi_a(Graph(0, 0, 0))
            gate_exp(Graph(0, 0, 0))
            step(Graph(0, 0, 0), b1=False, b2=False)
            step(Graph(1, 0, 1), b2=False)
            pairs_of_graphs(act, step, 2, B - 2)
            step(Graph(B - 2, B // 2 - 1, 0), nx2=False)
            step(Graph(B - 1, B // 2 - 1, 1), nxt=False, nx2=False)
            step(Graph(B, B // 2, 0), a=False, nxt=False, nx2=False)
            step(Graph(B + 1, B // 2, 1), a=False, nxt=False, nx2=False, b1=False)
            phase_end(act, 3)

            def prepare(j):
                act.wait_ge(sem("m_turned"), j + 1)
                wait_from(act, sem("layer1_done"), 4 * j)
                nc.scalar.copy(mT_hi[:, :], bank[0][:, :]).then_inc(sem("m_hi"), 1)
                act.wait_ge(sem("w1_in"), (j + 1) * 16)
                for k in range(KD):
                    nc.scalar.copy(m1h[:, k, :], wraw[:, k * F:(k + 1) * F]).then_inc(sem("w1_hi"), 1)

            def split_w2(j):
                wait_from(act, sem("layer2_done"), j)
                act.wait_ge(sem("w2_in"), (j + 1) * 16)
                for q in range(2):
                    nc.scalar.copy(wsplit[:, 2 * HW + q * HW // 2:2 * HW + (q + 1) * HW // 2],
                                   wraw[:, HW + q * HW // 2:HW + (q + 1) * HW // 2]).then_inc(sem("w2_hi"), 1)

            def gelu(j):
                for q in range(KF // 2):
                    act.wait_ge(sem("layer1_done"), j * 4 + (q + 1))
                    wait_from(act, sem("h_split"), (j - 1) * 4 + (q + 1))
                    nc.scalar.activation(hf[q][:, :], bank[2 + q][:, :], ACT.Gelu).then_inc(sem("gelu"), 1)

            def keep_y(j):
                act.wait_ge(sem("layer2_done"), j + 1)
                wait_from(act, sem("y_out"), j * 16)
                nc.scalar.copy(my[:, :], bank[1][:, :]).then_inc(sem("y_ready"), 1)

            def tile_step(g):
                if not (isinstance(g.n, int) and g.n == 1):
                    keep_y(g.n - 2)
                split_w2(g.n - 1)
                gelu(g.n)
                if has_next(g, 1):
                    prepare(g.n + 1)

            prepare(0)
            gelu(0)
            prepare(1)
            steps_of_tiles(act, tile_step)
            keep_y(TILES - 2)
            split_w2(TILES - 1)
            keep_y(TILES - 1)
            phase_end(act, 4)

        @block.vector
        def _(dve):
            count = 0

            def step_done(ins):
                nonlocal count
                ins.then_inc(sem("routed"), 1)
                count += 1
                return count

            dve.wait_ge(sem("route_in"), 16)
            indices = step_done(nc.vector.tensor_copy(ri_f[:, :], ri_i[:, :]))
            dve.wait_ge(sem("iotas_set"), 2)
            step_done(nc.vector.tensor_copy(steps_f[:, :], steps_i[:, :]))
            iotas = step_done(nc.vector.tensor_copy(tiles_f[:, :], tiles_i[:, :]))
            dve.wait_ge(sem("routed"), indices)
            for e in range(ME):
                nc.vector.tensor_scalar(oh3[:, e, :], ri_f[:, :], float(e), None, ALU.is_equal).then_inc(
                    sem("onehot"), 1)
            dve.wait_ge(sem("totals_done"), 1)

            def running_sum(bufs, width):
                cur, shift = 0, 1
                while shift < width:
                    dve.wait_ge(sem("routed"), count)
                    src, dst = bufs[cur], bufs[1 - cur]
                    step_done(nc.vector.tensor_tensor(dst[..., shift:], src[..., shift:], src[..., :width - shift],
                                                      ALU.add))
                    step_done(nc.vector.tensor_copy(dst[..., :shift], src[..., :shift]))
                    cur, shift = 1 - cur, shift * 2
                dve.wait_ge(sem("routed"), count)
                return cur

            step_done(nc.vector.tensor_copy(scan[0][:, :], bank[1][:, 0:ME * NG]))
            cur = running_sum(sc3, NG)
            step_done(nc.vector.tensor_copy(counts[:, :], sc3[cur][:, :, NG - 1]))
            dve.wait_ge(sem("routed"), step_done(nc.vector.tensor_tensor(
                ranks[:, :], scan[cur][:, :], bank[1][:, 0:ME * NG], ALU.subtract)))
            step_done(nc.vector.tensor_tensor(ranks[:, :], ranks[:, :], bank[1][:, ME * NG:2 * ME * NG], ALU.add))
            dve.wait_ge(sem("routed"), step_done(nc.vector.tensor_tensor(
                cmp_n[:, :].rearrange("p (e m) -> p e m", e=ME),
                counts[:, :].unsqueeze(2).broadcast_to([P, ME, MAXT]),
                steps_f[:, :].unsqueeze(1).broadcast_to([P, ME, MAXT]), ALU.is_gt)))
            dve.wait_ge(sem("routed"), step_done(nc.vector.tensor_reduce(
                ntiles[:, :], cmp_n[:, :].rearrange("p (e m) -> p e m", e=ME), AX.X, ALU.add)))
            step_done(nc.vector.tensor_copy(ends[0][:, :], ntiles[:, :]))
            cur = running_sum([t[:, :] for t in ends], ME)
            step_done(nc.vector.tensor_tensor(base[:, :], ends[cur][:, :], ntiles[:, :], ALU.subtract))
            dve.wait_ge(sem("routed"), step_done(nc.vector.tensor_tensor(
                cmp_t[:, :].rearrange("p (t e) -> p t e", e=ME),
                tiles_f[:, :].unsqueeze(2).broadcast_to([P, TILES, ME]),
                ends[cur][:, :].unsqueeze(1).broadcast_to([P, TILES, ME]), ALU.is_ge)))
            dve.wait_ge(sem("routed"), step_done(nc.vector.tensor_reduce(
                texp_f[:, :], cmp_t[:, :].rearrange("p (t e) -> p t e", e=ME), AX.X, ALU.add)))
            step_done(nc.vector.tensor_scalar(texp_i[:, :], texp_f[:, :], float(ME - 1), None, ALU.min))
            dve.wait_ge(sem("routed"), step_done(nc.vector.tensor_scalar(
                counts[:, :], base[:, :], float(SLOTS), None, ALU.mult)))
            for e in range(ME):
                step_done(nc.vector.scalar_tensor_tensor(
                    out=sc3[0][:, e, :], in0=rk3[:, e, :], scalar=counts[:, e:e + 1], in1=oh3[:, e, :],
                    op0=ALU.add, op1=ALU.mult))
            dve.wait_ge(sem("routed"), count)
            dve.wait_ge(sem("routed"), step_done(nc.vector.tensor_reduce(
                slot_f[:, :], scan[0][:, :].rearrange("p (e g) -> p g e", e=ME), AX.X, ALU.add)))
            step_done(nc.vector.tensor_copy(slot_i[:, :], slot_f[:, :]))
            dve.wait_ge(sem("mask_turned"), 1)
            nc.vector.tensor_copy(mask_all[:, :], bank[2][:, 0:B]).then_inc(sem("mask_ready"), 1)
            for c in range(2):
                dve.wait_ge(sem("qk_turned"), c + 1)
                nc.vector.tensor_copy(qkT[:, c * 512:(c + 1) * 512], bank[3 + c][:, :]).then_inc(sem("qkT_kept"), 1)
            mvf = mv_f[:, :].rearrange("p (k n) -> p k n", k=KD)
            dve.wait_ge(sem("m_done"), 1)
            for k in range(KD):
                nc.vector.tensor_copy(mvf[:, k, 0:D], bank[5][:, k * D:(k + 1) * D]).then_inc(sem("mv_ready"), 1)
            dve.wait_ge(sem("qkv_in"), 32)
            nc.vector.tensor_copy(mvf[:, :, D:2 * D],
                                  qkv_raw[:, KD * 2 * A:].rearrange("p (k n) -> p k n", k=KD)).then_inc(
                sem("mv_ready"), 1)
            dve.wait_ge(sem("experts_hi"), 2)
            for i in range(2):
                nc.vector.tensor_tensor(exl[:, i, :], wraw[:, i * HW:(i + 1) * HW], exh[:, i, :].bitcast(F32),
                                        ALU.subtract).then_inc(sem("experts_split"), 1)
            dve.wait_ge(sem("gnn_hi"), 1)
            nc.vector.tensor_tensor(gnn_lo[:, :], gnn_raw[:, :], gnn_hi[:, :].bitcast(F32),
                                    ALU.subtract).then_inc(sem("gnn_split"), 1)
            dve.wait_ge(sem("gate_hi"), 1)
            nc.vector.tensor_tensor(gate_lo[:, :], gate_raw[:, :], gate_hi[:, :].bitcast(F32),
                                    ALU.subtract).then_inc(sem("gate_split"), 1)
            dve.wait_ge(sem("mv_hi"), 1)
            nc.vector.tensor_tensor(mv_lo[:, :], mv_f[:, :], mv_hi[:, :].bitcast(F32),
                                    ALU.subtract).then_inc(sem("mv_split"), 1)
            phase_end(dve, 1)

            def stats_first(g):
                dve.wait_ge(sem(f"x_in{g.par}"), (g.half + 1) * 16)
                norm_stats(dve, xin[g.par][:, :], LNA, "a", g.n)

            def norm_first(g):
                wait_from(dve, sem("agg_done"), g.n - 1)
                norm_apply(dve, xin[g.par][:, :], xn[g.par][:, :], LNA, "a", g.n)

            def low_first(g):
                dve.wait_ge(sem("a_hi"), g.n + 1)
                wait_from(dve, sem("qv_done"), g.n - 1)
                nc.vector.tensor_tensor(xT_lo[g.par][:, :], bank[g.par][:, 0:D], xT_hi[g.par][:, :].bitcast(F32),
                                        ALU.subtract).then_inc(sem("a_split"), 1)

            def dot(g):
                wait_from(dve, sem("w_column"), g.n - 1)
                dve.wait_ge(sem("v_kept"), g.n + 1)
                dve.wait_ge(sem("agg_kept"), g.n + 1)
                nc.vector.tensor_tensor_reduce(out=agg_sb[g.par][:, :], in0=bank[4 + g.par][:, 0:D],
                                               in1=agg_sb[g.par][:, :], scale=1.0, scalar=0.0, op0=ALU.mult,
                                               op1=ALU.add, accum_out=wcol[g.par][:, :]).then_inc(
                    sem("w_dotted"), 1)

            def keep_column(g):
                dve.wait_ge(sem("w_dotted"), g.n + 1)
                nc.vector.tensor_copy(w_all[:, bass.ds(g.n, 1)], wcol[g.par][:, :]).then_inc(sem("w_column"), 1)

            def both(g, ahead=2):
                if not isinstance(g.n, int) or g.n >= 3:
                    keep_column(g.plus(-3))
                low_first(g)
                if ahead >= 1:
                    norm_first(g.plus(1))
                if ahead >= 2:
                    stats_first(g.plus(2))
                if not isinstance(g.n, int) or g.n >= 2:
                    dot(g.plus(-2))

            stats_first(Graph(0, 0, 0))
            norm_first(Graph(0, 0, 0))
            stats_first(Graph(1, 0, 1))
            both(Graph(0, 0, 0))
            both(Graph(1, 0, 1))
            both(Graph(2, 1, 0))
            both(Graph(3, 1, 1))
            pairs_of_graphs(dve, both, 4, B - 2)
            both(Graph(B - 2, B // 2 - 1, 0), ahead=1)
            both(Graph(B - 1, B // 2 - 1, 1), ahead=0)
            keep_column(Graph(B - 3, B // 2 - 2, 1))
            dot(Graph(B - 2, B // 2 - 1, 0))
            keep_column(Graph(B - 2, B // 2 - 1, 0))
            dot(Graph(B - 1, B // 2 - 1, 1))
            keep_column(Graph(B - 1, B // 2 - 1, 1))
            dve.wait_ge(sem("w_column"), B)
            nc.vector.scalar_tensor_tensor(out=w_all[:, :], in0=w_all[:, :], scalar=INV, in1=mask_all[:, :],
                                           op0=ALU.mult, op1=ALU.mult).then_inc(sem("w_kept"), 1)
            dve.wait_ge(sem("w_turned"), 1)
            nc.vector.tensor_reduce(wmx[:, :], bank[0][0:B, 0:P], AX.X, ALU.max).then_inc(sem("wmx_ready"), 1)
            dve.wait_ge(sem("wmx_ready"), 1)
            nc.vector.tensor_scalar(wneg[:, :], wmx[:, :], -1.0, None, ALU.mult).then_inc(sem("wneg_ready"), 1)
            dve.wait_ge(sem("wexp_ready"), 1)
            nc.vector.reciprocal(wrc[:, :], wsm[:, :]).then_inc(sem("wrc_ready"), 1)
            dve.wait_ge(sem("wrc_ready"), 1)
            nc.vector.tensor_scalar(prow[:, :], wrow[:, :], wrc[:, 0:1], None, ALU.mult).then_inc(
                sem("prow_ready"), 1)
            dve.wait_ge(sem("p_turned"), 1)
            nc.vector.tensor_copy(p_all[:, :], bank[1][:, 0:B]).then_inc(sem("p_ready"), 1)
            phase_end(dve, 2)

            def stats_a(g):
                dve.wait_ge(sem("x1_ready"), g.n + 1)
                norm_stats(dve, x1[g.par][:, :], LNA, "c", g.n)

            def norm_a(g):
                wait_from(dve, sem("c_turned"), g.n)
                norm_apply(dve, x1[g.par][:, :], xn[0][:, :], LNA, "c", g.n)

            def low_a(g):
                dve.wait_ge(sem("c_hi"), g.n + 1)
                wait_from(dve, sem("experts_done"), 4 * (g.n - 1))
                nc.vector.tensor_tensor(xT_lo[g.par][:, :], bank[0][:, 0:D], xT_hi[g.par][:, :].bitcast(F32),
                                        ALU.subtract).then_inc(sem("c_split"), 1)

            def low_b(g):
                dve.wait_ge(sem("d_hi"), g.n + 1)
                wait_from(dve, sem("sup0_done"), g.n)
                nc.vector.tensor_tensor(yT_lo[:, :], bank[1][:, 0:D], yT_hi[:, :].bitcast(F32),
                                        ALU.subtract).then_inc(sem("d_split"), 1)

            def gate_start(g):
                dve.wait_ge(sem("gate_done"), g.n + 1)
                nc.vector.scalar_tensor_tensor(out=gneg[:, :], in0=bank[2][:, 0:E + 1], scalar=-1.0,
                                               in1=gate_bias[:, :], op0=ALU.mult, op1=ALU.subtract).then_inc(
                    sem("gneg_ready"), 1)
                dve.wait_ge(sem("gneg_ready"), g.n + 1)
                nc.vector.tensor_reduce(gmin[:, :], gneg[:, 0:E], AX.X, ALU.min).then_inc(sem("gmin_ready"), 1)

            def gate_end(g):
                dve.wait_ge(sem("ge_ready"), 2 * g.n + 2)
                nc.vector.tensor_scalar(gthr[:, :], gtanh[:, :], 1.0, gesum[:, 0:1], ALU.add, ALU.mult).then_inc(
                    sem("gate_step"), 1)
                dve.wait_ge(sem("gate_step"), g.n * 4 + 1)
                nc.vector.scalar_tensor_tensor(out=gad[:, :], in0=ge[:, :], scalar=2.0 / MAX_THRESHOLD,
                                               in1=gthr[:, 0:1].broadcast_to([P, E]), op0=ALU.mult,
                                               op1=ALU.subtract).then_inc(sem("gate_step"), 1)
                dve.wait_ge(sem("gate_step"), g.n * 4 + 2)
                nc.vector.tensor_scalar(gsel[:, :], gad[:, :], 0.0, TINY, ALU.max, ALU.add,
                                        accum_out=gsum[:, :]).then_inc(sem("gate_step"), 1)
                dve.wait_ge(sem("gate_step"), g.n * 4 + 3)
                nc.vector.reciprocal(gri[:, :], gsum[:, :]).then_inc(sem("gate_step"), 1)
                dve.wait_ge(sem("gate_step"), g.n * 4 + 4)
                wait_from(dve, sem("combined"), (g.n - 1) * 9)
                wait_from(dve, sem("gw_turned"), g.n - 1)
                nc.vector.tensor_scalar(gw[g.par][:, :], gsel[:, :], gri[:, 0:1], None, ALU.mult).then_inc(
                    sem("gw_ready"), 1)

            def combine(g, c):
                dve.wait_ge(sem("experts_done"), g.n * 4 + (c + 1))
                if c == 0:
                    dve.wait_ge(sem("gw_ready"), g.n + 1)
                    dve.wait_ge(sem("bias_kept"), g.n + 1)
                    wait_from(dve, sem("combined"), g.n * 9)
                for h, (dst, start) in enumerate(((even, x1[g.par]), (odd, bias_sb))):
                    e = 2 * c + h
                    if c > 0:
                        dve.wait_ge(sem("combined"), g.n * 9 + (e - 1))
                    nc.vector.scalar_tensor_tensor(
                        out=dst[:, :], in0=bank[EXPERT_BANK[c]][:, h * D:(h + 1) * D], scalar=gw[g.par][:, e:e + 1],
                        in1=(dst if c > 0 else start)[:, :], op0=ALU.mult, op1=ALU.add).then_inc(
                        sem("combined"), 1)

            def merge(g):
                dve.wait_ge(sem("combined"), g.n * 9 + 8)
                wait_from(dve, sem("x2b_ready"), g.n - 1)
                nc.vector.tensor_tensor(x2[g.par][:, :], even[:, :], odd[:, :], ALU.add).then_inc(
                    sem("combined"), 1)

            def stats_b(g):
                dve.wait_ge(sem("combined"), g.n * 9 + 9)
                norm_stats(dve, x2[g.par][:, :], LNB, "d", g.n)

            def norm_b(g):
                wait_from(dve, sem("d_turned"), g.n)
                norm_apply(dve, x2[g.par][:, :], xn[1][:, :], LNB, "d", g.n)

            def finish(g):
                dve.wait_ge(sem("x3_summed"), g.n + 1)
                dve.wait_ge(sem("x2b_ready"), g.n + 1)
                wait_from(dve, sem(f"x3_out{g.par}"), g.half * 16)
                nc.vector.tensor_tensor(xo[g.par][:, :], bank[7][:, 0:D], x2b[g.par][:, :], ALU.add).then_inc(
                    sem("x3_ready"), 1)

            def step(g, a=True, nxt=True, b1=True, b2=True):
                one, two, new = g.plus(-1), g.plus(-2), g.plus(1)
                if nxt:
                    stats_a(new)
                if b1:
                    norm_b(one)
                if a:
                    combine(g, 0)
                if nxt:
                    norm_a(new)
                if a:
                    combine(g, 1)
                if b1:
                    low_b(one)
                if nxt:
                    low_a(new)
                if a:
                    combine(g, 2)
                if nxt:
                    gate_start(new)
                    gate_end(new)
                if a:
                    combine(g, 3)
                if b2:
                    finish(two)
                if a:
                    merge(g)
                    stats_b(g)

            dve.wait_ge(sem("p_ready"), 1)
            stats_a(Graph(0, 0, 0))
            norm_a(Graph(0, 0, 0))
            low_a(Graph(0, 0, 0))
            gate_start(Graph(0, 0, 0))
            gate_end(Graph(0, 0, 0))
            step(Graph(0, 0, 0), b1=False, b2=False)
            step(Graph(1, 0, 1), b2=False)
            pairs_of_graphs(dve, step, 2, B - 2)
            step(Graph(B - 2, B // 2 - 1, 0))
            step(Graph(B - 1, B // 2 - 1, 1), nxt=False)
            step(Graph(B, B // 2, 0), a=False, nxt=False)
            step(Graph(B + 1, B // 2, 1), a=False, nxt=False, b1=False)
            phase_end(dve, 3)

            def norm_rows(j):
                dve.wait_ge(sem("rows_in"), (j + 1) * 16)
                for h in range(HALVES):
                    norm_stats(dve, mx[:, h * D:(h + 1) * D], (LNA, LNB)[h], f"m{h}", j)
                wait_from(dve, sem("m_turned"), j)
                for h in range(HALVES):
                    norm_apply(dve, mx[:, h * D:(h + 1) * D], mxn[:, h * D:(h + 1) * D], (LNA, LNB)[h], f"m{h}", j)

            def prepare(j):
                dve.wait_ge(sem("m_hi"), j + 1)
                nc.vector.tensor_tensor(mT_lo[:, :], bank[0][:, :], mT_hi[:, :].bitcast(F32),
                                        ALU.subtract).then_inc(sem("m_split"), 1)
                for k in range(KD):
                    dve.wait_ge(sem("w1_hi"), j * 2 + (k + 1))
                    last = nc.vector.tensor_tensor(m1l[:, k, :], wraw[:, k * F:(k + 1) * F],
                                                   m1h[:, k, :].bitcast(F32), ALU.subtract)
                last.then_inc(sem("w1_split"), 1)

            def low_w2(j):
                for q in range(2):
                    dve.wait_ge(sem("w2_hi"), j * 2 + (q + 1))
                    lo = 3 * HW + q * HW // 2
                    last = nc.vector.tensor_tensor(wsplit[:, lo:lo + HW // 2],
                                                   wraw[:, HW + q * HW // 2:HW + (q + 1) * HW // 2],
                                                   wsplit[:, lo - HW:lo - HW // 2].bitcast(F32), ALU.subtract)
                last.then_inc(sem("w2_split"), 1)

            def high_h(g):
                wait_from(dve, sem("layer2_done"), g.n - 1)
                for q in range(KF // 2):
                    dve.wait_ge(sem("gelu"), g.n * 4 + (q + 1))
                    nc.vector.tensor_copy(h_hi[g.par][:, q * 512:(q + 1) * 512], hf[q][:, :]).then_inc(
                        sem("h_hi"), 1)

            def tile_step(g):
                low_w2(g.n - 1)
                high_h(g)
                if has_next(g, 1):
                    prepare(g.n + 1)
                if has_next(g, 2):
                    norm_rows(g.n + 2)

            norm_rows(0)
            prepare(0)
            norm_rows(1)
            high_h(Graph(0, 0, 0))
            prepare(1)
            norm_rows(2)
            steps_of_tiles(dve, tile_step)
            low_w2(TILES - 1)
            phase_end(dve, 4)

            def add(g):
                dve.wait_ge(sem(f"fx_in{g.par}"), (g.half + 1) * 16)
                dve.wait_ge(sem(f"fy_in{g.par}"), 16 * TOP * (g.half + 1))
                wait_from(dve, sem("f2"), g.n - 1)
                nc.vector.scalar_tensor_tensor(out=facc[g.par][:, :], in0=fy[g.par][0][:, :],
                                               scalar=rw[:, bass.ds(g.n * TOP, 1)], in1=fx[g.par][:, :],
                                               op0=ALU.mult, op1=ALU.add).then_inc(sem("f1"), 1)
                dve.wait_ge(sem("f1"), g.n + 1)
                wait_from(dve, sem(f"fo_out{g.par}"), g.half * 16)
                nc.vector.scalar_tensor_tensor(out=fo[g.par][:, :], in0=fy[g.par][1][:, :],
                                               scalar=rw[:, bass.ds(g.n * TOP + 1, 1)], in1=facc[g.par][:, :],
                                               op0=ALU.mult, op1=ALU.add).then_inc(sem("f2"), 1)

            dve.wait_ge(sem("route_w_in"), 16)
            for n in range(2):
                add(Graph(n, 0, n))
            pairs_of_graphs(dve, add, 2, TT)

        @block.tensor
        def _(pe):
            pe.wait_ge(sem("onehot"), ME)
            pe.wait_ge(sem("below_set"), 1)
            nc.tensor.matmul(bank[1][:, 0:ME * NG], ones[:, :], onehot[:, :], start=True, stop=True)
            nc.tensor.matmul(bank[1][:, ME * NG:2 * ME * NG], below[:, :], onehot[:, :], start=True,
                             stop=True).then_inc(sem("totals_done"), 1)
            pe.wait_ge(sem("mask_in"), 16)
            pe.wait_ge(sem("ident_set"), 1)
            nc.tensor.transpose(bank[2][:, 0:B], mask_rows[:, :], ident[0:B, 0:B]).then_inc(
                sem("mask_turned"), 1)
            pe.wait_ge(sem("qkv_in"), 32)
            for c in range(2):
                for a in range(KD):
                    for k in range(KD):
                        src = qkv_raw[:, k * 2 * A + c * A + a * P:k * 2 * A + c * A + (a + 1) * P]
                        last = nc.tensor.transpose(bank[3 + c][:, a * D + k * P:a * D + (k + 1) * P], src,
                                                   ident[:, :])
                last.then_inc(sem("qk_turned"), 1)
            pe.wait_ge(sem("qkT_kept"), 2)
            for k in range(KD):
                for a in range(KD):
                    last = nc.tensor.matmul(bank[5][:, k * D:(k + 1) * D],
                                            qkT[:, a * D + k * P:a * D + (k + 1) * P],
                                            qkT[:, KD * D + a * D:KD * D + (a + 1) * D],
                                            start=(a == 0), stop=(a == KD - 1))
            last.then_inc(sem("m_done"), 1)
            phase_end(pe, 1)

            def turn(g):
                pe.wait_ge(sem("a_normed"), g.n + 1)
                wait_from(pe, sem("a_split"), g.n - 1)
                for k in range(KD):
                    nc.tensor.transpose(bank[g.par][:, k * P:(k + 1) * P], xn[g.par][:, k * P:(k + 1) * P],
                                        ident[:, :])
                pe.wait_ge(sem(f"adj_in{g.par}"), (g.half + 1) * 16)
                wait_from(pe, sem("adjTm_ready"), g.n - 1)
                nc.tensor.transpose(bank[2 + g.par][:, 0:P], adjin[g.par][:, :], ident[:, :]).then_inc(
                    sem("a_turned"), 1)

            def products(g):
                pe.wait_ge(sem("adjTm_ready"), g.n + 1)
                wait_from(pe, sem("agg_kept"), g.n - 1)
                nc.tensor.matmul(bank[6 + g.par][:, 0:D], adjTm[g.par][:, :], xn[g.par][:, :], start=True,
                                 stop=True).then_inc(sem("agg_done"), 1)
                pe.wait_ge(sem("a_split"), g.n + 1)
                wait_from(pe, sem("w_dotted"), g.n - 1)
                for k in range(KD):
                    s = slice(k * P, (k + 1) * P)
                    last = split_product(nc.tensor, bank[4 + g.par][:, :],
                                         (xT_hi[g.par][:, s], xT_lo[g.par][:, s]), (mvh[:, k, :], mvl[:, k, :]),
                                         k == 0, k == KD - 1)
                last.then_inc(sem("qv_done"), 1)

            def both(g):
                turn(g)
                products(g.plus(-1))

            turn(Graph(0, 0, 0))
            both(Graph(1, 0, 1))
            pairs_of_graphs(pe, both, 2, B)
            products(Graph(B - 1, B // 2 - 1, 1))
            pe.wait_ge(sem("w_kept"), 1)
            nc.tensor.transpose(bank[0][0:B, 0:P], w_all[:, :], ident[:, :]).then_inc(sem("w_turned"), 1)
            pe.wait_ge(sem("prow_ready"), 1)
            nc.tensor.transpose(bank[1][:, 0:B], prow[:, :], ident[0:B, 0:B]).then_inc(sem("p_turned"), 1)
            phase_end(pe, 2)

            def turn_a(g):
                pe.wait_ge(sem("c_normed"), g.n + 1)
                wait_from(pe, sem("c_split"), g.n)
                for k in range(KD):
                    last = nc.tensor.transpose(bank[0][:, k * P:(k + 1) * P], xn[0][:, k * P:(k + 1) * P],
                                               ident[:, :])
                last.then_inc(sem("c_turned"), 1)

            def turn_b(g):
                pe.wait_ge(sem("d_normed"), g.n + 1)
                wait_from(pe, sem("d_split"), g.n)
                for k in range(KD):
                    last = nc.tensor.transpose(bank[1][:, k * P:(k + 1) * P], xn[1][:, k * P:(k + 1) * P],
                                               ident[:, :])
                last.then_inc(sem("d_turned"), 1)

            def gate(g):
                pe.wait_ge(sem("c_split"), g.n + 1)
                wait_from(pe, sem("bias_kept"), g.n)
                for k in range(KD):
                    s, w = slice(k * P, (k + 1) * P), slice(k * NGATE, (k + 1) * NGATE)
                    last = split_product(nc.tensor, bank[2][:, 0:NGATE],
                                         (xT_hi[g.par][:, s], xT_lo[g.par][:, s]),
                                         (gate_hi[:, w], gate_lo[:, w]), k == 0, k == KD - 1)
                last.then_inc(sem("gate_done"), 1)

            def experts(g, c, k):
                if k == 0:
                    behind = {0: 2 - 9, 1: 8 - 9, 2: 6 - 9, 3: 4}[c]
                    wait_from(pe, sem("combined"), g.n * 9 + behind)
                s = slice(k * P, (k + 1) * P)
                last = split_product(nc.tensor, bank[EXPERT_BANK[c]][:, :], (xT_hi[g.par][:, s], xT_lo[g.par][:, s]),
                                     (exh[:, k, c * 512:(c + 1) * 512], exl[:, k, c * 512:(c + 1) * 512]),
                                     k == 0, k == KD - 1)
                if k == KD - 1:
                    last.then_inc(sem("experts_done"), 1)

            def turn_gw(g):
                pe.wait_ge(sem("gw_ready"), g.n + 1)
                nc.tensor.transpose(bank[2][0:E, P:2 * P], gw[g.par][:, :], ident[:, :]).then_inc(sem("gw_turned"), 1)

            def bias(g):
                pe.wait_ge(sem("gwT_kept"), g.n + 1)
                nc.tensor.matmul(bank[2][:, D:2 * D], gwT[:, :], bexp[:, :], start=True, stop=True).then_inc(
                    sem("bexp_done"), 1)

            def support(l, g):
                pe.wait_ge(sem("d_split" if l == 0 else f"hid{l - 1}_split"), g.n + 1)
                if l == 1:
                    wait_from(pe, sem("sup2_kept"), g.n)
                elif l == 0:
                    wait_from(pe, sem("sup1_kept"), g.n)
                else:
                    nxt = g.n + 2
                    pe.wait_ge(sem("sup0_kept"), min(nxt, B) if isinstance(nxt, int) else nxt)
                hi, lo = (yT_hi, yT_lo) if l == 0 else (hid_hi[l - 1], hid_lo[l - 1])
                for k in range(KD):
                    s = slice(k * P, (k + 1) * P)
                    last = split_product(nc.tensor, bank[6][:, 0:D], (hi[:, s], lo[:, s]),
                                         (gnh[:, l, k, :], gnl[:, l, k, :]), k == 0, k == KD - 1)
                last.then_inc(sem(f"sup{l}_done"), 1)

            def aggregate(l, g):
                pe.wait_ge(sem(f"sup{l}_kept"), g.n + 1)
                if l == 1:
                    wait_from(pe, sem("x3_ready"), g.n)
                    wait_from(pe, sem("hid0_ready"), g.n + 1)
                else:
                    pe.wait_ge(sem("adjTs_ready"), g.n + 1)
                    wait_from(pe, sem("hid1_ready"), g.n)
                for c in range(KD):
                    last = nc.tensor.matmul(bank[7][:, c * P:(c + 1) * P], sup[l][:, c * P:(c + 1) * P],
                                            adjTs[g.par][:, :], start=True, stop=True)
                last.then_inc(sem(f"agg{l}_done"), 1)

            def last_sum(g):
                pe.wait_ge(sem("sup2_kept"), g.n + 1)
                after = g.n + 2
                pe.wait_ge(sem("hid0_ready"), after if not isinstance(after, int) else min(after, B))
                nc.tensor.matmul(bank[7][:, 0:D], adjTs[g.par][:, :], sup[2][:, :], start=True,
                                 stop=True).then_inc(sem("x3_summed"), 1)

            def step(g, a=True, nxt=True, b1=True, b2=True):
                one, two, new = g.plus(-1), g.plus(-2), g.plus(1)
                if a:
                    experts(g, 0, 0)
                    turn_gw(g)
                    experts(g, 0, 1)
                    bias(g)
                if b2:
                    support(1, two)
                if a:
                    experts(g, 1, 0)
                if b2:
                    aggregate(1, two)
                if a:
                    experts(g, 1, 1)
                if b1:
                    turn_b(one)
                if nxt:
                    turn_a(new)
                if a:
                    experts(g, 2, 0)
                    experts(g, 2, 1)
                if b1:
                    support(0, one)
                if nxt:
                    gate(new)
                if b1:
                    aggregate(0, one)
                if b2:
                    support(2, two)
                if a:
                    experts(g, 3, 0)
                    experts(g, 3, 1)
                if b2:
                    last_sum(two)

            turn_a(Graph(0, 0, 0))
            gate(Graph(0, 0, 0))
            step(Graph(0, 0, 0), b1=False, b2=False)
            step(Graph(1, 0, 1), b2=False)
            pairs_of_graphs(pe, step, 2, B - 2)
            step(Graph(B - 2, B // 2 - 1, 0))
            step(Graph(B - 1, B // 2 - 1, 1), nxt=False)
            step(Graph(B, B // 2, 0), a=False, nxt=False)
            step(Graph(B + 1, B // 2, 1), a=False, nxt=False, b1=False)
            phase_end(pe, 3)

            def turn_tile(j):
                for h in range(HALVES):
                    pe.wait_ge(sem(f"m{h}_normed"), j + 1)
                wait_from(pe, sem("m_split"), j)
                for k in range(KD):
                    for h in range(HALVES):
                        last = nc.tensor.transpose(bank[0][:, k * SLOTS + h * P:k * SLOTS + (h + 1) * P],
                                                   mxn[:, h * D + k * P:h * D + (k + 1) * P], ident[:, :])
                last.then_inc(sem("m_turned"), 1)

            def layer1(j):
                pe.wait_ge(sem("m_split"), j + 1)
                pe.wait_ge(sem("w1_split"), j + 1)
                for q in range(KF // 2):
                    wait_from(pe, sem("gelu"), (j - 1) * 4 + (q + 1))
                    for m in (2 * q, 2 * q + 1):
                        for k in range(KD):
                            f, s = slice(m * P, (m + 1) * P), slice(k * SLOTS, (k + 1) * SLOTS)
                            last = split_product(nc.tensor, bank[2 + q][:, (m % 2) * SLOTS:(m % 2 + 1) * SLOTS],
                                                 (m1h[:, k, f], m1l[:, k, f]), (mT_hi[:, s], mT_lo[:, s]),
                                                 k == 0, k == KD - 1)
                    last.then_inc(sem("layer1_done"), 1)

            def layer2(g):
                j = g.n
                pe.wait_ge(sem("w2_split"), j + 1)
                wait_from(pe, sem("y_ready"), j)
                for h in range(HALVES):
                    for m in range(KF):
                        if h == 0 and m % 2 == 0:
                            pe.wait_ge(sem("h_split"), j * 4 + (m // 2 + 1))
                        s = slice(m * SLOTS + h * P, m * SLOTS + (h + 1) * P)
                        last = split_product(nc.tensor, bank[1][:, h * D:(h + 1) * D], (h_hi[g.par][:, s], h_lo[g.par][:, s]),
                                             (m2h[:, m, :], m2l[:, m, :]), m == 0, m == KF - 1)
                last.then_inc(sem("layer2_done"), 1)

            def tile_step(g):
                layer1(g.n)
                if has_next(g, 1):
                    turn_tile(g.n + 1)
                layer2(g.plus(-1))

            turn_tile(0)
            layer1(0)
            turn_tile(1)
            steps_of_tiles(pe, tile_step)
            layer2(Graph(TILES - 1, (TILES - 1) // 2, (TILES - 1) % 2))
            phase_end(pe, 4)


_INS = ['x', 'adj', 'nodemask', 'L0_gnn_Wqk', 'L0_gnn_Wv', 'L0_ffn_W_gate', 'L0_ffn_b_gate', 'L0_ffn_W_thr',
        'L0_ffn_b_thr', 'L0_ffn_W_exp', 'L0_ffn_b_exp', 'L1_gnn_W1', 'L1_gnn_b1', 'L1_gnn_W2', 'L1_gnn_b2',
        'L1_gnn_W3', 'L1_gnn_b3', 'L1_ffn_expert_weights', 'L1_ffn_expert_indices', 'L1_ffn_w1', 'L1_ffn_w2']
_OUT = ((64, 128, 256), 'float32')


def kernel(**inputs):
    import numpy as _np
    import concourse.bacc as _bacc
    from concourse import mybir as _mybir
    from concourse.bass_utils import run_bass_kernel_spmd as _run

    nc = _bacc.Bacc("TRN2", target_bir_lowering=False, num_devices=1)
    arrays, args = {}, []
    for name in _INS:
        a = _np.ascontiguousarray(inputs[name])
        arrays[f"in_{name}_dram"] = a
        args.append(nc.dram_tensor(f"in_{name}_dram", a.shape, _mybir.dt.from_np(a.dtype), kind="ExternalInput").ap())
    shape, dtype = _OUT
    args.append(nc.dram_tensor("out_dram", shape, _mybir.dt.from_np(_np.dtype(dtype)), kind="ExternalOutput").ap())
    build(nc, *args)
    r = _run(nc, [arrays], core_ids=[0])
    return r.results[0]["out_dram"]
```

```python
from contextlib import ExitStack

import concourse.bass as bass
from concourse import mybir

ALU = mybir.AluOpType
ACT = mybir.ActivationFunctionType
AX = mybir.AxisListType
F32 = mybir.dt.float32
F32R = mybir.dt.float32r
I32 = mybir.dt.int32

P = 128
EPS = 1e-5
MAX_THRESHOLD = 0.25
ENGINES = 5
TINY = 1e-30
EXPERT_BANK = (3, 4, 5, 4)


class Graph:

    def __init__(self, n, half, par, quarter=None, slot=None):
        self.n, self.half, self.par = n, half, par
        self.quarter, self.slot = (n // 4, n % 4) if isinstance(n, int) else (quarter, slot)

    def plus(self, k):
        total = self.par + k
        if self.slot is None:
            return Graph(self.n + k, self.half + total // 2, total % 2)
        of_four = self.slot + k
        return Graph(self.n + k, self.half + total // 2, total % 2, self.quarter + of_four // 4, of_four % 4)


def wait_from(eng, sem, value):
    if not (isinstance(value, int) and value <= 0):
        eng.wait_ge(sem, value)


def pairs_of_graphs(eng, body, first, last):
    with eng.Fori(first // 2, last // 2) as half:
        for par in range(2):
            body(Graph(half * 2 + par, half, par))


def second_pair(body):
    for n in (2, 3):
        body(Graph(n, 1, n - 2))


def fours_of_graphs(eng, body, first, last):
    with eng.Fori(first // 4, last // 4) as quarter:
        for slot in range(4):
            body(Graph(quarter * 4 + slot, quarter * 2 + slot // 2, slot % 2, quarter, slot))


def split_product(pe, out, lhs, rhs, first, last):
    (lhs_hi, lhs_lo), (rhs_hi, rhs_lo) = lhs, rhs
    pe.matmul(out, lhs_lo, rhs_hi, start=first, stop=False)
    pe.matmul(out, lhs_hi, rhs_lo, start=False, stop=False)
    return pe.matmul(out, lhs_hi, rhs_hi, start=False, stop=last)


def build(nc, x, adj, nodemask, Wqk, Wv, W_gate, b_gate, W_thr, b_thr, W_exp, b_exp,
          W1, b1, W2, b2, W3, b3, moe_weights, moe_indices, moe_w1, moe_w2, out):
    B, N, D = x.shape
    A = Wqk.shape[1] // 2
    E = W_gate.shape[1]
    ME, _, F = moe_w1.shape
    T, TOP = moe_indices.shape
    KD = D // P
    KF = F // P
    TT = T // P
    SLOTS = 256
    HALVES = SLOTS // P
    TILES = (T * TOP + ME * (SLOTS - 1)) // SLOTS
    NG = TT * TOP
    MAXT = T * TOP // SLOTS
    INV = 1.0 / float(A) ** 0.5
    assert TILES * HALVES % 4 == 2 and B % 4 == 0 and N == P and D == A == 2 * P and E == ME == 8

    xg = nc.dram_tensor("routed_x", [TILES * SLOTS, D], F32)
    yg = nc.dram_tensor("routed_y", [TILES * SLOTS, D], F32)

    ctx = ExitStack()
    with ctx:
        def sb(name, shape, dt=F32, stack=ctx):
            return stack.enter_context(nc.sbuf_tensor(name, shape, dt))

        sems = {}

        def sem(name):
            if name not in sems:
                sems[name] = ctx.enter_context(nc.semaphore(name))
            return sems[name]

        bank = [ctx.enter_context(nc.psum_tensor(f"bank{i}", [P, 512], F32)) for i in range(8)]

        ident = sb("ident", [P, P])
        ones = sb("ones", [P, P])
        below = sb("below", [P, P])
        zeros = sb("zeros", [P, D])
        wraw = sb("wraw", [P, 2 * KD * F])
        wsplit = sb("wsplit", [P, 4 * KD * F], F32R)
        gnn_hi = sb("gnn_hi", [P, 3 * KD * D], F32R)
        gnn_lo = sb("gnn_lo", [P, 3 * KD * D], F32R)
        NGATE = E + 2
        gate_raw = sb("gate_raw", [P, KD * NGATE])
        gate_split = sb("gate_split", [P, KD * 2 * NGATE], F32R)
        gate_bias = sb("gate_bias", [P, E + 1])
        bexp = sb("bexp", [E, D])
        b12 = sb("b12", [P, 2 * KD])
        b3_all = sb("b3_all", [P, D])
        mask_rows = sb("mask_rows", [B, P])
        mask_all = sb("mask_all", [P, B])
        w_all = sb("w_all", [P, B])
        p_all = sb("p_all", [P, B])

        ri_i = sb("ri_i", [P, NG], I32)
        rw = sb("rw", [P, NG])
        ri_f = sb("ri_f", [P, NG])
        ends = [sb(f"ends{i}", [P, ME]) for i in range(2)]
        counts = sb("counts", [P, ME])
        first_slot = sb("first_slot", [P, ME])
        ntiles = sb("ntiles", [P, ME])
        base = sb("base", [P, ME])
        steps_i = sb("steps_i", [P, MAXT], I32)
        steps_f = sb("steps_f", [P, MAXT])
        tiles_i = sb("tiles_i", [P, TILES], I32)
        tiles_f = sb("tiles_f", [P, TILES])
        slot_f = sb("slot_f", [P, NG])
        slot_i = sb("slot_i", [P, NG], I32)
        texp_f = sb("texp_f", [P, TILES])
        texp_i = sb("texp_i", [P, TILES], I32)

        phase1 = ExitStack()
        adjin = [sb(f"adjin{i}", [P, P], F32, phase1) for i in range(2)]
        adjTm = [sb(f"adjTm{i}", [P, P], F32, phase1) for i in range(2)]
        agg_sb = [sb(f"agg_sb{i}", [P, D], F32, phase1) for i in range(2)]
        mv_hi = sb("mv_hi", [P, KD * 2 * D], F32R, phase1)
        mv_lo = sb("mv_lo", [P, KD * 2 * D], F32R, phase1)
        xa = [sb(f"xa{i}", [P, D], F32, phase1) for i in range(4)]
        phase1.close()
        x1 = [sb(f"x1_{i}", [P, D]) for i in range(2)]
        x2 = [sb(f"x2_{i}", [P, D]) for i in range(2)]
        x2b = [sb(f"x2b_{i}", [P, D]) for i in range(2)]
        xo = [sb(f"xo{i}", [P, D]) for i in range(2)]
        pv = sb("pv", [P, D])
        odd = sb("odd", [P, D])
        even = sb("even", [P, D])
        bias_sb = sb("bias_sb", [P, D])
        sup = [sb(f"sup{i}", [P, D]) for i in range(3)]
        hid = [sb(f"hid{i}", [P, D]) for i in range(2)]
        xin = [sb(f"xin{i}", [P, D]) for i in range(2)]
        stats = sb("stats", [P, 6])
        mv = sb("mv", [P, 2])
        veps = sb("veps", [P, 1])
        rstd = sb("rstd", [P, 1])
        statsb = sb("statsb", [P, 6])
        mvb = sb("mvb", [P, 2])
        vepsb = sb("vepsb", [P, 1])
        rstdb = sb("rstdb", [P, 1])
        minus_half = sb("minus_half", [P, 1])
        xn = [sb(f"xn{i}", [P, D]) for i in range(2)]
        wcol = [sb(f"wcol{i}", [P, 1]) for i in range(2)]
        xT_hi = [sb(f"xT_hi{i}", [P, D], F32R) for i in range(2)]
        xT_lo = [sb(f"xT_lo{i}", [P, D], F32R) for i in range(2)]
        yT_hi = sb("yT_hi", [P, D], F32R)
        yT_lo = sb("yT_lo", [P, D], F32R)
        gneg = sb("gneg", [P, E + 1])
        gpart = sb("gpart", [P, E + 1])
        gmin = sb("gmin", [P, 1])
        ge = sb("ge", [P, E])
        gesum = sb("gesum", [P, 1])
        gtanh = sb("gtanh", [P, 1])
        gthr = sb("gthr", [P, 1])
        gad = sb("gad", [P, E + 1])
        gsel = sb("gsel", [P, E + 1])
        gsum = sb("gsum", [P, 1])
        gri = sb("gri", [P, 1])
        gw = [sb(f"gw{i}", [P, E]) for i in range(2)]
        gwT = sb("gwT", [E, P])
        adjTs = [sb(f"adjTs{i}", [P, P]) for i in range(2)]
        hid_hi = [sb(f"hid_hi{i}", [P, D], F32R) for i in range(2)]
        hid_lo = [sb(f"hid_lo{i}", [P, D], F32R) for i in range(2)]
        sx = sb("sx", [P, D])
        sidx = sb("sidx", [P, TOP], I32)
        wmx = sb("wmx", [B, 1])
        wneg = sb("wneg", [B, 1])
        wrow = sb("wrow", [B, P])
        wsm = sb("wsm", [B, 1])
        wrc = sb("wrc", [B, 1])
        prow = sb("prow", [B, P])

        early = ExitStack()
        v_all = sb("v_all", [P, B * D], F32, early)
        adjT_all = sb("adjT_all", [P, B * P], F32, early)
        early.close()
        late = ExitStack()
        mx = sb("mx", [P, HALVES * D], F32, late)
        mxn = sb("mxn", [P, HALVES * D], F32, late)
        mT_hi = sb("mT_hi", [P, KD * SLOTS], F32R, late)
        mT_lo = sb("mT_lo", [P, KD * SLOTS], F32R, late)
        hf = [sb(f"hf{i}", [P, 512], F32, late) for i in range(KF // 2)]
        h_hi = [sb(f"h_hi{i}", [P, KF * SLOTS], F32R, late) for i in range(2)]
        h_lo = [sb(f"h_lo{i}", [P, KF * SLOTS], F32R, late) for i in range(2)]
        my = sb("my", [P, HALVES * D], F32, late)
        fx = [sb(f"fx{i}", [P, 2 * D], F32, late) for i in range(2)]
        fy = [[sb(f"fy{i}_{k}", [P, D], F32, late) for k in range(2 * TOP)] for i in range(2)]
        fslot = [sb(f"fslot{i}", [P, 2 * TOP], I32, late) for i in range(2)]
        facc = [sb(f"facc{i}", [P, 2 * D], F32, late) for i in range(2)]
        fo = [sb(f"fo{i}", [P, 2 * D], F32, late) for i in range(2)]
        late.close()
        setup = ExitStack()
        qkv_raw = sb("qkv_raw", [P, KD * (2 * A + D)], F32, setup)
        qkT = sb("qkT", [P, 2 * KD * D], F32, setup)
        gnn_raw = sb("gnn_raw", [P, 3 * KD * D], F32, setup)
        mv_f = sb("mv_f", [P, KD * 2 * D], F32, setup)
        onehot = sb("onehot", [P, ME * NG], F32, setup)
        scan = [sb(f"scan{i}", [P, ME * NG], F32, setup) for i in range(2)]
        ranks = sb("ranks", [P, ME * NG], F32, setup)
        cmp_n = sb("cmp_n", [P, ME * MAXT], F32, setup)
        cmp_t = sb("cmp_t", [P, TILES * ME], F32, setup)
        setup.close()

        mvh, mvl = (t[:, :].rearrange("p (k n) -> p k n", k=KD) for t in (mv_hi, mv_lo))
        gnh, gnl = (t[:, :].rearrange("p (l k n) -> p l k n", l=3, k=KD) for t in (gnn_hi, gnn_lo))
        graw = gate_raw[:, :].rearrange("p (k n) -> p k n", k=KD)
        gsplit = gate_split[:, :].rearrange("p (k t n) -> p k t n", k=KD, t=2)
        HW = KD * F
        exh, exl = (wsplit[:, i * 2 * HW:(i + 1) * 2 * HW].rearrange("p (k n) -> p k n", k=KD) for i in range(2))
        m1h, m1l = (wsplit[:, i * HW:(i + 1) * HW].rearrange("p (k n) -> p k n", k=KD) for i in range(2))
        W2_AT = {True: 0, False: 2 * HW}
        m2 = {last: [wsplit[:, at + i * HW:at + (i + 1) * HW].rearrange("p (k n) -> p k n", k=KF)
                     for i in range(2)] for last, at in W2_AT.items()}
        oh3 = onehot[:, :].rearrange("p (e g) -> p e g", e=ME)
        sc3 = [s[:, :].rearrange("p (e g) -> p e g", e=ME) for s in scan]
        rk3 = ranks[:, :].rearrange("p (e g) -> p e g", e=ME)

        PENULT, LAST = Graph(B - 2, B // 2 - 1, 0), Graph(B - 1, B // 2 - 1, 1)
        CHUNKS = 2 * HW // D
        HIGH_FROM, LOW_FROM = 6, 8

        block = ctx.enter_context(nc.Block())

        def phase_end(eng, k):
            eng.drain().then_inc(sem("phase_done"), 1)
            eng.wait_ge(sem("phase_done"), ENGINES * k)

        def steps_of_tiles(eng, step):
            last_pair = (TILES - 2) // 2 * 2
            step(Graph(1, 0, 1))
            second_pair(step)
            pairs_of_graphs(eng, step, 4, last_pair)
            for n in range(last_pair, TILES):
                step(Graph(n, n // 2, n % 2))

        def has_next(g, ahead):
            return not isinstance(g.n, int) or g.n + ahead < TILES

        def own_wait(eng, *waits):
            for s, v in waits:
                wait_from(eng, s, v)
            eng.sem_inc(sem("passed"), 1)

        def norm_stats(dve, src, bufs, name, n, between=None):
            st, mean_var, _, _ = bufs
            step = sem(name + "_step")
            nc.vector.bn_stats(st[:, :], src).then_inc(step, 1)
            if between is not None:
                between()
            own_wait(dve, (step, n * 2 + 1))
            nc.vector.bn_aggr(mean_var[:, :], st[:, :]).then_inc(step, 1)

        def norm_rstd(pool, bufs, name, n):
            _, mean_var, veps, rs = bufs
            own_wait(pool, (sem(name + "_step"), n * 2 + 2))
            nc.gpsimd.tensor_scalar(veps[:, :], mean_var[:, 1:2], EPS, None, ALU.add).then_inc(
                sem(name + "_veps"), 1)
            pool.wait_ge(sem(name + "_veps"), n + 1)
            nc.gpsimd.tensor_tensor(rs[:, :], veps[:, :], minus_half[:, :], ALU.pow).then_inc(
                sem(name + "_rstd"), 1)

        def norm_apply(dve, src, dst, bufs, name, n):
            _, mean_var, _, rs = bufs
            dve.wait_ge(sem(name + "_rstd"), n + 1)
            nc.vector.tensor_scalar(dst, src, mean_var[:, 0:1], rs[:, 0:1], ALU.subtract, ALU.mult).then_inc(
                sem(name + "_normed"), 1)

        LNA, LNB = (stats, mv, veps, rstd), (statsb, mvb, vepsb, rstdb)

        @block.sync
        def _(sp):
            sp.dma_start(qkv_raw[:, 0:KD * 2 * A].rearrange("p (k n) -> p k n", k=KD),
                         Wqk.rearrange("(k p) n -> p k n", p=P)).then_inc(sem("qkv_in"), 16)
            sp.dma_start(qkv_raw[:, KD * 2 * A:].rearrange("p (k n) -> p k n", k=KD),
                         Wv.rearrange("(k p) n -> p k n", p=P)).then_inc(sem("qkv_in"), 16)
            sp.dma_start(mask_rows[:, :], nodemask).then_inc(sem("mask_in"), 16)
            sp.dma_start(ri_i[:, :].rearrange("p (c k) -> p c k", k=TOP),
                         moe_indices.rearrange("(c p) k -> p c k", p=P)).then_inc(sem("route_in"), 16)
            sp.dma_start(rw[:, :].rearrange("p (c k) -> p c k", k=TOP),
                         moe_weights.rearrange("(c p) k -> p c k", p=P)).then_inc(sem("route_w_in"), 16)
            def load1(g):
                wait_from(sp, sem("a_normed"), g.n - 3)
                sp.dma_start(xa[g.slot][:, :], x[bass.ds(g.n, 1)].rearrange("o p d -> (o p) d")).then_inc(
                    sem(f"a_in{g.slot}"), 16)
                wait_from(sp, sem("a_turned"), g.n - 1)
                sp.dma_start(adjin[g.par][:, :], adj[bass.ds(g.n, 1)].rearrange("o p d -> (o p) d")).then_inc(
                    sem(f"adj_in{g.par}"), 16)

            for n in range(2):
                load1(Graph(n, 0, n))
            for l, w in enumerate((W1, W2, W3)):
                sp.dma_start(gnn_raw[:, l * KD * D:(l + 1) * KD * D].rearrange("p (k n) -> p k n", k=KD),
                             w.rearrange("(k p) n -> p k n", p=P)).then_inc(sem("gnn_in"), 16)
            sp.wait_ge(sem("gate_zeroed"), 1)
            gr = gate_raw[:, :].rearrange("p (k n) -> p k n", k=KD)
            sp.dma_start(gr[:, :, 0:E], W_gate.rearrange("(k p) n -> p k n", p=P)).then_inc(sem("gate_in"), 16)
            sp.dma_start(gr[:, :, E:E + 1], W_thr.rearrange("(k p) n -> p k n", p=P),
                         allow_slow_non_contiguous=True).then_inc(sem("gate_in"), 16)
            sp.dma_start(gate_bias[:, 0:E], b_gate.partition_broadcast(P)).then_inc(sem("gate_in"), 16)
            sp.dma_start(gate_bias[:, E:E + 1], b_thr.partition_broadcast(P)).then_inc(sem("gate_in"), 16)
            sp.dma_start(bexp[:, :], b_exp).then_inc(sem("bias_in"), 16)
            sp.dma_start(b3_all[:, :], b3.partition_broadcast(P)).then_inc(sem("bias_in"), 16)
            for l, b in enumerate((b1, b2)):
                sp.dma_start(b12[:, l * KD:(l + 1) * KD], b.rearrange("(k p) -> p k", p=P),
                             allow_slow_non_contiguous=True).then_inc(sem("bias_in"), 16)
            wv = wraw[:, :].rearrange("p (k e n) -> p k e n", k=KD, e=E)
            for e in range(E):
                sp.dma_start(wv[:, :, e, :], W_exp[e].rearrange("(k p) n -> p k n", p=P)).then_inc(
                    sem("experts_in"), 16)
            phase_end(sp, 1)

            def load_and_zero(g):
                load1(g)
                sp.dma_start(xg[bass.ds((g.n - 2) * P, P), :], zeros[:, :]).then_inc(sem("slots_zeroed"), 16)

            sp.wait_ge(sem("zeroed"), 1)
            zeroed_by = 2 + TILES * HALVES
            second_pair(load_and_zero)
            fours_of_graphs(sp, load_and_zero, 4, zeroed_by)
            fours_of_graphs(sp, load1, zeroed_by, B)
            for n in range(2):
                sp.dma_start(xin[n][:, :], x[n]).then_inc(sem(f"x_in{n}"), 16)
            phase_end(sp, 2)

            def load2(g):
                wait_from(sp, sem("x1_ready"), g.n - 1)
                sp.dma_start(xin[g.par][:, :], x[bass.ds(g.n, 1)].rearrange("o p d -> (o p) d")).then_inc(
                    sem(f"x_in{g.par}"), 16)

            def store(g):
                sp.wait_ge(sem("x3_ready"), g.n + 1)
                sp.dma_start(out[bass.ds(g.n, 1)].rearrange("o p d -> (o p) d"), xo[g.par][:, :]).then_inc(
                    sem(f"x3_out{g.par}"), 16)

            def step(g):
                load2(g.plus(3))
                store(g.plus(-2))

            for n in range(2, 5):
                load2(Graph(n, n // 2, n % 2))
            pairs_of_graphs(sp, step, 2, B - 4)
            step(Graph(B - 4, B // 2 - 2, 0))
            store(Graph(B - 5, B // 2 - 3, 1))
            store(Graph(B - 4, B // 2 - 2, 0))

            def load_rows(j):
                for h in range(HALVES):
                    wait_from(sp, sem(f"m{h}_normed"), j)
                sp.dma_start(mx[:, :].rearrange("p (h d) -> p h d", h=HALVES),
                             xg[bass.ds(j * SLOTS, SLOTS), :].rearrange("(h p) d -> p h d", p=P)).then_inc(
                    sem("rows_in"), 16)

            def load_w1(j):
                e = sp.value_load(texp_i[0:1, bass.ds(j, 1)], min_val=0, max_val=ME - 1)
                wait_from(sp, sem("w1_split"), j)
                sp.dma_start(wraw[:, 0:HW].rearrange("p (k n) -> p k n", k=KD),
                             moe_w1[bass.ds(e, 1)].rearrange("o (k p) n -> p (o k) n", p=P)).then_inc(
                    sem("w1_in"), 16)

            def load_w2(j):
                e = sp.value_load(texp_i[0:1, bass.ds(j, 1)], min_val=0, max_val=ME - 1)
                wait_from(sp, sem("w2_split"), j)
                sp.dma_start(wraw[:, HW:2 * HW].rearrange("p (k n) -> p k n", k=KF),
                             moe_w2[bass.ds(e, 1)].rearrange("o (k p) n -> p (o k) n", p=P)).then_inc(
                    sem("w2_in"), 16)

            def store_tile(j):
                sp.wait_ge(sem("y_ready"), j + 1)
                sp.dma_start(yg[bass.ds(j * SLOTS, SLOTS), :].rearrange("(h p) d -> p h d", p=P),
                             my[:, :].rearrange("p (h d) -> p h d", h=HALVES)).then_inc(sem("y_out"), 16)

            def tile_step(g):
                if has_next(g, 1):
                    load_w1(g.n + 1)
                if has_next(g, 2):
                    load_rows(g.n + 2)
                load_w2(g.n)
                if not (isinstance(g.n, int) and g.n == 1):
                    store_tile(g.n - 2)

            load_w1(0)
            load_w2(0)
            sp.wait_ge(sem("scattered"), 16 * TOP * TT)
            sp.wait_ge(sem("pv_ready"), B)
            load_rows(0)
            store(Graph(B - 3, B // 2 - 2, 1))
            load_w1(1)
            load_rows(1)
            store(Graph(B - 2, B // 2 - 1, 0))
            store(Graph(B - 1, B // 2 - 1, 1))
            load_rows(2)
            steps_of_tiles(sp, tile_step)
            store_tile(TILES - 2)
            store_tile(TILES - 1)
            def load_x3(g):
                wait_from(sp, sem("f1"), (g.n - 1) * 2)
                sp.dma_start(fx[g.par][:, :].rearrange("p (o d) -> p o d", o=2),
                             out[bass.ds(g.n * 2, 2)].rearrange("o p d -> p o d")).then_inc(
                    sem(f"fx_in{g.par}"), 16)

            def store_sum(g):
                sp.wait_ge(sem("f2"), (g.n + 1) * 2)
                sp.dma_start(out[bass.ds(g.n * 2, 2)].rearrange("o p d -> p o d"),
                             fo[g.par][:, :].rearrange("p (o d) -> p o d", o=2)).then_inc(
                    sem(f"fo_out{g.par}"), 16)

            def pair_step(g):
                load_x3(g)
                store_sum(g.plus(-2))

            for par in range(2):
                sp.wait_ge(sem(f"x3_out{par}"), 16 * (B // 2))
            load_x3(Graph(0, 0, 0))
            load_x3(Graph(1, 0, 1))
            sp.wait_ge(sem("y_out"), 16 * TILES)
            pairs_of_graphs(sp, pair_step, 2, TT // 2)
            store_sum(Graph(TT // 2 - 2, TT // 4 - 1, 0))
            store_sum(Graph(TT // 2 - 1, TT // 4 - 1, 1))
            for par in range(2):
                sp.wait_ge(sem(f"fo_out{par}"), 16 * (TT // 4))

        @block.gpsimd
        def _(pool):
            nc.gpsimd.memset(gate_raw[:, :], 0.0).then_inc(sem("gate_zeroed"), 1)
            nc.gpsimd.memset(minus_half[:, :], -0.5).then_inc(sem("minus_half_set"), 1)
            nc.gpsimd.memset(zeros[:, :], 0.0).then_inc(sem("zeroed"), 1)
            nc.gpsimd.memset(gad[:, E:E + 1], TINY).then_inc(sem("tiny_set"), 1)
            nc.gpsimd.memset(ones[:, :], 1.0).then_inc(sem("ones_set"), 1)
            nc.gpsimd.memset(ident[:, :], 0.0).then_inc(sem("ident_zeroed"), 1)
            pool.wait_ge(sem("ident_zeroed"), 1)
            nc.gpsimd.affine_select(out=ident[:, :], in_=ident[:, :], compare_op=ALU.not_equal, fill=1.0,
                                    base=0, pattern=[[-1, P]], channel_multiplier=1).then_inc(sem("ident_set"), 1)
            pool.wait_ge(sem("ones_set"), 1)
            nc.gpsimd.affine_select(out=below[:, :], in_=ones[:, :], compare_op=ALU.is_gt, fill=0.0,
                                    base=0, pattern=[[1, P]], channel_multiplier=-1).then_inc(sem("below_set"), 1)
            nc.gpsimd.iota(steps_i[:, :], pattern=[[SLOTS, MAXT]], base=0, channel_multiplier=0).then_inc(
                sem("iotas_set"), 1)
            nc.gpsimd.iota(tiles_i[:, :], pattern=[[1, TILES]], base=0, channel_multiplier=0).then_inc(
                sem("iotas_set"), 1)
            pool.wait_ge(sem("minus_half_set"), 1)
            norm_rstd(pool, LNA, "a", 0)
            pool.wait_ge(sem("gnn_hi"), 1)
            nc.gpsimd.tensor_tensor(gnn_lo[:, :], gnn_raw[:, :], gnn_hi[:, :].bitcast(F32),
                                    ALU.subtract).then_inc(sem("gnn_split"), 1)
            pool.wait_ge(sem("gate_hi"), 1)
            nc.gpsimd.tensor_tensor(gsplit[:, :, 1, :], graw, gsplit[:, :, 0, :].bitcast(F32),
                                    ALU.subtract).then_inc(sem("gate_split"), 1)
            phase_end(pool, 1)

            def rstd_and_weights(n):
                norm_rstd(pool, LNA, "a", n)
                c = n - LOW_FROM
                pool.wait_ge(sem("experts_hi"), c + 1)
                nc.gpsimd.tensor_tensor(wsplit[:, bass.ds(c * D + 2 * HW, D)], wraw[:, bass.ds(c * D, D)],
                                        wsplit[:, bass.ds(c * D, D)].bitcast(F32), ALU.subtract).then_inc(
                    sem("experts_split"), 1)

            for n in range(1, LOW_FROM):
                norm_rstd(pool, LNA, "a", n)
            with pool.Fori(LOW_FROM, LOW_FROM + CHUNKS) as n:
                rstd_and_weights(n)
            with pool.Fori(LOW_FROM + CHUNKS, B) as n:
                norm_rstd(pool, LNA, "a", n)
            phase_end(pool, 2)

            def split_hidden(l, g):
                pool.wait_ge(sem(f"hid{l}_ready"), g.n + 1)
                wait_from(pool, sem(f"sup{l + 1}_done"), g.n)
                nc.gpsimd.tensor_tensor(hid_lo[l][:, :], hid[l][:, :], hid_hi[l][:, :].bitcast(F32),
                                        ALU.subtract).then_inc(sem(f"hid{l}_split"), 1)

            def attend(g):
                pool.wait_ge(sem("pv_ready"), g.n + 1)
                pool.wait_ge(sem(f"x_in{g.par}"), (g.half + 1) * 16)
                wait_from(pool, sem("combined"), (g.n - 2) * 9 + 1)
                nc.gpsimd.tensor_tensor(x1[g.par][:, :], pv[:, :], xin[g.par][:, :], ALU.add).then_inc(
                    sem("x1_ready"), 1)

            def add_b3(g):
                pool.wait_ge(sem("combined"), g.n * 9 + 9)
                wait_from(pool, sem("x3_ready"), g.n - 1)
                nc.gpsimd.tensor_tensor(x2b[g.par][:, :], x2[g.par][:, :], b3_all[:, :], ALU.add).then_inc(
                    sem("x2b_ready"), 1)

            def step(g, nxt=True, nx2=True, b1=True, b2=True, routed=None):
                if b1:
                    add_b3(g.plus(-1))
                if nx2:
                    attend(g.plus(2))
                if b2:
                    split_hidden(1, g.plus(-2))
                if routed is not None:
                    (scatter if g.par else route)(routed)
                if b1:
                    split_hidden(0, g.plus(-1))
                if nx2:
                    norm_rstd(pool, LNA, "c", g.n + 2)
                norm_rstd(pool, LNB, "d", g.n)

            def route(c):
                own_wait(pool, (sem("scattered"), c * (16 * TOP)))
                pool.dma_start(sx[:, :], out[bass.ds(c, 1)].rearrange("o p d -> (o p) d")).then_inc(
                    sem("sx_in"), 16)
                nc.gpsimd.tensor_copy(sidx[:, :], slot_i[:, bass.ds(c * TOP, TOP)]).then_inc(sem("sidx_ready"), 1)

            def scatter(c):
                own_wait(pool, (sem("sx_in"), (c + 1) * 16), (sem("sidx_ready"), c + 1))
                for k in range(TOP):
                    nc.gpsimd.indirect_dma_start(
                        out=xg[:, :], out_offset=bass.IndirectOffsetOnAxis(ap=sidx[:, k:k + 1], axis=0),
                        in_=sx[:, :], in_offset=None).then_inc(sem("scattered"), 16)

            LEAD = TT + 4
            attend(Graph(0, 0, 0))
            norm_rstd(pool, LNA, "c", 0)
            attend(Graph(1, 0, 1))
            norm_rstd(pool, LNA, "c", 1)
            step(Graph(0, 0, 0), b1=False, b2=False)
            step(Graph(1, 0, 1), b2=False)
            second_pair(step)
            pairs_of_graphs(pool, step, 4, LEAD)
            for par in range(2):
                pool.wait_ge(sem(f"x3_out{par}"), 16 * (TT // 2))
            pool.wait_ge(sem("slots_zeroed"), 16 * TILES * HALVES)

            def routed_pair(half):
                g = Graph(half * 2, half, 0)
                step(g, routed=half - LEAD // 2)
                step(g.plus(1), routed=half - LEAD // 2)

            routed_pair(LEAD // 2)
            with pool.Fori(LEAD // 2 + 1, LEAD // 2 + TT) as half:
                routed_pair(half)
            pairs_of_graphs(pool, step, LEAD + 2 * TT, B - 2)
            step(Graph(B - 2, B // 2 - 1, 0), nx2=False)
            step(Graph(B - 1, B // 2 - 1, 1), nxt=False, nx2=False)

            def rstd_rows(j):
                for h in range(HALVES):
                    norm_rstd(pool, (LNA, LNB)[h], f"m{h}", j)

            def split_h(g):
                wait_from(pool, sem("layer2_done"), g.n - 1)
                for q in range(KF // 2):
                    pool.wait_ge(sem("h_hi"), g.n * (KF // 2) + (q + 1))
                    nc.gpsimd.tensor_tensor(h_lo[g.par][:, q * 512:(q + 1) * 512], hf[q][:, :],
                                            h_hi[g.par][:, q * 512:(q + 1) * 512].bitcast(F32),
                                            ALU.subtract).then_inc(sem("h_split"), 1)

            def tile_step(g):
                split_h(g)
                if has_next(g, 2):
                    rstd_rows(g.n + 2)

            add_b3(LAST)
            split_hidden(1, PENULT)
            rstd_rows(0)
            split_hidden(0, LAST)
            rstd_rows(1)
            split_hidden(1, LAST)
            split_h(Graph(0, 0, 0))
            rstd_rows(2)
            steps_of_tiles(pool, tile_step)

            def gather(g):
                own_wait(pool, (sem(f"fy_in{g.par}_0"), g.half * (16 * TOP)),
                         (sem(f"fy_in{g.par}_1"), g.half * (16 * TOP)), (sem("f2"), (g.n - 1) * 2))
                nc.gpsimd.tensor_copy(fslot[g.par][:, :], slot_i[:, bass.ds(g.n * (2 * TOP), 2 * TOP)]).then_inc(
                    sem("gidx_ready"), 1)
                own_wait(pool, (sem("gidx_ready"), g.n + 1))
                for k in range(2 * TOP):
                    nc.gpsimd.indirect_dma_start(
                        out=fy[g.par][k][:, :], out_offset=None, in_=yg[:, :],
                        in_offset=bass.IndirectOffsetOnAxis(ap=fslot[g.par][:, k:k + 1], axis=0)).then_inc(
                        sem(f"fy_in{g.par}_{k // TOP}"), 16)

            own_wait(pool, (sem("y_out"), 16 * TILES))
            gather(Graph(0, 0, 0))
            gather(Graph(1, 0, 1))
            pairs_of_graphs(pool, gather, 2, TT // 2)

        @block.scalar
        def _(act):
            def copy_const(dst, src, name):
                return nc.scalar.copy(dst, src).then_inc(sem(name), 1)

            for c in range(2):
                act.wait_ge(sem("qk_turned"), c + 1)
                copy_const(qkT[:, c * 512:(c + 1) * 512], bank[3 + c][:, :], "qkT_kept")
            mvf = mv_f[:, :].rearrange("p (k n) -> p k n", k=KD)
            act.wait_ge(sem("qkv_in"), 32)
            copy_const(mvf[:, :, D:2 * D], qkv_raw[:, KD * 2 * A:].rearrange("p (k n) -> p k n", k=KD), "mv_kept")
            act.wait_ge(sem("m_done"), 1)
            copy_const(mvf[:, :, 0:D], bank[5][:, :].rearrange("p (k n) -> p k n", k=KD), "mv_kept")
            act.wait_ge(sem("mv_kept"), 2)
            copy_const(mv_hi[:, :], mv_f[:, :], "mv_hi")
            act.wait_ge(sem("gnn_in"), 48)
            copy_const(gnn_hi[:, :], gnn_raw[:, :], "gnn_hi")
            act.wait_ge(sem("gate_in"), 64)
            copy_const(gsplit[:, :, 0, :], graw, "gate_hi")

            def first(g):
                act.wait_ge(sem("a_turned"), g.n + 1)
                wait_from(act, sem("qv_done"), g.n - 1)
                nc.scalar.copy(xT_hi[g.par][:, :], bank[g.par][:, 0:D]).then_inc(sem("a_hi"), 1)
                nc.scalar.copy(adjT_all[:, bass.ds(g.n * P, P)], bank[2 + g.par][:, 0:P]).then_inc(
                    sem("adjT_kept"), 1)
                wait_from(act, sem("agg_done"), g.n - 1)
                nc.scalar.activation(adjTm[g.par][:, :], bank[2 + g.par][:, 0:P], ACT.Copy,
                                     scale=mask_all[:, bass.ds(g.n, 1)]).then_inc(sem("adjTm_ready"), 1)

            act.wait_ge(sem("mask_ready"), 1)
            first(Graph(0, 0, 0))
            phase_end(act, 1)

            def second(g):
                act.wait_ge(sem("agg_done"), g.n + 1)
                wait_from(act, sem("w_dotted"), g.n - 1)
                nc.scalar.copy(agg_sb[g.par][:, :], bank[6 + g.par][:, 0:D]).then_inc(sem("agg_kept"), 1)
                act.wait_ge(sem("qv_done"), g.n + 1)
                nc.scalar.copy(v_all[:, bass.ds(g.n * D, D)], bank[4 + g.par][:, D:2 * D]).then_inc(
                    sem("v_kept"), 1)

            def both(g):
                first(g)
                second(g.plus(-1))

            both(Graph(1, 0, 1))
            def both_and_weights(g):
                both(g)
                c = g.n - HIGH_FROM
                nc.scalar.copy(wsplit[:, bass.ds(c * D, D)], wraw[:, bass.ds(c * D, D)]).then_inc(
                    sem("experts_hi"), 1)

            second_pair(both)
            pairs_of_graphs(act, both, 4, HIGH_FROM)
            act.wait_ge(sem("experts_in"), 16 * E)
            pairs_of_graphs(act, both_and_weights, HIGH_FROM, HIGH_FROM + CHUNKS)
            pairs_of_graphs(act, both, HIGH_FROM + CHUNKS, B)
            second(Graph(B - 1, B // 2 - 1, 1))
            act.wait_ge(sem("wneg_ready"), 1)
            nc.scalar.activation(wrow[:, :], bank[0][0:B, 0:P], ACT.Exp, bias=wneg[:, 0:1],
                                 accum_out=wsm[:, :]).then_inc(sem("wexp_ready"), 1)
            phase_end(act, 2)

            def gate_exp(g):
                act.wait_ge(sem("gmin_ready"), g.n + 1)
                nc.scalar.activation(ge[:, :], gneg[:, 0:E], ACT.Exp, bias=gmin[:, 0:1], scale=-1.0,
                                     accum_out=gesum[:, :]).then_inc(sem("ge_ready"), 1)
                nc.scalar.activation(gtanh[:, :], gneg[:, E:E + 1], ACT.Tanh, scale=-0.5).then_inc(
                    sem("ge_ready"), 1)

            def scale_v(g):
                wait_from(act, sem("x1_ready"), g.n)
                nc.scalar.activation(pv[:, :], v_all[:, bass.ds(g.n * D, D)], ACT.Copy,
                                     scale=p_all[:, bass.ds(g.n, 1)]).then_inc(sem("pv_ready"), 1)

            def take_adj(g):
                wait_from(act, sem("x3_summed"), g.n - 1)
                nc.scalar.copy(adjTs[g.par][:, :], adjT_all[:, bass.ds(g.n * P, P)]).then_inc(
                    sem("adjTs_ready"), 1)

            def keep_bias(g):
                act.wait_ge(sem("bexp_done"), g.n + 1)
                wait_from(act, sem("combined"), (g.n - 1) * 9 + 2)
                nc.scalar.copy(bias_sb[:, :], bank[2][:, D:2 * D]).then_inc(sem("bias_kept"), 1)

            def keep_sup(l, g):
                act.wait_ge(sem(f"sup{l}_done"), g.n + 1)
                wait_from(act, sem("x3_summed" if l == 2 else f"agg{l}_done"), g.n)
                nc.scalar.copy(sup[l][:, :], bank[6][:, 0:D]).then_inc(sem(f"sup{l}_kept"), 1)

            def relu(l, g):
                act.wait_ge(sem(f"agg{l}_done"), g.n + 1)
                wait_from(act, sem(f"hid{l}_split"), g.n)
                wait_from(act, sem(f"sup{l + 1}_done"), g.n)
                for dst in (hid_hi[l], hid[l]):
                    for c in range(KD):
                        last = nc.scalar.activation(dst[:, c * P:(c + 1) * P], bank[7][:, c * P:(c + 1) * P],
                                                    ACT.Relu, bias=b12[:, l * KD + c:l * KD + c + 1])
                last.then_inc(sem(f"hid{l}_ready"), 1)

            def hi_a(g):
                act.wait_ge(sem("c_turned"), g.n + 1)
                wait_from(act, sem("experts_done"), 4 * (g.n - 1))
                nc.scalar.copy(xT_hi[g.par][:, :], bank[0][:, 0:D]).then_inc(sem("c_hi"), 1)

            def hi_b(g):
                act.wait_ge(sem("d_turned"), g.n + 1)
                wait_from(act, sem("sup0_done"), g.n)
                nc.scalar.copy(yT_hi[:, :], bank[1][:, 0:D]).then_inc(sem("d_hi"), 1)

            def keep_gwT(g):
                act.wait_ge(sem("gw_turned"), g.n + 1)
                nc.scalar.copy(gwT[:, :], bank[2][0:E, P:2 * P]).then_inc(sem("gwT_kept"), 1)

            def step(g, nxt=True, nx2=True, b1=True, b2=True):
                one, two = g.plus(-1), g.plus(-2)
                keep_gwT(g)
                if b1:
                    take_adj(one)
                if nx2:
                    scale_v(g.plus(2))
                keep_bias(g)
                if b2:
                    keep_sup(1, two)
                if nxt:
                    hi_a(g.plus(1))
                if b1:
                    hi_b(one)
                if b2:
                    relu(1, two)
                if b1:
                    keep_sup(0, one)
                if nxt:
                    gate_exp(g.plus(1))
                if b1:
                    relu(0, one)
                if b2:
                    keep_sup(2, two)

            act.wait_ge(sem("bias_in"), 64)
            act.wait_ge(sem("p_ready"), 1)
            scale_v(Graph(0, 0, 0))
            scale_v(Graph(1, 0, 1))
            hi_a(Graph(0, 0, 0))
            gate_exp(Graph(0, 0, 0))
            step(Graph(0, 0, 0), b1=False, b2=False)
            step(Graph(1, 0, 1), b2=False)
            second_pair(step)
            pairs_of_graphs(act, step, 4, B - 2)
            step(Graph(B - 2, B // 2 - 1, 0), nx2=False)
            step(Graph(B - 1, B // 2 - 1, 1), nxt=False, nx2=False)

            def prepare(j):
                high_rows(j)
                high_w1(j)

            def high_rows(j):
                act.wait_ge(sem("m_turned"), j + 1)
                wait_from(act, sem("layer1_done"), 4 * j)
                nc.scalar.copy(mT_hi[:, :], bank[0][:, :]).then_inc(sem("m_hi"), 1)

            def high_w1(j):
                act.wait_ge(sem("w1_in"), (j + 1) * 16)
                for k in range(KD):
                    nc.scalar.copy(m1h[:, k, :], wraw[:, k * F:(k + 1) * F]).then_inc(sem("w1_hi"), 1)

            def split_w2(j, last=False):
                if last:
                    act.wait_ge(sem("layer1_done"), 4 * TILES)
                else:
                    wait_from(act, sem("layer2_done"), j)
                act.wait_ge(sem("w2_in"), (j + 1) * 16)
                for q in range(2):
                    at = W2_AT[last] + q * HW // 2
                    nc.scalar.copy(wsplit[:, at:at + HW // 2],
                                   wraw[:, HW + q * HW // 2:HW + (q + 1) * HW // 2]).then_inc(sem("w2_hi"), 1)

            def gelu(j):
                for q in range(KF // 2):
                    act.wait_ge(sem("layer1_done"), j * 4 + (q + 1))
                    wait_from(act, sem("h_split"), (j - 1) * 4 + (q + 1))
                    nc.scalar.activation(hf[q][:, :], bank[2 + q][:, :], ACT.Gelu).then_inc(sem("gelu"), 1)

            def keep_y(j):
                act.wait_ge(sem("layer2_done"), j + 1)
                wait_from(act, sem("y_out"), j * 16)
                nc.scalar.copy(my[:, :], bank[1][:, :]).then_inc(sem("y_ready"), 1)

            def tile_step(g):
                if not (isinstance(g.n, int) and g.n == 1):
                    keep_y(g.n - 2)
                split_w2(g.n - 1)
                gelu(g.n)
                if has_next(g, 1):
                    prepare(g.n + 1)

            take_adj(LAST)
            keep_sup(1, PENULT)
            act.wait_ge(sem("experts_done"), 4 * B)
            high_w1(0)
            hi_b(LAST)
            relu(1, PENULT)
            keep_sup(0, LAST)
            relu(0, LAST)
            high_rows(0)
            keep_sup(2, PENULT)
            keep_sup(1, LAST)
            relu(1, LAST)
            gelu(0)
            keep_sup(2, LAST)
            prepare(1)
            steps_of_tiles(act, tile_step)
            split_w2(TILES - 1, last=True)
            keep_y(TILES - 2)
            keep_y(TILES - 1)

        @block.vector
        def _(dve):
            def stats_first(g, between=None):
                dve.wait_ge(sem(f"a_in{g.slot}"), (g.quarter + 1) * 16)
                norm_stats(dve, xa[g.slot][:, :], LNA, "a", g.n, between)

            def norm_first(g):
                wait_from(dve, sem("agg_done"), g.n - 1)
                norm_apply(dve, xa[g.slot][:, :], xn[g.par][:, :], LNA, "a", g.n)

            count = 0

            def step_done(ins):
                nonlocal count
                ins.then_inc(sem("routed"), 1)
                count += 1
                return count

            dve.wait_ge(sem("route_in"), 16)
            indices = step_done(nc.vector.tensor_copy(ri_f[:, :], ri_i[:, :]))
            dve.wait_ge(sem("iotas_set"), 2)
            step_done(nc.vector.tensor_copy(steps_f[:, :], steps_i[:, :]))
            iotas = step_done(nc.vector.tensor_copy(tiles_f[:, :], tiles_i[:, :]))
            dve.wait_ge(sem("routed"), indices)
            for e in range(ME):
                nc.vector.tensor_scalar(oh3[:, e, :], ri_f[:, :], float(e), None, ALU.is_equal).then_inc(
                    sem("onehot"), 1)
            stats_first(Graph(0, 0, 0))
            dve.wait_ge(sem("mask_turned"), 1)
            nc.vector.tensor_copy(mask_all[:, :], bank[2][:, 0:B]).then_inc(sem("mask_ready"), 1)
            norm_first(Graph(0, 0, 0))
            dve.wait_ge(sem("totals_done"), 1)

            def running_sum(bufs, width):
                cur, shift = 0, 1
                while shift < width:
                    dve.wait_ge(sem("routed"), count)
                    src, dst = bufs[cur], bufs[1 - cur]
                    step_done(nc.vector.tensor_tensor(dst[..., shift:], src[..., shift:], src[..., :width - shift],
                                                      ALU.add))
                    step_done(nc.vector.tensor_copy(dst[..., :shift], src[..., :shift]))
                    cur, shift = 1 - cur, shift * 2
                dve.wait_ge(sem("routed"), count)
                return cur

            step_done(nc.vector.tensor_copy(scan[0][:, :], bank[1][:, 0:ME * NG]))
            cur = running_sum(sc3, NG)
            step_done(nc.vector.tensor_copy(counts[:, :], sc3[cur][:, :, NG - 1]))
            dve.wait_ge(sem("routed"), step_done(nc.vector.tensor_tensor(
                ranks[:, :], scan[cur][:, :], bank[1][:, 0:ME * NG], ALU.subtract)))
            step_done(nc.vector.tensor_tensor(ranks[:, :], ranks[:, :], bank[1][:, ME * NG:2 * ME * NG], ALU.add))
            dve.wait_ge(sem("routed"), step_done(nc.vector.tensor_tensor(
                cmp_n[:, :].rearrange("p (e m) -> p e m", e=ME),
                counts[:, :].unsqueeze(2).broadcast_to([P, ME, MAXT]),
                steps_f[:, :].unsqueeze(1).broadcast_to([P, ME, MAXT]), ALU.is_gt)))
            dve.wait_ge(sem("routed"), step_done(nc.vector.tensor_reduce(
                ntiles[:, :], cmp_n[:, :].rearrange("p (e m) -> p e m", e=ME), AX.X, ALU.add)))
            step_done(nc.vector.tensor_copy(ends[0][:, :], ntiles[:, :]))
            cur = running_sum([t[:, :] for t in ends], ME)
            step_done(nc.vector.tensor_tensor(base[:, :], ends[cur][:, :], ntiles[:, :], ALU.subtract))
            dve.wait_ge(sem("routed"), step_done(nc.vector.tensor_tensor(
                cmp_t[:, :].rearrange("p (t e) -> p t e", e=ME),
                tiles_f[:, :].unsqueeze(2).broadcast_to([P, TILES, ME]),
                ends[cur][:, :].unsqueeze(1).broadcast_to([P, TILES, ME]), ALU.is_ge)))
            dve.wait_ge(sem("routed"), step_done(nc.vector.tensor_reduce(
                texp_f[:, :], cmp_t[:, :].rearrange("p (t e) -> p t e", e=ME), AX.X, ALU.add)))
            step_done(nc.vector.tensor_scalar(texp_i[:, :], texp_f[:, :], float(ME - 1), None, ALU.min))
            dve.wait_ge(sem("routed"), step_done(nc.vector.tensor_scalar(
                first_slot[:, :], base[:, :], float(SLOTS), None, ALU.mult)))
            for e in range(ME):
                step_done(nc.vector.scalar_tensor_tensor(
                    out=sc3[0][:, e, :], in0=rk3[:, e, :], scalar=first_slot[:, e:e + 1], in1=oh3[:, e, :],
                    op0=ALU.add, op1=ALU.mult))
            dve.wait_ge(sem("routed"), count)
            dve.wait_ge(sem("routed"), step_done(nc.vector.tensor_reduce(
                slot_f[:, :], scan[0][:, :].rearrange("p (e g) -> p g e", e=ME), AX.X, ALU.add)))
            step_done(nc.vector.tensor_copy(slot_i[:, :], slot_f[:, :]))
            dve.wait_ge(sem("mv_hi"), 1)
            nc.vector.tensor_tensor(mv_lo[:, :], mv_f[:, :], mv_hi[:, :].bitcast(F32),
                                    ALU.subtract).then_inc(sem("mv_split"), 1)
            phase_end(dve, 1)

            def low_first(g):
                dve.wait_ge(sem("a_hi"), g.n + 1)
                wait_from(dve, sem("qv_done"), g.n - 1)
                nc.vector.tensor_tensor(xT_lo[g.par][:, :], bank[g.par][:, 0:D], xT_hi[g.par][:, :].bitcast(F32),
                                        ALU.subtract).then_inc(sem("a_split"), 1)

            def dot(g):
                wait_from(dve, sem("w_column"), g.n - 1)
                dve.wait_ge(sem("v_kept"), g.n + 1)
                dve.wait_ge(sem("agg_kept"), g.n + 1)
                nc.vector.tensor_tensor_reduce(out=agg_sb[g.par][:, :], in0=bank[4 + g.par][:, 0:D],
                                               in1=agg_sb[g.par][:, :], scale=1.0, scalar=0.0, op0=ALU.mult,
                                               op1=ALU.add, accum_out=wcol[g.par][:, :]).then_inc(
                    sem("w_dotted"), 1)

            def keep_column(g):
                dve.wait_ge(sem("w_dotted"), g.n + 1)
                nc.vector.tensor_copy(w_all[:, bass.ds(g.n, 1)], wcol[g.par][:, :]).then_inc(sem("w_column"), 1)

            def both(g, ahead=2):
                if not isinstance(g.n, int) or g.n >= 3:
                    keep_column(g.plus(-3))
                low_first(g)
                if ahead >= 1:
                    norm_first(g.plus(1))
                has_dot = not isinstance(g.n, int) or g.n >= 2
                if ahead >= 2:
                    stats_first(g.plus(2), (lambda: dot(g.plus(-2))) if has_dot else None)
                elif has_dot:
                    dot(g.plus(-2))

            stats_first(Graph(1, 0, 1))
            both(Graph(0, 0, 0))
            both(Graph(1, 0, 1))
            second_pair(both)
            fours_of_graphs(dve, both, 4, B - 4)
            both(Graph(B - 4, B // 2 - 2, 0))
            both(Graph(B - 3, B // 2 - 2, 1))
            both(Graph(B - 2, B // 2 - 1, 0), ahead=1)
            both(Graph(B - 1, B // 2 - 1, 1), ahead=0)
            keep_column(Graph(B - 3, B // 2 - 2, 1))
            dot(Graph(B - 2, B // 2 - 1, 0))
            keep_column(Graph(B - 2, B // 2 - 1, 0))
            dot(Graph(B - 1, B // 2 - 1, 1))
            keep_column(Graph(B - 1, B // 2 - 1, 1))
            dve.wait_ge(sem("w_column"), B)
            nc.vector.scalar_tensor_tensor(out=w_all[:, :], in0=w_all[:, :], scalar=INV, in1=mask_all[:, :],
                                           op0=ALU.mult, op1=ALU.mult).then_inc(sem("w_kept"), 1)
            dve.wait_ge(sem("w_turned"), 1)
            nc.vector.tensor_reduce(wmx[:, :], bank[0][0:B, 0:P], AX.X, ALU.max).then_inc(sem("wmx_ready"), 1)
            dve.wait_ge(sem("wmx_ready"), 1)
            nc.vector.tensor_scalar(wneg[:, :], wmx[:, :], -1.0, None, ALU.mult).then_inc(sem("wneg_ready"), 1)
            dve.wait_ge(sem("wexp_ready"), 1)
            nc.vector.reciprocal(wrc[:, :], wsm[:, :]).then_inc(sem("wrc_ready"), 1)
            dve.wait_ge(sem("wrc_ready"), 1)
            nc.vector.tensor_scalar(prow[:, :], wrow[:, :], wrc[:, 0:1], None, ALU.mult).then_inc(
                sem("prow_ready"), 1)
            dve.wait_ge(sem("p_turned"), 1)
            nc.vector.tensor_copy(p_all[:, :], bank[1][:, 0:B]).then_inc(sem("p_ready"), 1)
            phase_end(dve, 2)

            def stats_a(g):
                dve.wait_ge(sem("x1_ready"), g.n + 1)
                norm_stats(dve, x1[g.par][:, :], LNA, "c", g.n)

            def norm_a(g):
                wait_from(dve, sem("c_turned"), g.n)
                norm_apply(dve, x1[g.par][:, :], xn[0][:, :], LNA, "c", g.n)

            def low_a(g):
                dve.wait_ge(sem("c_hi"), g.n + 1)
                wait_from(dve, sem("experts_done"), 4 * (g.n - 1))
                nc.vector.tensor_tensor(xT_lo[g.par][:, :], bank[0][:, 0:D], xT_hi[g.par][:, :].bitcast(F32),
                                        ALU.subtract).then_inc(sem("c_split"), 1)

            def low_b(g):
                dve.wait_ge(sem("d_hi"), g.n + 1)
                wait_from(dve, sem("sup0_done"), g.n)
                nc.vector.tensor_tensor(yT_lo[:, :], bank[1][:, 0:D], yT_hi[:, :].bitcast(F32),
                                        ALU.subtract).then_inc(sem("d_split"), 1)

            def gate_start(g):
                dve.wait_ge(sem("gate_done"), g.n + 1)
                nc.vector.scalar_tensor_tensor(out=gpart[:, :], in0=bank[2][:, 0:E + 1], scalar=-1.0,
                                               in1=gate_bias[:, :], op0=ALU.mult, op1=ALU.subtract).then_inc(
                    sem("gpart_ready"), 1)
                dve.wait_ge(sem("gpart_ready"), g.n + 1)
                nc.vector.scalar_tensor_tensor(out=gneg[:, :], in0=bank[2][:, NGATE:NGATE + E + 1], scalar=-1.0,
                                               in1=gpart[:, :], op0=ALU.mult, op1=ALU.add).then_inc(
                    sem("gneg_ready"), 1)
                dve.wait_ge(sem("gneg_ready"), g.n + 1)
                nc.vector.tensor_reduce(gmin[:, :], gneg[:, 0:E], AX.X, ALU.min).then_inc(sem("gmin_ready"), 1)

            def gate_end(g):
                dve.wait_ge(sem("ge_ready"), 2 * g.n + 2)
                nc.vector.tensor_scalar(gthr[:, :], gtanh[:, :], 1.0, gesum[:, 0:1], ALU.add, ALU.mult).then_inc(
                    sem("gate_step"), 1)
                dve.wait_ge(sem("gate_step"), g.n * 4 + 1)
                nc.vector.scalar_tensor_tensor(out=gad[:, 0:E], in0=ge[:, :], scalar=2.0 / MAX_THRESHOLD,
                                               in1=gthr[:, 0:1].broadcast_to([P, E]), op0=ALU.mult,
                                               op1=ALU.subtract).then_inc(sem("gate_step"), 1)
                dve.wait_ge(sem("gate_step"), g.n * 4 + 2)
                nc.vector.tensor_scalar(gsel[:, :], gad[:, :], 0.0, 0.0, ALU.max, ALU.add,
                                        accum_out=gsum[:, :]).then_inc(sem("gate_step"), 1)
                dve.wait_ge(sem("gate_step"), g.n * 4 + 3)
                nc.vector.reciprocal(gri[:, :], gsum[:, :]).then_inc(sem("gate_step"), 1)
                dve.wait_ge(sem("gate_step"), g.n * 4 + 4)
                wait_from(dve, sem("combined"), (g.n - 1) * 9)
                wait_from(dve, sem("gw_turned"), g.n - 1)
                nc.vector.tensor_scalar(gw[g.par][:, :], gsel[:, 0:E], gri[:, 0:1], None, ALU.mult).then_inc(
                    sem("gw_ready"), 1)

            def combine(g, c):
                dve.wait_ge(sem("experts_done"), g.n * 4 + (c + 1))
                if c == 0:
                    dve.wait_ge(sem("gw_ready"), g.n + 1)
                    dve.wait_ge(sem("bias_kept"), g.n + 1)
                    wait_from(dve, sem("combined"), g.n * 9)
                for h, (dst, start) in enumerate(((even, x1[g.par]), (odd, bias_sb))):
                    e = 2 * c + h
                    if c > 0:
                        dve.wait_ge(sem("combined"), g.n * 9 + (e - 1))
                    nc.vector.scalar_tensor_tensor(
                        out=dst[:, :], in0=bank[EXPERT_BANK[c]][:, h * D:(h + 1) * D], scalar=gw[g.par][:, e:e + 1],
                        in1=(dst if c > 0 else start)[:, :], op0=ALU.mult, op1=ALU.add).then_inc(
                        sem("combined"), 1)

            def merge(g):
                dve.wait_ge(sem("combined"), g.n * 9 + 8)
                wait_from(dve, sem("x2b_ready"), g.n - 1)
                nc.vector.tensor_tensor(x2[g.par][:, :], even[:, :], odd[:, :], ALU.add).then_inc(
                    sem("combined"), 1)

            def stats_b(g):
                dve.wait_ge(sem("combined"), g.n * 9 + 9)
                norm_stats(dve, x2[g.par][:, :], LNB, "d", g.n)

            def norm_b(g):
                wait_from(dve, sem("d_turned"), g.n)
                norm_apply(dve, x2[g.par][:, :], xn[1][:, :], LNB, "d", g.n)

            def finish(g):
                dve.wait_ge(sem("x3_summed"), g.n + 1)
                dve.wait_ge(sem("x2b_ready"), g.n + 1)
                wait_from(dve, sem(f"x3_out{g.par}"), g.half * 16)
                nc.vector.tensor_tensor(xo[g.par][:, :], bank[7][:, 0:D], x2b[g.par][:, :], ALU.add).then_inc(
                    sem("x3_ready"), 1)

            def step(g, nxt=True, nx2=True, b1=True, b2=True):
                one, two, new = g.plus(-1), g.plus(-2), g.plus(1)
                if nxt:
                    norm_a(new)
                combine(g, 0)
                if b1:
                    norm_b(one)
                if nxt:
                    low_a(new)
                if b1:
                    low_b(one)
                combine(g, 1)
                combine(g, 2)
                if nxt:
                    gate_start(new)
                    gate_end(new)
                if nx2:
                    stats_a(g.plus(2))
                combine(g, 3)
                merge(g)
                stats_b(g)
                if b2:
                    finish(two)

            dve.wait_ge(sem("p_ready"), 1)
            stats_a(Graph(0, 0, 0))
            norm_a(Graph(0, 0, 0))
            low_a(Graph(0, 0, 0))
            gate_start(Graph(0, 0, 0))
            gate_end(Graph(0, 0, 0))
            stats_a(Graph(1, 0, 1))
            step(Graph(0, 0, 0), b1=False, b2=False)
            step(Graph(1, 0, 1), b2=False)
            second_pair(step)
            pairs_of_graphs(dve, step, 4, B - 2)
            step(Graph(B - 2, B // 2 - 1, 0), nx2=False)
            step(Graph(B - 1, B // 2 - 1, 1), nxt=False, nx2=False)

            def norm_rows(j):
                dve.wait_ge(sem("rows_in"), (j + 1) * 16)
                for h in range(HALVES):
                    norm_stats(dve, mx[:, h * D:(h + 1) * D], (LNA, LNB)[h], f"m{h}", j)
                wait_from(dve, sem("m_turned"), j)
                for h in range(HALVES):
                    norm_apply(dve, mx[:, h * D:(h + 1) * D], mxn[:, h * D:(h + 1) * D], (LNA, LNB)[h], f"m{h}", j)

            def prepare(j):
                low_rows(j)
                low_w1(j)

            def low_rows(j):
                dve.wait_ge(sem("m_hi"), j + 1)
                nc.vector.tensor_tensor(mT_lo[:, :], bank[0][:, :], mT_hi[:, :].bitcast(F32),
                                        ALU.subtract).then_inc(sem("m_split"), 1)

            def low_w1(j):
                for k in range(KD):
                    dve.wait_ge(sem("w1_hi"), j * 2 + (k + 1))
                    last = nc.vector.tensor_tensor(m1l[:, k, :], wraw[:, k * F:(k + 1) * F],
                                                   m1h[:, k, :].bitcast(F32), ALU.subtract)
                last.then_inc(sem("w1_split"), 1)

            def low_w2(j, last_tile=False):
                for q in range(2):
                    dve.wait_ge(sem("w2_hi"), j * 2 + (q + 1))
                    lo = W2_AT[last_tile] + HW + q * HW // 2
                    last = nc.vector.tensor_tensor(wsplit[:, lo:lo + HW // 2],
                                                   wraw[:, HW + q * HW // 2:HW + (q + 1) * HW // 2],
                                                   wsplit[:, lo - HW:lo - HW // 2].bitcast(F32), ALU.subtract)
                last.then_inc(sem("w2_split"), 1)

            def high_h(g):
                wait_from(dve, sem("layer2_done"), g.n - 1)
                for q in range(KF // 2):
                    dve.wait_ge(sem("gelu"), g.n * 4 + (q + 1))
                    nc.vector.tensor_copy(h_hi[g.par][:, q * 512:(q + 1) * 512], hf[q][:, :]).then_inc(
                        sem("h_hi"), 1)

            def tile_step(g):
                low_w2(g.n - 1)
                high_h(g)
                if has_next(g, 1):
                    prepare(g.n + 1)
                if has_next(g, 2):
                    norm_rows(g.n + 2)

            norm_b(LAST)
            low_w1(0)
            low_b(LAST)
            norm_rows(0)
            low_rows(0)
            finish(PENULT)
            norm_rows(1)
            high_h(Graph(0, 0, 0))
            prepare(1)
            finish(LAST)
            norm_rows(2)
            steps_of_tiles(dve, tile_step)
            low_w2(TILES - 1, last_tile=True)

            def add(g):
                dve.wait_ge(sem(f"fx_in{g.par}"), (g.half + 1) * 16)
                for t in range(2):
                    dve.wait_ge(sem(f"fy_in{g.par}_{t}"), 16 * TOP * (g.half + 1))
                    wait_from(dve, sem("f2"), (g.n - 1) * 2)
                    d = slice(t * D, (t + 1) * D)
                    nc.vector.scalar_tensor_tensor(out=facc[g.par][:, d], in0=fy[g.par][t * TOP][:, :],
                                                   scalar=rw[:, bass.ds((g.n * 2 + t) * TOP, 1)],
                                                   in1=fx[g.par][:, d], op0=ALU.mult, op1=ALU.add).then_inc(
                        sem("f1"), 1)
                for t in range(2):
                    dve.wait_ge(sem("f1"), g.n * 2 + (t + 1))
                    wait_from(dve, sem(f"fo_out{g.par}"), g.half * 16)
                    d = slice(t * D, (t + 1) * D)
                    nc.vector.scalar_tensor_tensor(out=fo[g.par][:, d], in0=fy[g.par][t * TOP + 1][:, :],
                                                   scalar=rw[:, bass.ds((g.n * 2 + t) * TOP + 1, 1)],
                                                   in1=facc[g.par][:, d], op0=ALU.mult, op1=ALU.add).then_inc(
                        sem("f2"), 1)

            dve.wait_ge(sem("route_w_in"), 16)
            add(Graph(0, 0, 0))
            add(Graph(1, 0, 1))
            pairs_of_graphs(dve, add, 2, TT // 2)

        @block.tensor
        def _(pe):
            pe.wait_ge(sem("onehot"), ME)
            pe.wait_ge(sem("below_set"), 1)
            nc.tensor.matmul(bank[1][:, 0:ME * NG], ones[:, :], onehot[:, :], start=True, stop=True)
            nc.tensor.matmul(bank[1][:, ME * NG:2 * ME * NG], below[:, :], onehot[:, :], start=True,
                             stop=True).then_inc(sem("totals_done"), 1)
            pe.wait_ge(sem("mask_in"), 16)
            pe.wait_ge(sem("ident_set"), 1)
            nc.tensor.transpose(bank[2][:, 0:B], mask_rows[:, :], ident[0:B, 0:B]).then_inc(
                sem("mask_turned"), 1)
            pe.wait_ge(sem("qkv_in"), 32)
            for c in range(2):
                for a in range(KD):
                    for k in range(KD):
                        src = qkv_raw[:, k * 2 * A + c * A + a * P:k * 2 * A + c * A + (a + 1) * P]
                        last = nc.tensor.transpose(bank[3 + c][:, a * D + k * P:a * D + (k + 1) * P], src,
                                                   ident[:, :])
                last.then_inc(sem("qk_turned"), 1)
            pe.wait_ge(sem("qkT_kept"), 2)
            for k in range(KD):
                for a in range(KD):
                    last = nc.tensor.matmul(bank[5][:, k * D:(k + 1) * D],
                                            qkT[:, a * D + k * P:a * D + (k + 1) * P],
                                            qkT[:, KD * D + a * D:KD * D + (a + 1) * D],
                                            start=(a == 0), stop=(a == KD - 1))
            last.then_inc(sem("m_done"), 1)
            def turn(g):
                pe.wait_ge(sem("a_normed"), g.n + 1)
                wait_from(pe, sem("a_split"), g.n - 1)
                for k in range(KD):
                    nc.tensor.transpose(bank[g.par][:, k * P:(k + 1) * P], xn[g.par][:, k * P:(k + 1) * P],
                                        ident[:, :])
                pe.wait_ge(sem(f"adj_in{g.par}"), (g.half + 1) * 16)
                wait_from(pe, sem("adjTm_ready"), g.n - 1)
                nc.tensor.transpose(bank[2 + g.par][:, 0:P], adjin[g.par][:, :], ident[:, :]).then_inc(
                    sem("a_turned"), 1)

            pe.wait_ge(sem("mask_ready"), 1)
            turn(Graph(0, 0, 0))
            phase_end(pe, 1)

            def products(g):
                pe.wait_ge(sem("adjTm_ready"), g.n + 1)
                wait_from(pe, sem("agg_kept"), g.n - 1)
                nc.tensor.matmul(bank[6 + g.par][:, 0:D], adjTm[g.par][:, :], xn[g.par][:, :], start=True,
                                 stop=True).then_inc(sem("agg_done"), 1)
                pe.wait_ge(sem("a_split"), g.n + 1)
                wait_from(pe, sem("w_dotted"), g.n - 1)
                for k in range(KD):
                    s = slice(k * P, (k + 1) * P)
                    last = split_product(nc.tensor, bank[4 + g.par][:, :],
                                         (xT_hi[g.par][:, s], xT_lo[g.par][:, s]), (mvh[:, k, :], mvl[:, k, :]),
                                         k == 0, k == KD - 1)
                last.then_inc(sem("qv_done"), 1)

            def both(g):
                turn(g)
                products(g.plus(-1))

            both(Graph(1, 0, 1))
            second_pair(both)
            pairs_of_graphs(pe, both, 4, B)
            products(Graph(B - 1, B // 2 - 1, 1))
            pe.wait_ge(sem("w_kept"), 1)
            nc.tensor.transpose(bank[0][0:B, 0:P], w_all[:, :], ident[:, :]).then_inc(sem("w_turned"), 1)
            pe.wait_ge(sem("prow_ready"), 1)
            nc.tensor.transpose(bank[1][:, 0:B], prow[:, :], ident[0:B, 0:B]).then_inc(sem("p_turned"), 1)
            phase_end(pe, 2)

            def turn_a(g):
                pe.wait_ge(sem("c_normed"), g.n + 1)
                wait_from(pe, sem("c_split"), g.n)
                for k in range(KD):
                    last = nc.tensor.transpose(bank[0][:, k * P:(k + 1) * P], xn[0][:, k * P:(k + 1) * P],
                                               ident[:, :])
                last.then_inc(sem("c_turned"), 1)

            def turn_b(g):
                pe.wait_ge(sem("d_normed"), g.n + 1)
                wait_from(pe, sem("d_split"), g.n)
                for k in range(KD):
                    last = nc.tensor.transpose(bank[1][:, k * P:(k + 1) * P], xn[1][:, k * P:(k + 1) * P],
                                               ident[:, :])
                last.then_inc(sem("d_turned"), 1)

            def gate(g):
                pe.wait_ge(sem("c_split"), g.n + 1)
                wait_from(pe, sem("bias_kept"), g.n)
                nc.tensor.matmul(bank[2][:, 0:2 * NGATE], xT_hi[g.par][:, 0:P], gate_split[:, 0:2 * NGATE],
                                 start=True, stop=False)
                for k in range(KD):
                    nc.tensor.matmul(bank[2][:, NGATE:2 * NGATE], xT_lo[g.par][:, k * P:(k + 1) * P],
                                     gsplit[:, k, 0, :], start=False, stop=False)
                for k in range(1, KD):
                    last = nc.tensor.matmul(bank[2][:, 0:2 * NGATE], xT_hi[g.par][:, k * P:(k + 1) * P],
                                            gate_split[:, k * 2 * NGATE:(k + 1) * 2 * NGATE], start=False,
                                            stop=(k == KD - 1))
                last.then_inc(sem("gate_done"), 1)

            def experts(g, c, k):
                if k == 0:
                    behind = {0: 2 - 9, 1: 8 - 9, 2: 6 - 9, 3: 4}[c]
                    wait_from(pe, sem("combined"), g.n * 9 + behind)
                s = slice(k * P, (k + 1) * P)
                last = split_product(nc.tensor, bank[EXPERT_BANK[c]][:, :], (xT_hi[g.par][:, s], xT_lo[g.par][:, s]),
                                     (exh[:, k, c * 512:(c + 1) * 512], exl[:, k, c * 512:(c + 1) * 512]),
                                     k == 0, k == KD - 1)
                if k == KD - 1:
                    last.then_inc(sem("experts_done"), 1)

            def turn_gw(g):
                pe.wait_ge(sem("gw_ready"), g.n + 1)
                nc.tensor.transpose(bank[2][0:E, P:2 * P], gw[g.par][:, :], ident[:, :]).then_inc(sem("gw_turned"), 1)

            def bias(g):
                pe.wait_ge(sem("gwT_kept"), g.n + 1)
                nc.tensor.matmul(bank[2][:, D:2 * D], gwT[:, :], bexp[:, :], start=True, stop=True).then_inc(
                    sem("bexp_done"), 1)

            def support(l, g):
                pe.wait_ge(sem("d_split" if l == 0 else f"hid{l - 1}_split"), g.n + 1)
                if l == 1:
                    wait_from(pe, sem("sup2_kept"), g.n)
                elif l == 0:
                    wait_from(pe, sem("sup1_kept"), g.n)
                else:
                    nxt = g.n + 2
                    pe.wait_ge(sem("sup0_kept"), min(nxt, B) if isinstance(nxt, int) else nxt)
                hi, lo = (yT_hi, yT_lo) if l == 0 else (hid_hi[l - 1], hid_lo[l - 1])
                for k in range(KD):
                    s = slice(k * P, (k + 1) * P)
                    last = split_product(nc.tensor, bank[6][:, 0:D], (hi[:, s], lo[:, s]),
                                         (gnh[:, l, k, :], gnl[:, l, k, :]), k == 0, k == KD - 1)
                last.then_inc(sem(f"sup{l}_done"), 1)

            def aggregate(l, g):
                pe.wait_ge(sem(f"sup{l}_kept"), g.n + 1)
                if l == 1:
                    wait_from(pe, sem("x3_ready"), g.n)
                    wait_from(pe, sem("hid0_ready"), g.n + 1)
                else:
                    pe.wait_ge(sem("adjTs_ready"), g.n + 1)
                    wait_from(pe, sem("hid1_ready"), g.n)
                for c in range(KD):
                    last = nc.tensor.matmul(bank[7][:, c * P:(c + 1) * P], sup[l][:, c * P:(c + 1) * P],
                                            adjTs[g.par][:, :], start=True, stop=True)
                last.then_inc(sem(f"agg{l}_done"), 1)

            def last_sum(g):
                pe.wait_ge(sem("sup2_kept"), g.n + 1)
                after = g.n + 2
                pe.wait_ge(sem("hid0_ready"), after if not isinstance(after, int) else min(after, B))
                nc.tensor.matmul(bank[7][:, 0:D], adjTs[g.par][:, :], sup[2][:, :], start=True,
                                 stop=True).then_inc(sem("x3_summed"), 1)

            def step(g, nxt=True, b1=True, b2=True):
                one, two, new = g.plus(-1), g.plus(-2), g.plus(1)
                turn_gw(g)
                experts(g, 0, 1)
                bias(g)
                if b2:
                    support(1, two)
                experts(g, 1, 0)
                if b2:
                    aggregate(1, two)
                if nxt:
                    turn_a(new)
                experts(g, 1, 1)
                if b1:
                    turn_b(one)
                experts(g, 2, 0)
                experts(g, 2, 1)
                if b1:
                    support(0, one)
                if nxt:
                    gate(new)
                experts(g, 3, 0)
                if b1:
                    aggregate(0, one)
                if b2:
                    support(2, two)
                experts(g, 3, 1)
                if nxt:
                    experts(new, 0, 0)
                if b2:
                    last_sum(two)

            turn_a(Graph(0, 0, 0))
            gate(Graph(0, 0, 0))
            experts(Graph(0, 0, 0), 0, 0)
            step(Graph(0, 0, 0), b1=False, b2=False)
            step(Graph(1, 0, 1), b2=False)
            second_pair(step)
            pairs_of_graphs(pe, step, 4, B - 2)
            step(Graph(B - 2, B // 2 - 1, 0))
            step(Graph(B - 1, B // 2 - 1, 1), nxt=False)

            def turn_tile(j):
                for h in range(HALVES):
                    pe.wait_ge(sem(f"m{h}_normed"), j + 1)
                wait_from(pe, sem("m_split"), j)
                for k in range(KD):
                    for h in range(HALVES):
                        last = nc.tensor.transpose(bank[0][:, k * SLOTS + h * P:k * SLOTS + (h + 1) * P],
                                                   mxn[:, h * D + k * P:h * D + (k + 1) * P], ident[:, :])
                last.then_inc(sem("m_turned"), 1)

            def layer1(j, parts=range(KF // 2)):
                pe.wait_ge(sem("m_split"), j + 1)
                pe.wait_ge(sem("w1_split"), j + 1)
                for q in parts:
                    wait_from(pe, sem("gelu"), (j - 1) * 4 + (q + 1))
                    for m in (2 * q, 2 * q + 1):
                        for k in range(KD):
                            f, s = slice(m * P, (m + 1) * P), slice(k * SLOTS, (k + 1) * SLOTS)
                            last = split_product(nc.tensor, bank[2 + q][:, (m % 2) * SLOTS:(m % 2 + 1) * SLOTS],
                                                 (m1h[:, k, f], m1l[:, k, f]), (mT_hi[:, s], mT_lo[:, s]),
                                                 k == 0, k == KD - 1)
                    last.then_inc(sem("layer1_done"), 1)

            def layer2(g):
                j = g.n
                m2h, m2l = m2[isinstance(j, int) and j == TILES - 1]
                pe.wait_ge(sem("w2_split"), j + 1)
                wait_from(pe, sem("y_ready"), j)
                for h in range(HALVES):
                    for m in range(KF):
                        if h == 0 and m % 2 == 0:
                            pe.wait_ge(sem("h_split"), j * 4 + (m // 2 + 1))
                        s = slice(m * SLOTS + h * P, m * SLOTS + (h + 1) * P)
                        last = split_product(nc.tensor, bank[1][:, h * D:(h + 1) * D],
                                             (h_hi[g.par][:, s], h_lo[g.par][:, s]),
                                             (m2h[:, m, :], m2l[:, m, :]), m == 0, m == KF - 1)
                last.then_inc(sem("layer2_done"), 1)

            def tile_step(g):
                layer1(g.n)
                if has_next(g, 1):
                    turn_tile(g.n + 1)
                layer2(g.plus(-1))

            support(1, PENULT)
            aggregate(1, PENULT)
            turn_b(LAST)
            support(0, LAST)
            aggregate(0, LAST)
            pe.wait_ge(sem("c_split"), B)
            turn_tile(0)
            support(2, PENULT)
            pe.wait_ge(sem("combined"), 9 * B)
            pe.wait_ge(sem("bias_kept"), B)
            layer1(0, [0])
            last_sum(PENULT)
            support(1, LAST)
            layer1(0, [1])
            aggregate(1, LAST)
            layer1(0, [2, 3])
            turn_tile(1)
            support(2, LAST)
            last_sum(LAST)
            pe.wait_ge(sem("d_split"), B)
            steps_of_tiles(pe, tile_step)
            layer2(Graph(TILES - 1, (TILES - 1) // 2, (TILES - 1) % 2))


_INS = ['x', 'adj', 'nodemask', 'L0_gnn_Wqk', 'L0_gnn_Wv', 'L0_ffn_W_gate', 'L0_ffn_b_gate', 'L0_ffn_W_thr',
        'L0_ffn_b_thr', 'L0_ffn_W_exp', 'L0_ffn_b_exp', 'L1_gnn_W1', 'L1_gnn_b1', 'L1_gnn_W2', 'L1_gnn_b2',
        'L1_gnn_W3', 'L1_gnn_b3', 'L1_ffn_expert_weights', 'L1_ffn_expert_indices', 'L1_ffn_w1', 'L1_ffn_w2']
_OUT = ((64, 128, 256), 'float32')


def kernel(**inputs):
    import numpy as _np
    import concourse.bacc as _bacc
    from concourse import mybir as _mybir
    from concourse.bass_utils import run_bass_kernel_spmd as _run

    nc = _bacc.Bacc("TRN2", target_bir_lowering=False, num_devices=1)
    arrays, args = {}, []
    for name in _INS:
        a = _np.ascontiguousarray(inputs[name])
        arrays[f"in_{name}_dram"] = a
        args.append(nc.dram_tensor(f"in_{name}_dram", a.shape, _mybir.dt.from_np(a.dtype), kind="ExternalInput").ap())
    shape, dtype = _OUT
    args.append(nc.dram_tensor("out_dram", shape, _mybir.dt.from_np(_np.dtype(dtype)), kind="ExternalOutput").ap())
    build(nc, *args)
    r = _run(nc, [arrays], core_ids=[0])
    return r.results[0]["out_dram"]
```
